# Optimizing a Trainium2 kernel written in Bass

```python
import numpy as np
import jax
import jax.numpy as jnp

def _softmax(x, axis=-1):
    return jax.nn.softmax(x, axis=axis)

def _gelu(x):
    return jax.nn.gelu(x, approximate=True)

def _silu(x):
    return jax.nn.silu(x)

def _sigmoid(x):
    return jax.nn.sigmoid(x)

def _layernorm(x, axis=-1, eps=1e-05):
    m = jnp.mean(x, axis=axis, keepdims=True)
    v = jnp.var(x, axis=axis, keepdims=True)
    return (x - m) / jnp.sqrt(v + eps)

def _scatter_add(tgt, idx, src, axis=0):
    return tgt.at[idx].add(src)

def _segment_sum(src, seg, n):
    return jax.ops.segment_sum(src, seg, n)
kernel_name = 'mk_early_fusion_embed_d2_tok_img256_r4_675be0'

def setup_inputs(seed: int=0):
    np.random.seed(seed)
    _w = jnp.asarray

    def _rec_inputs():
        import jax
        import jax.numpy as jnp
        _rk = jax.random.key(seed)
        x = 7.22013e-05 + 1.00017 * jax.random.normal(jax.random.fold_in(_rk, 1), (4, 64, 64, 64), jnp.float32)
        x_txt = jax.random.randint(jax.random.fold_in(_rk, 51), (4, 32), 0, 31993, jnp.int32)
        return (x, x_txt)
    x, x_txt = _rec_inputs()

    def _L0_tok_setup():
        import jax, jax.numpy as jnp
        import numpy as np
        K = 3
        PAD = (K - 1) // 2
        BN_EPS = 1e-05

        def _unfold(x):
            b, c, h, w = x.shape
            xp = jnp.pad(x, ((0, 0), (0, 0), (PAD, PAD), (PAD, PAD)))
            shifts = [xp[:, :, i:i + h, j:j + w] for i in range(K) for j in range(K)]
            return jnp.stack(shifts, axis=2)
        key = jax.random.key(seed)
        ks = jax.random.split(key, 4)
        b, c, h, w = (8, 64, 64, 64)
        cr = c // 4
        x = jax.random.normal(ks[0], (b, c, h, w), dtype=jnp.float32)
        conv1_w = jax.random.normal(ks[1], (cr, c), dtype=jnp.float32) * (1.0 / np.sqrt(c))
        conv1_b = jnp.zeros((cr,), dtype=jnp.float32)
        bn_gamma = jnp.ones((cr,), dtype=jnp.float32)
        bn_beta = jnp.zeros((cr,), dtype=jnp.float32)
        bn_mean = jnp.zeros((cr,), dtype=jnp.float32)
        bn_var = jnp.ones((cr,), dtype=jnp.float32)
        conv2_w = jax.random.normal(ks[2], (K * K, cr), dtype=jnp.float32) * (1.0 / np.sqrt(cr))
        conv2_b = jnp.zeros((K * K,), dtype=jnp.float32)
        return {'x': x, 'conv1_w': conv1_w, 'conv1_b': conv1_b, 'bn_gamma': bn_gamma, 'bn_beta': bn_beta, 'bn_mean': bn_mean, 'bn_var': bn_var, 'conv2_w': conv2_w, 'conv2_b': conv2_b}
    _L0_tok_all = _L0_tok_setup()
    _L0_tok_in = {k: v for k, v in _L0_tok_all.items() if k in ('conv1_w', 'conv1_b', 'bn_gamma', 'bn_beta', 'bn_mean', 'bn_var', 'conv2_w', 'conv2_b')}
    del _L0_tok_all

    def _L0_txt_setup():
        import jax, jax.numpy as jnp
        import numpy as np
        VOCAB = 8000
        DIM = 64
        ROUND = 3
        SEQ = 2048
        LN_EPS = 1e-05
        key = jax.random.key(seed)
        ks = jax.random.split(key, 8)
        inputs = jax.random.randint(ks[0], (1, SEQ), 0, VOCAB, dtype=jnp.int64)
        scale = 1.0 / np.sqrt(DIM)
        A_w = jax.random.normal(ks[1], (VOCAB, DIM), dtype=jnp.float32) * scale
        C_w = jax.random.normal(ks[2], (VOCAB, DIM), dtype=jnp.float32) * scale
        U_w = jax.random.normal(ks[3], (VOCAB, DIM), dtype=jnp.float32) * scale
        ln_g = jnp.ones((DIM,), dtype=jnp.float32)
        ln_b = jnp.zeros((DIM,), dtype=jnp.float32)
        W = jax.random.normal(ks[4], (DIM, DIM), dtype=jnp.float32) * scale
        b = jnp.zeros((DIM,), dtype=jnp.float32)
        return {'inputs': inputs, 'A_w': A_w, 'C_w': C_w, 'U_w': U_w, 'ln_g': ln_g, 'ln_b': ln_b, 'W': W, 'b': b}
    _L0_txt_all = _L0_txt_setup()
    _L0_txt_in = {k: v for k, v in _L0_txt_all.items() if k in ('A_w', 'C_w', 'U_w', 'ln_g', 'ln_b', 'W', 'b')}
    del _L0_txt_all

    def _L0_attn_setup():
        import jax, jax.numpy as jnp
        import numpy as np
        import math
        N_SEQ, L_RES, D_MODEL = (128, 96, 64)
        N_HEAD, C_HEAD = (8, 32)
        EPS = 1e-05
        key = jax.random.key(seed)
        ks = jax.random.split(key, 8)
        s = 1.0 / math.sqrt(D_MODEL)
        return {'m': jax.random.normal(ks[0], (N_SEQ, L_RES, D_MODEL), jnp.float32), 'gamma': jnp.ones((D_MODEL,), jnp.float32), 'beta': jnp.zeros((D_MODEL,), jnp.float32), 'Wq': jax.random.normal(ks[1], (D_MODEL, N_HEAD * C_HEAD), jnp.float32) * s, 'Wk': jax.random.normal(ks[2], (D_MODEL, N_HEAD * C_HEAD), jnp.float32) * s, 'Wv': jax.random.normal(ks[3], (D_MODEL, N_HEAD * C_HEAD), jnp.float32) * s, 'Wg': jax.random.normal(ks[4], (D_MODEL, N_HEAD * C_HEAD), jnp.float32) * s, 'bg': jnp.zeros((N_HEAD * C_HEAD,), jnp.float32), 'Wo': jax.random.normal(ks[5], (N_HEAD * C_HEAD, D_MODEL), jnp.float32) * s, 'bo': jnp.zeros((D_MODEL,), jnp.float32)}
    _L0_attn_all = _L0_attn_setup()
    _L0_attn_in = {k: v for k, v in _L0_attn_all.items() if k in ('gamma', 'beta', 'Wq', 'Wk', 'Wv', 'Wg', 'bg', 'Wo', 'bo')}
    del _L0_attn_all

    def _L0_ffn_setup():
        import jax, jax.numpy as jnp
        import numpy as np
        NUM_EXPERTS = 8
        TOP_K = 2
        B, S, D = (8, 2048, 64)

        def _moe(tokens, router_w, w1, b1, w2, b2):
            N = tokens.shape[0]
            E = router_w.shape[0]
            logits = tokens.astype(jnp.float32) @ router_w.astype(jnp.float32).T
            probs = jax.nn.softmax(logits, axis=-1)
            rw, re = jax.lax.top_k(probs, TOP_K)
            if TOP_K > 1:
                rw = rw / jnp.maximum(rw.sum(-1, keepdims=True), 1e-12)
            rw = rw.astype(tokens.dtype)
            combine = jnp.zeros((N, E), tokens.dtype).at[jnp.arange(N)[:, None], re].set(rw)
            out = tokens
            for e in range(E):
                h = jax.nn.gelu(tokens @ w1[e] + b1[e], approximate=False)
                y = h @ w2[e] + b2[e]
                out = out + combine[:, e:e + 1] * y
            return out
        key = jax.random.key(seed)
        ks = jax.random.split(key, 4)
        scale = 1.0 / np.sqrt(D).astype(np.float32)
        return {'input_embeddings': jax.random.normal(ks[0], (B, S, D), jnp.float32), 'router_w': jax.random.normal(ks[1], (NUM_EXPERTS, D), jnp.float32) * scale, 'w1': jax.random.normal(ks[2], (NUM_EXPERTS, D, D), jnp.float32) * scale, 'b1': jnp.zeros((NUM_EXPERTS, D), jnp.float32), 'w2': jax.random.normal(ks[3], (NUM_EXPERTS, D, D), jnp.float32) * scale, 'b2': jnp.zeros((NUM_EXPERTS, D), jnp.float32)}
    _L0_ffn_all = _L0_ffn_setup()
    _L0_ffn_in = {k: v for k, v in _L0_ffn_all.items() if k in ('router_w', 'w1', 'b1', 'w2', 'b2')}
    del _L0_ffn_all

    def _L1_attn_setup():
        import jax, jax.numpy as jnp
        import numpy as np
        GAMMA = 0.96875
        SCALE_BASE = 512.0

        def xpos_rope(x, downscale=False):
            B, S, D = x.shape
            half = D // 2
            inv_freq = 1.0 / 10000.0 ** (jnp.arange(0, D, 2, dtype=jnp.float32) / D)
            pos = jnp.arange(S, dtype=jnp.float32)
            ang = pos[:, None] * inv_freq[None, :]
            sin, cos = (jnp.sin(ang), jnp.cos(ang))
            base = (jnp.arange(0, D, 2, dtype=jnp.float32) + 0.4 * D) / (1.4 * D)
            scale = base[None, :] ** (pos[:, None] / SCALE_BASE)
            if downscale:
                scale = 1.0 / scale
            x1 = x[..., 0::2]
            x2 = x[..., 1::2]
            r1 = (x1 * cos - x2 * sin) * scale
            r2 = (x1 * sin + x2 * cos) * scale
            out = jnp.stack([r1, r2], axis=-1).reshape(B, S, D)
            return out

        def get_D(gamma, seq_len):
            n = jnp.arange(seq_len, dtype=jnp.float32)
            diff = n[:, None] - n[None, :]
            mask = diff >= 0
            D = jnp.where(mask, gamma ** jnp.where(mask, diff, 0.0), 0.0)
            return D

        def _reference_tuple_inner(x, W_Q, W_K, W_V):
            S = x.shape[1]
            D = get_D(GAMMA, S)
            Q = xpos_rope(x @ W_Q, downscale=False)
            K = xpos_rope(x @ W_K, downscale=True)
            V = x @ W_V
            ret = jnp.einsum('bnd,bmd->bnm', Q, K) * D[None, :, :]
            out = jnp.einsum('bnm,bmv->bnv', ret, V)
            return (out, ret)
        key = jax.random.key(seed)
        k1, k2, k3, k4 = jax.random.split(key, 4)
        B, S, d_model, d_k, d_v = (8, 1024, 64, 64, 64)
        x = jax.random.normal(k1, (B, S, d_model), dtype=jnp.float32)
        W_Q = jax.random.normal(k2, (d_model, d_k), dtype=jnp.float32) / d_model
        W_K = jax.random.normal(k3, (d_model, d_k), dtype=jnp.float32) / d_model
        W_V = jax.random.normal(k4, (d_model, d_v), dtype=jnp.float32) / d_model
        return {'x': x, 'W_Q': W_Q, 'W_K': W_K, 'W_V': W_V}
    _L1_attn_all = _L1_attn_setup()
    _L1_attn_in = {k: v for k, v in _L1_attn_all.items() if k in ('W_Q', 'W_K', 'W_V')}
    del _L1_attn_all

    def _L1_ffn_setup():
        import jax, jax.numpy as jnp
        import numpy as np
        D_MODEL = 64
        EXPERT_DIM = 128
        NUM_EXPERTS = 8
        TOP_K = 2
        SEQ_LEN = 512
        BATCH = 2
        key = jax.random.key(seed)
        ks = jax.random.split(key, 8)
        s = 0.02
        x = jax.random.normal(ks[0], (SEQ_LEN, BATCH, D_MODEL), dtype=jnp.float32)
        Wg = jax.random.normal(ks[1], (D_MODEL, NUM_EXPERTS), dtype=jnp.float32) * s
        bg = jax.random.normal(ks[2], (NUM_EXPERTS,), dtype=jnp.float32) * s
        bias = jnp.zeros((NUM_EXPERTS,), dtype=jnp.float32)
        W1 = jax.random.normal(ks[3], (NUM_EXPERTS, D_MODEL, EXPERT_DIM), dtype=jnp.float32) * s
        b1 = jax.random.normal(ks[4], (NUM_EXPERTS, EXPERT_DIM), dtype=jnp.float32) * s
        W2 = jax.random.normal(ks[5], (NUM_EXPERTS, EXPERT_DIM, D_MODEL), dtype=jnp.float32) * s
        b2 = jax.random.normal(ks[6], (NUM_EXPERTS, D_MODEL), dtype=jnp.float32) * s
        return {'x': x, 'Wg': Wg, 'bg': bg, 'bias': bias, 'W1': W1, 'b1': b1, 'W2': W2, 'b2': b2}
    _L1_ffn_all = _L1_ffn_setup()
    _L1_ffn_in = {k: v for k, v in _L1_ffn_all.items() if k in ('Wg', 'bg', 'bias', 'W1', 'b1', 'W2', 'b2')}
    del _L1_ffn_all
    return {'x': x, 'x_txt': x_txt, 'L0_tok_conv1_w': _L0_tok_in['conv1_w'], 'L0_tok_conv1_b': _L0_tok_in['conv1_b'], 'L0_tok_bn_gamma': _L0_tok_in['bn_gamma'], 'L0_tok_bn_beta': _L0_tok_in['bn_beta'], 'L0_tok_bn_mean': _L0_tok_in['bn_mean'], 'L0_tok_bn_var': _L0_tok_in['bn_var'], 'L0_tok_conv2_w': _L0_tok_in['conv2_w'], 'L0_tok_conv2_b': _L0_tok_in['conv2_b'], 'L0_txt_A_w': _L0_txt_in['A_w'], 'L0_txt_C_w': _L0_txt_in['C_w'], 'L0_txt_U_w': _L0_txt_in['U_w'], 'L0_txt_ln_g': _L0_txt_in['ln_g'], 'L0_txt_ln_b': _L0_txt_in['ln_b'], 'L0_txt_W': _L0_txt_in['W'], 'L0_txt_b': _L0_txt_in['b'], 'L0_attn_gamma': _L0_attn_in['gamma'], 'L0_attn_beta': _L0_attn_in['beta'], 'L0_attn_Wq': _L0_attn_in['Wq'], 'L0_attn_Wk': _L0_attn_in['Wk'], 'L0_attn_Wv': _L0_attn_in['Wv'], 'L0_attn_Wg': _L0_attn_in['Wg'], 'L0_attn_bg': _L0_attn_in['bg'], 'L0_attn_Wo': _L0_attn_in['Wo'], 'L0_attn_bo': _L0_attn_in['bo'], 'L0_ffn_router_w': _L0_ffn_in['router_w'], 'L0_ffn_w1': _L0_ffn_in['w1'], 'L0_ffn_b1': _L0_ffn_in['b1'], 'L0_ffn_w2': _L0_ffn_in['w2'], 'L0_ffn_b2': _L0_ffn_in['b2'], 'L1_attn_W_Q': _L1_attn_in['W_Q'], 'L1_attn_W_K': _L1_attn_in['W_K'], 'L1_attn_W_V': _L1_attn_in['W_V'], 'L1_ffn_Wg': _L1_ffn_in['Wg'], 'L1_ffn_bg': _L1_ffn_in['bg'], 'L1_ffn_bias': _L1_ffn_in['bias'], 'L1_ffn_W1': _L1_ffn_in['W1'], 'L1_ffn_b1': _L1_ffn_in['b1'], 'L1_ffn_W2': _L1_ffn_in['W2'], 'L1_ffn_b2': _L1_ffn_in['b2']}

def reference(x, x_txt, L0_tok_conv1_w, L0_tok_conv1_b, L0_tok_bn_gamma, L0_tok_bn_beta, L0_tok_bn_mean, L0_tok_bn_var, L0_tok_conv2_w, L0_tok_conv2_b, L0_txt_A_w, L0_txt_C_w, L0_txt_U_w, L0_txt_ln_g, L0_txt_ln_b, L0_txt_W, L0_txt_b, L0_attn_gamma, L0_attn_beta, L0_attn_Wq, L0_attn_Wk, L0_attn_Wv, L0_attn_Wg, L0_attn_bg, L0_attn_Wo, L0_attn_bo, L0_ffn_router_w, L0_ffn_w1, L0_ffn_b1, L0_ffn_w2, L0_ffn_b2, L1_attn_W_Q, L1_attn_W_K, L1_attn_W_V, L1_ffn_Wg, L1_ffn_bg, L1_ffn_bias, L1_ffn_W1, L1_ffn_b1, L1_ffn_W2, L1_ffn_b2):
    import jax
    import jax.numpy as jnp

    def _L0_tok_ref(x, conv1_w, conv1_b, bn_gamma, bn_beta, bn_mean, bn_var, conv2_w, conv2_b):
        import jax, jax.numpy as jnp
        import numpy as np
        K = 3
        PAD = (K - 1) // 2
        BN_EPS = 1e-05

        def _unfold(x):
            b, c, h, w = x.shape
            xp = jnp.pad(x, ((0, 0), (0, 0), (PAD, PAD), (PAD, PAD)))
            shifts = [xp[:, :, i:i + h, j:j + w] for i in range(K) for j in range(K)]
            return jnp.stack(shifts, axis=2)
        b, c, h, w = x.shape
        y = jnp.einsum('oc,bchw->bohw', conv1_w, x) + conv1_b[None, :, None, None]
        y = (y - bn_mean[None, :, None, None]) * (bn_gamma[None, :, None, None] * jax.lax.rsqrt(bn_var + BN_EPS)[None, :, None, None]) + bn_beta[None, :, None, None]
        y = jax.nn.relu(y)
        wdyn = jnp.einsum('ok,bkhw->bohw', conv2_w, y) + conv2_b[None, :, None, None]
        patches = _unfold(x)
        out = jnp.einsum('bckhw,bkhw->bchw', patches, wdyn)
        return out.reshape(b, h * w, c)

    def _L0_txt_ref(inputs, A_w, C_w, U_w, ln_g, ln_b, W, b):
        import jax, jax.numpy as jnp
        import numpy as np
        VOCAB = 8000
        DIM = 64
        ROUND = 3
        SEQ = 2048
        LN_EPS = 1e-05
        ids = jnp.clip(inputs, 0, A_w.shape[0] - 1)
        S = ids.shape[1]
        pos = jnp.clip(jnp.arange(S), 0, U_w.shape[0] - 1)[None, :]
        u = U_w[pos]
        a = A_w[ids]
        c = C_w[ids]
        for _ in range(ROUND):
            p = jax.nn.softmax(jnp.einsum('bsd,btd->bst', a, u), axis=-1)
            o = jnp.einsum('bst,bsd->btd', p, c)
            u = o + u
        mu = jnp.mean(u, axis=-1, keepdims=True)
        var = jnp.mean(jnp.square(u - mu), axis=-1, keepdims=True)
        ln = (u - mu) * jax.lax.rsqrt(var + LN_EPS) * ln_g + ln_b
        return jnp.einsum('bsd,ed->bse', ln, W) + b

    def _L0_attn_ref(m, gamma, beta, Wq, Wk, Wv, Wg, bg, Wo, bo):
        import jax, jax.numpy as jnp
        import numpy as np
        import math
        N_SEQ, L_RES, D_MODEL = (128, 96, 64)
        N_HEAD, C_HEAD = (8, 32)
        EPS = 1e-05
        N, L, D = m.shape
        H, C = (N_HEAD, C_HEAD)
        mu = jnp.mean(m, axis=-1, keepdims=True)
        var = jnp.mean(jnp.square(m - mu), axis=-1, keepdims=True)
        mn = (m - mu) * jax.lax.rsqrt(var + EPS) * gamma + beta
        q = (mn @ Wq).reshape(N, L, H, C)
        k = (mn @ Wk).reshape(N, L, H, C)
        v = (mn @ Wv).reshape(N, L, H, C)
        g = jax.nn.sigmoid(mn @ Wg + bg).reshape(N, L, H, C)
        scale = 1.0 / math.sqrt(C) / math.sqrt(L)
        att = jnp.einsum('slhc,tlhc->sth', q, k) * scale
        att = jax.nn.softmax(att, axis=1)
        o = jnp.einsum('sth,tlhc->slhc', att, v) * g
        return o.reshape(N, L, H * C) @ Wo + bo

    def _L0_ffn_ref(input_embeddings, router_w, w1, b1, w2, b2):
        import jax, jax.numpy as jnp
        import numpy as np
        NUM_EXPERTS = 8
        TOP_K = 2
        B, S, D = (8, 2048, 64)

        def _moe(tokens, router_w, w1, b1, w2, b2):
            N = tokens.shape[0]
            E = router_w.shape[0]
            logits = tokens.astype(jnp.float32) @ router_w.astype(jnp.float32).T
            probs = jax.nn.softmax(logits, axis=-1)
            rw, re = jax.lax.top_k(probs, TOP_K)
            if TOP_K > 1:
                rw = rw / jnp.maximum(rw.sum(-1, keepdims=True), 1e-12)
            rw = rw.astype(tokens.dtype)
            combine = jnp.zeros((N, E), tokens.dtype).at[jnp.arange(N)[:, None], re].set(rw)
            out = tokens
            for e in range(E):
                h = jax.nn.gelu(tokens @ w1[e] + b1[e], approximate=False)
                y = h @ w2[e] + b2[e]
                out = out + combine[:, e:e + 1] * y
            return out
        b, s, d = input_embeddings.shape
        tokens = input_embeddings.reshape(b * s, d)
        return _moe(tokens, router_w, w1, b1, w2, b2).reshape(b, s, d)

    def _L1_attn_ref(x, W_Q, W_K, W_V):
        import jax, jax.numpy as jnp
        import numpy as np
        GAMMA = 0.96875
        SCALE_BASE = 512.0

        def xpos_rope(x, downscale=False):
            B, S, D = x.shape
            half = D // 2
            inv_freq = 1.0 / 10000.0 ** (jnp.arange(0, D, 2, dtype=jnp.float32) / D)
            pos = jnp.arange(S, dtype=jnp.float32)
            ang = pos[:, None] * inv_freq[None, :]
            sin, cos = (jnp.sin(ang), jnp.cos(ang))
            base = (jnp.arange(0, D, 2, dtype=jnp.float32) + 0.4 * D) / (1.4 * D)
            scale = base[None, :] ** (pos[:, None] / SCALE_BASE)
            if downscale:
                scale = 1.0 / scale
            x1 = x[..., 0::2]
            x2 = x[..., 1::2]
            r1 = (x1 * cos - x2 * sin) * scale
            r2 = (x1 * sin + x2 * cos) * scale
            out = jnp.stack([r1, r2], axis=-1).reshape(B, S, D)
            return out

        def get_D(gamma, seq_len):
            n = jnp.arange(seq_len, dtype=jnp.float32)
            diff = n[:, None] - n[None, :]
            mask = diff >= 0
            D = jnp.where(mask, gamma ** jnp.where(mask, diff, 0.0), 0.0)
            return D

        def _reference_tuple_inner(x, W_Q, W_K, W_V):
            S = x.shape[1]
            D = get_D(GAMMA, S)
            Q = xpos_rope(x @ W_Q, downscale=False)
            K = xpos_rope(x @ W_K, downscale=True)
            V = x @ W_V
            ret = jnp.einsum('bnd,bmd->bnm', Q, K) * D[None, :, :]
            out = jnp.einsum('bnm,bmv->bnv', ret, V)
            return (out, ret)
        return _reference_tuple_inner(x, W_Q, W_K, W_V)[0]

    def _L1_ffn_ref(x, Wg, bg, bias, W1, b1, W2, b2):
        import jax, jax.numpy as jnp
        import numpy as np
        D_MODEL = 64
        EXPERT_DIM = 128
        NUM_EXPERTS = 8
        TOP_K = 2
        SEQ_LEN = 512
        BATCH = 2
        x_flat = x.reshape(-1, D_MODEL)
        gate_logits = x_flat @ Wg + bg + bias
        topk_vals, topk_idx = jax.lax.top_k(gate_logits, TOP_K)
        topk_w = jax.nn.softmax(topk_vals, axis=-1)
        combine = (jax.nn.one_hot(topk_idx, NUM_EXPERTS, dtype=x.dtype) * topk_w[..., None]).sum(axis=1)
        h = jax.nn.relu(jnp.einsum('td,edh->teh', x_flat, W1) + b1)
        y = jnp.einsum('teh,ehd->ted', h, W2) + b2
        out = jnp.einsum('ted,te->td', y, combine)
        return out.reshape(x.shape)
    h = _L0_tok_ref(x, L0_tok_conv1_w, L0_tok_conv1_b, L0_tok_bn_gamma, L0_tok_bn_beta, L0_tok_bn_mean, L0_tok_bn_var, L0_tok_conv2_w, L0_tok_conv2_b)
    h = jnp.concatenate([h, _L0_txt_ref(x_txt, L0_txt_A_w, L0_txt_C_w, L0_txt_U_w, L0_txt_ln_g, L0_txt_ln_b, L0_txt_W, L0_txt_b)], axis=1)
    h = h + _L0_attn_ref(_layernorm(h, axis=-1), L0_attn_gamma, L0_attn_beta, L0_attn_Wq, L0_attn_Wk, L0_attn_Wv, L0_attn_Wg, L0_attn_bg, L0_attn_Wo, L0_attn_bo)
    h = h + _L0_ffn_ref(_layernorm(h, axis=-1), L0_ffn_router_w, L0_ffn_w1, L0_ffn_b1, L0_ffn_w2, L0_ffn_b2)
    h = h + _L1_attn_ref(_layernorm(h, axis=-1), L1_attn_W_Q, L1_attn_W_K, L1_attn_W_V)
    h = h + _L1_ffn_ref(_layernorm(h, axis=-1), L1_ffn_Wg, L1_ffn_bg, L1_ffn_bias, L1_ffn_W1, L1_ffn_b1, L1_ffn_W2, L1_ffn_b2)
    return h

_drawn_inputs = setup_inputs


def setup_inputs(seed=0):
    import zlib

    import numpy as np

    out = dict(_drawn_inputs(seed))
    spreads = {'L0_tok_conv1_b': (0.0, 0.1),
     'L0_tok_bn_gamma': (1.0, 0.2),
     'L0_tok_bn_beta': (0.0, 0.1),
     'L0_tok_bn_mean': (0.0, 0.1),
     'L0_tok_bn_var': (1.0, 0.2),
     'L0_tok_conv2_b': (0.0, 0.1),
     'L0_txt_ln_g': (1.0, 0.6),
     'L0_txt_ln_b': (0.0, 0.8),
     'L0_txt_b': (0.0, 0.8),
     'L0_attn_gamma': (1.0, 0.2),
     'L0_attn_beta': (0.0, 0.1),
     'L0_attn_bg': (0.0, 0.374),
     'L0_attn_bo': (0.0, 0.1),
     'L0_ffn_b1': (0.0, 0.518),
     'L0_ffn_b2': (0.0, 0.368),
     'L1_ffn_bias': (0.0, 0.8)}
    factors = {'L0_txt_A_w': 8.0,
     'L1_ffn_Wg': 8.0,
     'L1_ffn_bg': 8.0,
     'L1_ffn_W1': 8.0,
     'L1_ffn_b1': 8.0,
     'L1_ffn_W2': 8.0,
     'L1_ffn_b2': 8.0}
    for name, (base, spread) in spreads.items():
        noise = np.random.default_rng([zlib.crc32(name.encode()), seed]).standard_normal(out[name].shape)
        drawn = base * np.exp(spread * noise) if base else spread * noise
        out[name] = jnp.asarray(drawn.astype(out[name].dtype))
    for name, factor in factors.items():
        out[name] = (out[name] * factor).astype(out[name].dtype)
    return out
```

```python
from contextlib import ExitStack
import numpy as np
import concourse.bass as bass
from concourse import mybir

F32 = mybir.dt.float32
F32R = mybir.dt.float32r
I32 = mybir.dt.int32
U32 = mybir.dt.uint32
ALU = mybir.AluOpType
ACT = mybir.ActivationFunctionType
X = mybir.AxisListType.X

P = 128
B, C, HH, WW = 4, 64, 64, 64
D = 64
TXT = 32
L = C * HH + TXT
NT = (L + P - 1) // P
TG = 3
NG = NT // TG
GT = TG * B
GW = GT * D
SETS = 3
EPS = 1e-5
HEADS, HC = 8, 32
E = 8
GAMMA = 0.96875
CP = C // 2


def walk(eng, front, back):
    front(0, 0)
    front(1, 1)
    back(0, 0)
    with eng.Fori(0, (NG - 3) // 2) as i:
        for u in (0, 1):
            front(2 * i + 2 + u, u)
            back(2 * i + 1 + u, 1 - u)
    front(NG - 1, 0)
    back(NG - 2, 1)
    back(NG - 1, 0)


def late(g, n):
    return not isinstance(g, int) or g >= n


def build(nc, a, out):
    with ExitStack() as ctx:
        top = ctx

        def sb(name, shape, dt=F32, where=None):
            return (where or ctx).enter_context(nc.sbuf_tensor(name, shape, dt))

        def sem(name):
            return ctx.enter_context(nc.semaphore(name))

        hid = sb("hid", [P, B, NT, D])
        ident = sb("ident", [P, P])
        ones = sb("ones", [P, P])
        causal = sb("causal", [P, P])
        desc = sb("desc", [P, E])
        nhalf = sb("nhalf", [P, GT])
        gam = sb("gam", [P, D])
        bet = sb("bet", [P, D])
        bo_row = sb("bo_row", [P, D])
        lgb = sb("lgb", [P, E])
        lgb2 = sb("lgb2", [P, E])
        ln_sum = sb("ln_sum", [P, 2, GT])
        ln_mean = sb("ln_mean", [P, 2, GT])
        ln_var = sb("ln_var", [P, 2, GT])
        ln_ve = sb("ln_ve", [P, 2, GT])
        ln_rs = sb("ln_rs", [P, 2, GT])
        cen = sb("cen", [P, 2, GW])
        sq = sb("sq", [P, 2, GW])
        zz = sb("zz", [P, 2, GW])

        sems = {}

        def S(name):
            if name not in sems:
                sems[name] = sem(name)
            return sems[name]

        const_ready = S("const_ready")

        def grp(g):
            return hid[:, :, bass.ds(g * TG, TG) if not isinstance(g, int) else slice(g * TG, g * TG + TG), :]

        def four(x):
            return x.rearrange("p (b t d) -> p b t d", b=B, t=TG)

        def three(x):
            return x.rearrange("p (b t) -> p b t", b=B)

        def bc(x, n):
            return x.unsqueeze(3).to_broadcast([P, B, TG, n])

        embed = ExitStack()
        XW = WW + 2
        with embed:
            rows = sb("rows", [P, 2, 3, CP, XW], F32, embed)
            xch = sb("xch", [P, HH * WW], F32, embed)
            yact = sb("yact", [32, HH * WW], F32, embed)
            wdyn = sb("wdyn", [P, 2, 9, WW], F32, embed)
            dA, dB, dC, dT, pD, pE, pT = [sb(n, [P, CP, WW], F32, embed) for n in ("dA", "dB", "dC", "dT", "pD", "pE", "pT")]
            w1c = sb("w1c", [P, 16], F32, embed)
            w2c = sb("w2c", [17, 9], F32, embed)
            bnv = sb("bnv", [16, 10], F32, embed)
            tx = {n: sb("tx_" + n, s, F32, embed) for n, s in dict(
                a=[P, D], c=[P, D], u=[P, D], uT=[D, P], aT=[D, P], s=[P, TXT], p=[P, TXT], m=[P, 8],
                g=[P, D], b=[P, D], wT=[D, D], ob=[P, D], z=[P, D], zT=[D, P], o=[P, D], q=[P, D]).items()}
            ids = sb("tx_ids", [P, 1], I32, embed)
            idc = sb("tx_idc", [P, 2], U32, embed)
        attn = ExitStack()
        with attn:
            zs1 = sb("zs1", [P, 2, GW], F32, attn)
            ztH = sb("ztH", [P, 2, NT * P], F32R, attn)
            ztL = sb("ztL", [P, 2, NT * P], F32R, attn)
            wk2 = sb("wk2", [P, 256], F32, attn)
            wq2 = sb("wq2", [P, 256], F32, attn)
            wv2 = sb("wv2", [P, 256], F32, attn)
            wgp = sb("wgp", [P, 2, 256], F32, attn)
            wgH = sb("wgH", [P, 2, 256], F32R, attn)
            wgL = sb("wgL", [P, 2, 256], F32R, attn)
            wo = sb("wo", [P, 2, D], F32, attn)
            bgc = sb("bgc", [P, 2], F32, attn)
            gramS = sb("gramS", [P, 2, 256], F32, attn)
            prodX = sb("prodX", [P, 8, 256], F32, attn)
            part = sb("part", [P, 64], F32, attn)
            at = sb("at", [P, P], F32, attn)
            at2 = sb("at2", [P, P], F32, attn)
            atm = sb("atm", [P, 4 * HEADS], F32, attn)
            wmix = sb("wmix", [P, B, 2, 256], F32, attn)
            wmH = sb("wmH", [P, B, 2, 256], F32R, attn)
            wmL = sb("wmL", [P, B, 2, 256], F32R, attn)
            sig = sb("sig", [P, 2, TG * P], F32, attn)
            og = sb("og", [P, 2, 2, TG * P], F32, attn)
        deep = ExitStack()
        with deep:
            zst = sb("zst", [P, 2, GT, 2, D], F32R, deep)
            zt = sb("zt", [P, 2, GT * P], F32R, deep)
            lg = sb("lg", [P, 12, GT * E], F32, deep)
            rt = sb("rt", [P, 8, GT], F32, deep)
            comb = sb("comb", [P, 2, GT * E], F32, deep)
            wr = sb("wr", [P, 2, E], F32, deep)
            wrH = sb("wrH", [P, 2, E], F32R, deep)
            wrL = sb("wrL", [P, 2, E], F32R, deep)
            fw1 = sb("fw1", [P, E * D], F32, deep)
            fw1H = sb("fw1H", [P, E * D], F32R, deep)
            fw1L = sb("fw1L", [P, E * D], F32R, deep)
            fb1 = sb("fb1", [P, 4], F32, deep)
            fw2 = sb("fw2", [P, 4, P], F32, deep)
            gw1 = sb("gw1", [P, E * P], F32, deep)
            gw1H = sb("gw1H", [P, E * P], F32R, deep)
            gw1L = sb("gw1L", [P, E * P], F32R, deep)
            gb1 = sb("gb1", [P, E], F32, deep)
            gw2 = sb("gw2", [P, E, D], F32, deep)
            bias2 = sb("bias2", [D, 2, E * D], F32, deep)
            b2sp = sb("b2sp", [D, 2, E * D], F32R, deep)
            onesR = sb("onesR", [D, P], F32R, deep)
            hact = sb("hact", [P, 2, E, 512], F32, deep)
            prod = sb("prod", [P, 2, 4, E * D], F32, deep)
            tree = sb("tree", [P, 4, 4 * D], F32, deep)
            tree2 = sb("tree2", [P, 4, 2 * D], F32, deep)
            ysum = sb("ysum", [P, 2, GW], F32, deep)
            NQ = 5 * D
            wqk = sb("wqk", [P, NQ], F32, deep)
            wqkH = sb("wqkH", [P, NQ], F32R, deep)
            wqkL = sb("wqkL", [P, NQ], F32R, deep)
            tabc = sb("tabc", [P, 2, 2 * TG, 2 * D], F32, deep)
            rA = sb("rA", [P, 2, B, D], F32, deep)
            rB = sb("rB", [P, 2, B, D], F32, deep)
            rot = sb("rot", [P, 2, 2, B, D], F32, deep)
            val = sb("val", [P, 2, B, D], F32, deep)
            qkT = sb("qkT", [P, 2, 4, P], F32, deep)
            pmat = sb("pmat", [P, 2, B, P], F32, deep)
            state = sb("state", [P, B, D], F32, deep)
            stt = sb("stt", [P, 2, D], F32, deep)

        ps = ctx.enter_context(nc.psum_tensor("ps", [P, 8, 512], F32))

        block = ctx.enter_context(nc.Block())
        A = a

        def gram_pe(pe):
            pe.wait_ge(S("txt_put"), 16 * B)

            def nothing(g, par):
                pass

            def back(g, par):
                z = zs1[:, par].rearrange("p (t b d) -> p t b d", b=B, t=TG)
                pe.wait_ge(S("z1_ready"), g + 1)
                if late(g, 1):
                    pe.wait_ge(S("zt_split"), g)
                for pair in range(2):
                    for t in range(TG):
                        mm = pe.transpose(ps[:, 2 + pair, P * t:P * t + P], z[:, t, 2 * pair:2 * pair + 2, :].rearrange("p b d -> p (b d)"), ident[:, :])
                mm.then_inc(S("z1_turned"), 1)
                for t in range(TG):
                    rows_ = TXT if isinstance(g, int) and g == NG - 1 and t == TG - 1 else P
                    for m in range(2):
                        first = isinstance(g, int) and g == 0 and t == 0
                        last = isinstance(g, int) and g == NG - 1 and t == TG - 1
                        mm = pe.matmul(ps[:, m, 0:256], z[0:rows_, t, 2 * m:2 * m + 2, :].rearrange("p b d -> p (b d)"), z[0:rows_, t, :, :],
                                       start=first, stop=last, skip_group_check=True)
                mm.then_inc(S("gram_mm"), 1)

            walk(pe, nothing, back)
            pe.wait_ge(S("gram_out"), 1)
            pe.wait_ge(S("attw_in"), 16 * 10)
            for m in range(2):
                for t in range(B):
                    h = 64 * (t % 2)
                    mm = pe.matmul(ps[:, 4 + 2 * m + t % 2, 256 * (t // 2):256 * (t // 2) + 256], gramS[h:h + 64, t // 2, P * m:P * m + P],
                                   wk2[h:h + 64, :], start=True, stop=True, skip_group_check=True)
            mm.then_inc(S("x_ready"), 1)
            pe.wait_ge(S("part_ready"), 1)
            for s in range(B):
                h = 64 * (s % 2)
                mm = pe.matmul(ps[:, 2 + s % 2, 32 * (s // 2):32 * (s // 2) + 32], ones[h:h + 64, :], part[h:h + 64, 32 * (s // 2):32 * (s // 2) + 32],
                               start=True, stop=True, skip_group_check=True)
            mm.then_inc(S("att_ready"), 1)
            pe.wait_ge(S("wmix_ready"), 1)

            def mix(g, par):
                for s in range(B):
                    for mc in range(2):
                        k = 2 * s + mc
                        if late(g, 1) or k >= 2:
                            pe.wait_ge(S("og_ready"), 8 * g + k - 1)
                        cs = slice(P * mc, P * mc + P)
                        tok = bass.ds(g * TG * P, TG * P) if not isinstance(g, int) else slice(g * TG * P, (g + 1) * TG * P)
                        n = 0
                        for pair in range(2):
                            for w, z in ((wmH, ztH), (wmH, ztL), (wmL, ztH)):
                                pe.matmul(ps[:, mc, 0:TG * P], w[:, s, pair, cs], z[:, pair, tok], start=(n == 0), stop=(n == 5))
                                n += 1
                        for n, (w, z) in enumerate(((wgH, ztH), (wgH, ztL), (wgL, ztH))):
                            mm = pe.matmul(ps[:, 2 + mc, 0:TG * P], w[:, s % 2, cs], z[:, s // 2, tok], start=(n == 0), stop=(n == 2))
                        mm.then_inc(S("mix_ready"), 1)
                    if late(g, 1) or s >= 1:
                        project(4 * g + s - 1, (s - 1) % 2, (s - 1) % 2)

            def project(k, slot, bank):
                pe.wait_ge(S("og_ready"), 2 * k + 2)
                if not isinstance(k, int) or k >= 2:
                    pe.wait_ge(S("att_added"), k - 1)
                for t in range(TG):
                    for mc in range(2):
                        mm = pe.matmul(ps[:, 4 + bank, D * t:D * t + D], og[:, slot, mc, P * t:P * t + P], wo[:, mc, :],
                                       start=(mc == 0), stop=(mc == 1), skip_group_check=True)
                mm.then_inc(S("proj_ready"), 1)

            mix(0, 0)
            with pe.Fori(1, NG) as g:
                mix(g, 0)
            project(4 * NG - 1, 1, 1)

        def ln_vector(v, ph, g, par, k1, k0):
            link = chain(v, ph + "mean_v", g, 2)
            link(v.tensor_reduce(three(ln_sum[:, par]), grp(g), X, ALU.add))
            link(v.tensor_scalar(ln_mean[:, par], ln_sum[:, par], 1.0 / D, None, ALU.mult))
            v.tensor_tensor(four(cen[:, par]), grp(g), bc(three(ln_mean[:, par]), D), ALU.subtract).then_inc(S(ph + "cen_ready"), 1)

        def ln_vector2(v, ph, g, par, k1, k0, dst, used):
            v.wait_ge(S(ph + "sq_ready"), g + 1)
            link = chain(v, ph + "var_v", g, 1)
            link(v.tensor_reduce(three(ln_var[:, par]), four(sq[:, par]), X, ALU.add))
            v.tensor_scalar(ln_ve[:, par], ln_var[:, par], k1, k0, ALU.mult, ALU.add).then_inc(S(ph + "ve_ready"), 1)
            v.wait_ge(S(ph + "rs_ready"), g + 1)
            used(g)
            v.tensor_tensor(four(dst[:, par]), four(cen[:, par]), bc(three(ln_rs[:, par]), D), ALU.mult).then_inc(S(ph + "z_ready"), 1)

        def chain(eng, name, g, per, start=0):
            k = [start]

            def link(ins):
                k[0] += 1
                ins.then_inc(S(name), 1)
                eng.wait_ge(S(name), g * per + k[0])
            return link

        def ln_scalar(s, ph, g, par):
            s.wait_ge(S(ph + "cen_ready"), g + 1)
            s.activation(sq[:, par], cen[:, par], ACT.Square).then_inc(S(ph + "sq_ready"), 1)

        def ln_pool(p, ph, g, par):
            p.wait_ge(S(ph + "ve_ready"), g + 1)
            p.tensor_tensor(ln_rs[:, par], ln_ve[:, par], nhalf[:, :], ALU.pow).then_inc(S(ph + "rs_ready"), 1)

        def turn_pe(pe, ph, g, par):
            pe.wait_ge(S(ph + "zl_ready"), g + 1)
            for q in range(SETS):
                if late(g, 1) or q >= 2:
                    pe.wait_ge(S(ph + "zt_ready"), SETS * g + q - 1)
                for j in range(4):
                    mm = pe.transpose(ps[:, 5 + q % 2, P * j:P * j + P] if (q % 2 == 0) else ps[:, 6, P * j:P * j + P],
                                      zst[:, par, 4 * q + j].rearrange("p s d -> p (s d)").bitcast(F32), ident[:, :])
                mm.then_inc(S(ph + "tp_ready"), 1)

        def moe_pe(pe, ph, CH):
            lay = 0 if ph == "m" else 1
            w1H, w1L = (fw1H, fw1L) if lay == 0 else (gw1H, gw1L)
            pe.wait_ge(S("deep_ready"), 1)

            def front(g, par):
                turn_pe(pe, ph, g, par)
                pe.wait_ge(S(ph + "zt_ready"), SETS * g + SETS)
                if late(g, 1):
                    pe.wait_ge(S(ph + "lg_read"), g)
                for j in range(GT):
                    for n, w in enumerate((wrH, wrL)):
                        mm = pe.matmul(ps[:, 7, E * j:E * j + E], zt[:, par, P * j:P * j + P], w[:, lay, :], start=(n == 0), stop=(n == 1),
                                       skip_group_check=True)
                mm.then_inc(S(ph + "lg_ready"), 1)

            def hidden(g, par, q):
                for c in range(CH):
                    k = CH * q + c
                    if late(g, 1) or k >= 3:
                        pe.wait_ge(S(ph + "h_ready"), SETS * CH * g + k - 2)
                    for n, w in enumerate((w1H, w1L)):
                        mm = pe.matmul(ps[:, k % 3, :], w[:, P * c:P * c + P], zt[:, par, 512 * q:512 * q + 512], start=(n == 0), stop=(n == 1))
                    mm.then_inc(S(ph + "h_mm"), 1)

            def outputs(g, q, slot):
                pe.wait_ge(S(ph + "h_ready"), SETS * CH * g + CH * q + CH)
                for j in range(4):
                    k = 4 * q + j
                    if late(g, 1) or k >= 2:
                        pe.wait_ge(S(ph + "y_used"), GT * g + k - 1)
                    y = ps[:, 3 + k % 2, :]
                    pe.matmul(y, onesR[:, :], b2sp[:, lay, :], start=True, stop=False, skip_group_check=True)
                    for c in range(CH):
                        if CH == 4:
                            mm = pe.matmul(y[:, P * c:P * c + P], hact[:, slot, c, P * j:P * j + P], fw2[:, c, :], start=False, stop=(c == CH - 1),
                                           skip_group_check=True)
                        else:
                            mm = pe.matmul(y[:, D * c:D * c + D], hact[:, slot, c, P * j:P * j + P], gw2[:, c, :], start=False, stop=(c == CH - 1),
                                           skip_group_check=True)
                    mm.then_inc(S(ph + "y_ready"), 1)

            def step(g, par, ahead):
                for q in range(SETS):
                    if q == 2 and ahead is not None:
                        front(ahead, 1 - par)
                    hidden(g, par, q)
                    if q or late(g, 1):
                        outputs(g if q else g - 1, (q - 1) % SETS, (par + q + 1) % 2)

            front(0, 0)
            step(0, 0, 1)
            with pe.Fori(0, (NG - 3) // 2) as i:
                for u in (0, 1):
                    step(2 * i + 1 + u, 1 - u, 2 * i + 2 + u)
            step(NG - 2, 1, NG - 1)
            step(NG - 1, 0, None)
            outputs(NG - 1, SETS - 1, 0)

        def ret_pe(pe):
            def turn(g, par):
                pe.wait_ge(S("rzl_ready"), g + 1)
                for q in range(SETS):
                    if late(g, 1) or q >= 1:
                        pe.wait_ge(S("rzt_ready"), SETS * g + q)
                    for j in range(4):
                        mm = pe.transpose(ps[:, 7, P * j:P * j + P], zst[:, par, 4 * q + j].rearrange("p s d -> p (s d)").bitcast(F32), ident[:, :])
                    mm.then_inc(S("rtp_ready"), 1)

            def project(g, par, t):
                k = TG * g + t
                pe.wait_ge(S("rzt_ready"), SETS * g + SETS)
                if late(g, 1) or t >= 1:
                    pe.wait_ge(S("rope_read"), k)
                    pe.wait_ge(S("val_ready"), k)
                for b in range(B):
                    zb = zt[:, par, P * (TG * b + t):P * (TG * b + t) + P]
                    for dst, c in ((ps[:, b // 2, 256 * (b % 2):256 * (b % 2) + 256], slice(0, 4 * D)), (ps[:, 2, D * b:D * b + D], slice(4 * D, NQ))):
                        for n, w in enumerate((wqkH, wqkL)):
                            mm = pe.matmul(dst, zb, w[:, c], start=(n == 0), stop=(n == 1), skip_group_check=True)
                mm.then_inc(S("qkv_mm"), 1)

            def attend(g, t, sl):
                k = TG * g + t
                pe.wait_ge(S("rot_ready"), k + 1)
                if late(g, 1) or t >= 1:
                    pe.wait_ge(S("qkT_ready"), k)
                for pair in range(2):
                    for n in range(2):
                        mm = pe.transpose(ps[:, 4, P * (2 * pair + n):P * (2 * pair + n) + P], rot[:, sl, n, 2 * pair:2 * pair + 2, :].rearrange("p b d -> p (b d)"), ident[:, :])
                mm.then_inc(S("qkT_mm"), 1)
                if late(g, 1) or t >= 1:
                    pe.wait_ge(S("ret_added"), k)
                    pe.wait_ge(S("state_ready"), k)
                pe.wait_ge(S("val_ready"), k + 1)
                for pair in range(2):
                    pe.matmul(ps[:, 3, 256 + P * pair:256 + P * pair + P], rot[:, sl, 1, 2 * pair:2 * pair + 2, :].rearrange("p b d -> p (b d)"), val[:, sl, 2 * pair:2 * pair + 2, :],
                              start=True, stop=True, skip_group_check=True)
                pe.wait_ge(S("qkT_ready"), k + 1)
                if late(g, 1) or t >= 1:
                    pe.wait_ge(S("pmat_ready"), k)
                for b in range(B):
                    h = slice(64 * (b % 2), 64 * (b % 2) + 64)
                    mm = pe.matmul(ps[:, 5 + b % 2, P * (b // 2):P * (b // 2) + P], qkT[h, sl, 2 * (b // 2) + 1, :], qkT[h, sl, 2 * (b // 2), :], start=True, stop=True,
                                   skip_group_check=True)
                mm.then_inc(S("score_mm"), 1)
                for b in range(B):
                    if b == 0:
                        pe.wait_ge(S("state_ready"), k) if late(g, 1) or t >= 1 else pe.wait_ge(S("deep_ready"), 1)
                    mm = pe.matmul(ps[:, 3, D * b:D * b + D], qkT[:, sl, 2 * (b // 2), :], state[:, b, :], start=True, stop=False,
                                   skip_group_check=True)
                    if b == 0:
                        pe.wait_ge(S("pmat_ready"), k + 1)
                    mm = pe.matmul(ps[:, 3, D * b:D * b + D], pmat[:, sl, b, :], val[:, sl, b, :], start=False, stop=True,
                                   skip_group_check=True)
                mm.then_inc(S("ret_mm"), 1)

            def step(g, par, ahead):
                for t in range(TG):
                    if t == 1 and ahead is not None:
                        turn(ahead, 1 - par)
                    if t < TG - 1:
                        project(g, par, t + 1)
                    elif ahead is not None:
                        project(ahead, 1 - par, 0)
                    attend(g, t, (par + t) % 2)

            turn(0, 0)
            project(0, 0, 0)
            step(0, 0, 1)
            with pe.Fori(0, (NG - 3) // 2) as i:
                for u in (0, 1):
                    step(2 * i + 1 + u, 1 - u, 2 * i + 2 + u)
            step(NG - 2, 1, NG - 1)
            step(NG - 1, 0, None)

        def attn_v(v):
            def front(g, par):
                ln_vector(v, "a", g, par, 0, 0)

            def back(g, par):
                def used(g):
                    pass
                ln_vector2(v, "a", g, par, (1.0 + EPS) / D, EPS * EPS, zz, used)
                v.wait_ge(S("z1h_ready"), g + 1)
                tok = bass.ds(g * TG * P, TG * P) if not isinstance(g, int) else slice(g * TG * P, (g + 1) * TG * P)
                for pair in range(2):
                    ins = v.tensor_tensor(ztL[:, pair, tok], ps[:, 2 + pair, 0:TG * P], ztH[:, pair, tok].bitcast(F32), ALU.subtract)
                ins.then_inc(S("zt_split"), 1)

            walk(v, front, back)
            v.wait_ge(S("gram_mm"), NG)
            v.tensor_copy(gramS[:, :, :], ps[:, 0:2, 0:256]).then_inc(S("gram_out"), 1)
            v.wait_ge(S("attw_in"), 16 * 10)
            link = chain(v, "v_mid", 0, 0)
            link(v.tensor_scalar(wgH[:, :, :], wgp[:, :, :], 1.0, None, ALU.mult))
            link(v.tensor_tensor(wgL[:, :, :], wgp[:, :, :], wgH[:, :, :].bitcast(F32), ALU.subtract))
            v.wait_ge(S("x_ready"), 1)
            for h in range(2):
                link(v.tensor_tensor(prodX[:, 4 * h:4 * h + 4, :].rearrange("p (s r) c -> p r s c", r=2), ps[:, 4 + 2 * h:6 + 2 * h, :].rearrange("p r (s c) -> p r s c", s=2),
                                     wq2[:, :].unsqueeze(1).unsqueeze(1).to_broadcast([P, 2, 2, 256]), ALU.mult))
            v.tensor_reduce(part[:, :], prodX[:, :, :].rearrange("p m (h c) -> p (m h) c", c=HC), X, ALU.add).then_inc(S("part_ready"), 1)
            v.wait_ge(S("att_ready"), 1)
            SC = 1.0 / np.sqrt(HC) / np.sqrt(L)
            a4 = at[:, :].rearrange("p (s t h) -> p s t h", s=B, t=B)
            b4 = at2[:, :].rearrange("p (s t h) -> p s t h", s=B, t=B)
            m3 = atm[:, :].rearrange("p (s h) -> p s h", s=B)
            link(v.tensor_scalar(at[:, :].rearrange("p (q r x) -> p r q x", q=2, r=2), ps[:, 2:4, 0:64].rearrange("p r (q x) -> p r q x", q=2), float(SC), None, ALU.mult))
            link(v.tensor_reduce(m3, a4.rearrange("p s t h -> p s h t"), X, ALU.max))
            v.tensor_tensor(a4, a4, m3.unsqueeze(2).to_broadcast([P, B, B, HEADS]), ALU.subtract).then_inc(S("att_sub"), 1)
            v.wait_ge(S("att_exp"), 1)
            link(v.tensor_reduce(m3, b4.rearrange("p s t h -> p s h t"), X, ALU.add))
            link(v.reciprocal(atm[:, :], atm[:, :]))
            link(v.tensor_tensor(b4, b4, m3.unsqueeze(2).to_broadcast([P, B, B, HEADS]), ALU.mult))
            for s in range(B):
                for pair in range(2):
                    for h in range(2):
                        r = slice(64 * h, 64 * h + 64)
                        ins = v.tensor_tensor(wmix[r, s, pair, :].rearrange("p (h c) -> p h c", c=HC), wv2[r, :].rearrange("p (h c) -> p h c", c=HC),
                                              b4[r, s, 2 * pair + h, :].unsqueeze(2).to_broadcast([64, HEADS, HC]), ALU.mult)
            link(ins)
            link(v.tensor_scalar(wmH[:, :, :, :], wmix[:, :, :, :], 1.0, None, ALU.mult))
            v.tensor_tensor(wmL[:, :, :, :], wmix[:, :, :, :], wmH[:, :, :, :].bitcast(F32), ALU.subtract).then_inc(S("wmix_ready"), 1)
            v.wait_ge(S("bo_added"), 1)

            def gate(g):
                for s in range(B):
                    for mc in range(2):
                        k = 2 * s + mc
                        v.wait_ge(S("sig_ready"), 8 * g + k + 1)
                        if (late(g, 1) or s >= 2) and mc == 0:
                            v.wait_ge(S("proj_ready"), 4 * g + s - 1)
                        v.tensor_tensor(og[:, s % 2, mc, :], sig[:, mc, :], ps[:, mc, 0:TG * P], ALU.mult).then_inc(S("og_ready"), 1)
                    if late(g, 1) or s >= 1:
                        add(g if s else g - 1, (s - 1) % B, 4 * g + s - 1)

            def add(g, s, k):
                v.wait_ge(S("proj_ready"), k + 1)
                dst = hid[:, s, bass.ds(g * TG, TG) if not isinstance(g, int) else slice(g * TG, g * TG + TG), :]
                v.tensor_tensor(dst, dst, ps[:, 4 + s % 2, 0:TG * D].rearrange("p (t d) -> p t d", d=D), ALU.add).then_inc(S("att_added"), 1)

            gate(0)
            with v.Fori(1, NG) as g:
                gate(g)
            add(NG - 1, B - 1, 4 * NG - 1)
            v.wait_ge(S("att_added"), 4 * NG)
            v.sem_inc(S("attn_free"), 1)

        def deep_prep_v(v):
            v.memset(fw2[:, :, :], 0.0).then_inc(S("fw2_zero"), 1)
            link = chain(v, "v_deep", 0, 0)
            link(v.tensor_scalar(onesR[:, :], ones[0:D, :], 1.0, None, ALU.mult))
            v.wait_ge(S("deepw_in"), 16 * (14 + 3 + 8))
            link(v.memset(b2sp[:, :, :].bitcast(F32), 0.0))
            for src, hi, lo in ((wr, wrH, wrL), (fw1, fw1H, fw1L), (gw1, gw1H, gw1L), (wqk, wqkH, wqkL)):
                i = tuple(slice(None) for _ in src.shape)
                link(v.tensor_scalar(hi[i], src[i], 1.0, None, ALU.mult))
                link(v.tensor_tensor(lo[i], src[i], hi[i].bitcast(F32), ALU.subtract))
            link(v.tensor_scalar(b2sp[0:1, :, :], bias2[0:1, :, :], 1.0, None, ALU.mult))
            link(v.tensor_scalar(b2sp[32:33, :, :], bias2[32:33, :, :], 1.0, None, ALU.mult))
            link(v.tensor_tensor(b2sp[32:33, :, :], bias2[32:33, :, :], b2sp[32:33, :, :].bitcast(F32), ALU.subtract))
            link(v.memset(state[:, :, :], 0.0))
            link(v.tensor_tensor(lgb[:, :], lgb[:, :], lgb2[:, :], ALU.add))
            for e in range(E):
                ins = v.memset(desc[:, e:e + 1], float(E - e))
            link(ins)
            v.sem_inc(S("deep_ready"), 1)

        def moe_v(v, ph, CH):
            def lnA(g, par):
                ln_vector(v, ph, g, par, 0, 0)

            def lnB(g, par):
                def used(g):
                    if late(g, 2):
                        v.wait_ge(S(ph + "zl_ready"), g - 1)
                ln_vector2(v, ph, g, par, 1.0 / D, EPS, zz, used)

            def route(g, par):
                R = lambda n: lg[:, n, :].rearrange("p (j e) -> p j e", e=E)
                bce = lambda x: x.unsqueeze(2).to_broadcast([P, GT, E])
                row = lambda x: x.unsqueeze(1).to_broadcast([P, GT, E])
                link = chain(v, ph + "rt_v", g, 14)
                v.wait_ge(S(ph + "lg_ready"), g + 1)
                src = ps[:, 7, 0:GT * E].rearrange("p (j e) -> p j e", e=E)
                if ph == "x":
                    v.tensor_tensor(R(0), src, row(lgb[:, :]), ALU.add).then_inc(S(ph + "lg_read"), 1)
                else:
                    v.tensor_copy(R(0), src).then_inc(S(ph + "lg_read"), 1)
                v.wait_ge(S(ph + "lg_read"), g + 1)
                cur = 0
                for n in range(2):
                    link(v.tensor_reduce(rt[:, n, :], R(cur), X, ALU.max))
                    link(v.tensor_tensor(R(1), R(cur), bce(rt[:, n, :]), ALU.is_equal))
                    link(v.tensor_tensor(R(1), R(1), row(desc[:, :]), ALU.mult))
                    link(v.tensor_reduce(rt[:, 2, :], R(1), X, ALU.max))
                    link(v.tensor_tensor(R(2 + n), R(1), bce(rt[:, 2, :]), ALU.is_equal))
                    if n == 0:
                        link(v.scalar_tensor_tensor(lg[:, 4, :], lg[:, 2, :], -1e30, lg[:, 0, :], ALU.mult, ALU.add))
                        cur = 4
                v.tensor_tensor(rt[:, 3, :], rt[:, 0, :], rt[:, 1, :], ALU.subtract).then_inc(S(ph + "gap_ready"), 1)
                v.wait_ge(S(ph + "tanh_ready"), g + 1)
                link(v.tensor_scalar(rt[:, 5, :], rt[:, 4, :], 0.5, 0.5, ALU.mult, ALU.add))
                link(v.tensor_scalar(rt[:, 6, :], rt[:, 4, :], -0.5, 0.5, ALU.mult, ALU.add))
                v.tensor_tensor(R(2), R(2), bce(rt[:, 5, :]), ALU.mult)
                link(v.tensor_tensor(R(3), R(3), bce(rt[:, 6, :]), ALU.mult))
                v.tensor_tensor(comb[:, par], lg[:, 2, :], lg[:, 3, :], ALU.add).then_inc(S(ph + "comb_ready"), 1)
                v.wait_ge(S(ph + "comb_ready"), g + 1)

            def scale(g, par, q, slot):
                if late(g, 1) or q >= 2:
                    v.wait_ge(S(ph + "prod_used"), SETS * g + q - 1)
                for j in range(4):
                    k = 4 * q + j
                    v.wait_ge(S(ph + "y_ready"), GT * g + k + 1)
                    v.tensor_tensor(prod[:, slot, j, :].rearrange("p (e d) -> p e d", d=D), ps[:, 3 + k % 2, :].rearrange("p (e d) -> p e d", d=D),
                                    comb[:, par, E * k:E * k + E].unsqueeze(2).to_broadcast([P, E, D]), ALU.mult).then_inc(S(ph + "y_used"), 1)

            def step(g, par, ahead):
                if ahead is not None:
                    lnA(ahead, 1 - par)
                if late(g, 1):
                    scale(g - 1, 1 - par, SETS - 1, (par + 1) % 2)
                if ahead is not None:
                    lnB(ahead, 1 - par)
                scale(g, par, 0, par)
                scale(g, par, 1, (par + 1) % 2)
                if ahead is not None:
                    route(ahead, 1 - par)

            if ph == "x":
                v.wait_ge(S("ret_added"), NT)
            lnA(0, 0)
            lnB(0, 0)
            route(0, 0)
            step(0, 0, 1)
            with v.Fori(0, (NG - 3) // 2) as i:
                for u in (0, 1):
                    step(2 * i + 1 + u, 1 - u, 2 * i + 2 + u)
            step(NG - 2, 1, NG - 1)
            step(NG - 1, 0, None)
            scale(NG - 1, 0, SETS - 1, 0)

        def ret_v(v):
            def lnA(g, par):
                ln_vector(v, "r", g, par, 0, 0)

            def lnB(g, par):
                def used(g):
                    if late(g, 2):
                        v.wait_ge(S("rzl_ready"), g - 1)
                ln_vector2(v, "r", g, par, 1.0 / D, EPS, zz, used)

            def rope(g, par, t, sl):
                k = TG * g + t
                if t == 0:
                    v.wait_ge(S("tab_in%d" % par), 16 * (g // 2 + 1) if isinstance(g, int) else 8 * (g - par) + 16)
                v.wait_ge(S("qkv_mm"), k + 1)
                if late(g, 1) or t >= 1:
                    v.wait_ge(S("rot_ready"), k)
                tb = lambda n: tabc[:, par, 2 * t + n, :].rearrange("p (n d) -> p n d", n=2).unsqueeze(1).to_broadcast([P, B, 2, D])
                q4 = lambda c: ps[:, 0:2, :].rearrange("p a (c y) -> p (a c) y", c=2)[:, :, c:c + 2 * D].rearrange("p b (n d) -> p b n d", n=2)
                v.tensor_tensor(rA[:, :, :, :].rearrange("p n b d -> p b n d"), q4(0), tb(0), ALU.mult)
                v.tensor_tensor(rB[:, :, :, :].rearrange("p n b d -> p b n d"), q4(2 * D), tb(1), ALU.mult).then_inc(S("rope_read"), 1)

            def after(g, t, sl):
                k = TG * g + t
                v.wait_ge(S("score_mm"), k + 1)
                v.tensor_tensor(pmat[:, sl, :, :].rearrange("p (j r) n -> p r j n", r=2), ps[:, 5:7, 0:256].rearrange("p r (j n) -> p r j n", j=2), causal[:, :].unsqueeze(1).unsqueeze(1).to_broadcast([P, 2, 2, P]),
                                ALU.mult).then_inc(S("pmat_ready"), 1)
                v.wait_ge(S("ret_mm"), k + 1)
                for h in range(2):
                    r = slice(64 * h, 64 * h + 64)
                    own = state[r, :, :].rearrange("p (j r) d -> p r j d", r=2)[:, h]
                    kv = ps[r, 3, 256:512].rearrange("p (j c) -> p j c", j=2)[:, :, D * h:D * h + D]
                    ins = v.tensor_tensor(stt[r, :, :], own, kv, ALU.add)
                ins.then_inc(S("stt_v"), 1)
                dst = hid[:, :, bass.ds(k, 1) if not isinstance(k, int) else slice(k, k + 1), :].rearrange("p b t d -> p b (t d)")
                v.tensor_tensor(dst, dst, ps[:, 3, 0:256].rearrange("p (b d) -> p b d", b=B), ALU.add).then_inc(S("ret_added"), 1)
                v.wait_ge(S("stt_v"), k + 1)
                for h in range(2):
                    r = slice(64 * h, 64 * h + 64)
                    own = state[r, :, :].rearrange("p (j r) d -> p r j d", r=2)[:, h]
                    ins = v.tensor_scalar(own, stt[r, :, :], float(GAMMA ** P), None, ALU.mult)
                ins.then_inc(S("state_ready"), 1)

            def step(g, par, ahead):
                for t in range(TG):
                    sl = (par + t) % 2
                    if ahead is not None and t == 0:
                        lnA(ahead, 1 - par)
                        lnB(ahead, 1 - par)
                    if t < TG - 1:
                        rope(g, par, t + 1, 1 - sl)
                    elif ahead is not None:
                        rope(ahead, 1 - par, 0, 1 - sl)
                    after(g, t, sl)

            v.wait_ge(S("mh_added"), NG)
            lnA(0, 0)
            lnB(0, 0)
            rope(0, 0, 0, 0)
            step(0, 0, 1)
            with v.Fori(0, (NG - 3) // 2) as i:
                for u in (0, 1):
                    step(2 * i + 1 + u, 1 - u, 2 * i + 2 + u)
            step(NG - 2, 1, NG - 1)
            step(NG - 1, 0, None)

        def attn_s(s):
            def front(g, par):
                ln_scalar(s, "a", g, par)

            def back(g, par):
                tok = bass.ds(g * TG * P, TG * P) if not isinstance(g, int) else slice(g * TG * P, (g + 1) * TG * P)
                s.wait_ge(S("z1_turned"), g + 1)
                s.activation(ztH[:, :, tok], ps[:, 2:4, 0:TG * P], ACT.Copy).then_inc(S("z1h_ready"), 1)

            walk(s, front, back)
            s.wait_ge(S("att_sub"), 1)
            s.activation(at2[:, :], at[:, :], ACT.Exp).then_inc(S("att_exp"), 1)

            def gate(g):
                for k in range(8):
                    s.wait_ge(S("mix_ready"), 8 * g + k + 1)
                    if late(g, 1) or k >= 2:
                        s.wait_ge(S("og_ready"), 8 * g + k - 1)
                    s.activation(sig[:, k % 2, :], ps[:, 2 + k % 2, 0:TG * P], ACT.Sigmoid, bias=bgc[:, k % 2:k % 2 + 1]).then_inc(S("sig_ready"), 1)

            gate(0)
            with s.Fori(1, NG) as g:
                gate(g)

        def split_s(s, ph, g, par, turned):
            s.wait_ge(S(ph + "z_ready"), g + 1)
            if late(g, 2):
                s.wait_ge(S(ph + "tp_ready"), SETS * (g - 1))
            s.activation(zst[:, par, :, 0, :], zz[:, par].rearrange("p (j d) -> p j d", d=D), ACT.Copy).then_inc(S(ph + "zh_ready"), 1)

        def evac_s(s, ph, g, par, banks):
            for q in range(SETS):
                s.wait_ge(S(ph + "tp_ready"), SETS * g + q + 1)
                s.activation(zt[:, par, 512 * q:512 * q + 512], ps[:, banks[q % len(banks)], :], ACT.Copy).then_inc(S(ph + "zt_ready"), 1)

        def moe_s(s, ph, CH):
            bias = fb1 if ph == "m" else gb1
            fn = ACT.Gelu if ph == "m" else ACT.Relu
            s.wait_ge(S("deep_ready"), 1)

            def act(g, q, slot):
                for c in range(CH):
                    k = CH * q + c
                    s.wait_ge(S(ph + "h_mm"), SETS * CH * g + k + 1)
                    if (late(g, 1) or q >= 2) and c == 0:
                        s.wait_ge(S(ph + "y_ready"), GT * g + 4 * q - 4)
                    s.activation(hact[:, slot, c, :], ps[:, k % 3, :], fn, bias=bias[:, c:c + 1]).then_inc(S(ph + "h_ready"), 1)

            def tail(g, par):
                evac_s(s, ph, g, par, (5, 6))
                s.wait_ge(S(ph + "gap_ready"), g + 1)
                s.activation(rt[:, 4, :], rt[:, 3, :], ACT.Tanh, scale=0.5).then_inc(S(ph + "tanh_ready"), 1)

            def step(g, par, ahead):
                if ahead is not None:
                    ln_scalar(s, ph, ahead, 1 - par)
                act(g, 0, par)
                if ahead is not None:
                    split_s(s, ph, ahead, 1 - par, None)
                act(g, 1, 1 - par)
                if ahead is not None:
                    evac_s(s, ph, ahead, 1 - par, (5, 6))
                act(g, 2, par)
                if ahead is not None:
                    s.wait_ge(S(ph + "gap_ready"), ahead + 1)
                    s.activation(rt[:, 4, :], rt[:, 3, :], ACT.Tanh, scale=0.5).then_inc(S(ph + "tanh_ready"), 1)

            ln_scalar(s, ph, 0, 0)
            split_s(s, ph, 0, 0, None)
            tail(0, 0)
            step(0, 0, 1)
            with s.Fori(0, (NG - 3) // 2) as i:
                for u in (0, 1):
                    step(2 * i + 1 + u, 1 - u, 2 * i + 2 + u)
            step(NG - 2, 1, NG - 1)
            step(NG - 1, 0, None)

        def ret_s(s):
            def values(g, t, sl):
                k = TG * g + t
                s.wait_ge(S("qkv_mm"), k + 1)
                if late(g, 1) or t >= 2:
                    s.wait_ge(S("ret_mm"), k - 1)
                s.activation(val[:, sl, :, :], ps[:, 2, 0:4 * D].rearrange("p (b d) -> p b d", b=B), ACT.Copy).then_inc(S("val_ready"), 1)

            def turned(g, t, sl):
                k = TG * g + t
                s.wait_ge(S("qkT_mm"), k + 1)
                s.activation(qkT[:, sl, :, :], ps[:, 4, :].rearrange("p (n q) -> p n q", n=4), ACT.Copy).then_inc(S("qkT_ready"), 1)

            def step(g, par, ahead):
                for t in range(TG):
                    sl = (par + t) % 2
                    if ahead is not None and t == 0:
                        ln_scalar(s, "r", ahead, 1 - par)
                        split_s(s, "r", ahead, 1 - par, None)
                    if ahead is not None and t == 1:
                        evac_s(s, "r", ahead, 1 - par, (7,))
                    if t < TG - 1:
                        values(g, t + 1, 1 - sl)
                    elif ahead is not None:
                        values(ahead, 0, 1 - sl)
                    turned(g, t, sl)

            ln_scalar(s, "r", 0, 0)
            split_s(s, "r", 0, 0, None)
            evac_s(s, "r", 0, 0, (7,))
            values(0, 0, 0)
            step(0, 0, 1)
            with s.Fori(0, (NG - 3) // 2) as i:
                for u in (0, 1):
                    step(2 * i + 1 + u, 1 - u, 2 * i + 2 + u)
            step(NG - 2, 1, NG - 1)
            step(NG - 1, 0, None)

        def attn_p(p):
            p.wait_ge(S("embed_done"), 1)
            p.memset(wgp[:, :, :], 0.0).then_inc(S("wgp_zero"), 1)
            p.wait_ge(S("row_in"), 16 * 5)
            row = lambda x: x[:, :].unsqueeze(1).unsqueeze(1).to_broadcast([P, B, TG, D])

            def front(g, par):
                pass

            def back(g, par):
                link = chain(p, "p_aff", g, 1)
                ln_pool(p, "a", g, par)
                p.wait_ge(S("az_ready"), g + 1)
                if late(g, 1):
                    p.wait_ge(S("gram_mm"), g)
                z3 = zs1[:, par].rearrange("p (t b d) -> p b t d", b=B, t=TG)
                link(p.tensor_tensor(z3, four(zz[:, par]), row(gam), ALU.mult))
                p.tensor_tensor(z3, z3, row(bet), ALU.add).then_inc(S("z1_ready"), 1)

            walk(p, front, back)
            p.wait_ge(S("acen_ready"), NG)
            for b in range(B):
                ins = p.tensor_tensor(hid[:, b], hid[:, b], bo_row[:, :].unsqueeze(1).to_broadcast([P, NT, D]), ALU.add)
            ins.then_inc(S("bo_added"), 1)

        def split_p(p, ph, g, par, residual):
            ln_pool(p, ph, g, par)
            p.wait_ge(S(ph + "zh_ready"), g + 1)
            if residual:
                z = four(zz[:, par])
                p.tensor_tensor(grp(g), grp(g), z, ALU.add).then_inc(S(ph + "hz_added"), 1)
            p.tensor_tensor(zst[:, par, :, 1, :], zz[:, par].rearrange("p (j d) -> p j d", d=D), zst[:, par, :, 0, :].bitcast(F32), ALU.subtract).then_inc(S(ph + "zl_ready"), 1)

        def moe_p(p, ph, CH):
            def sums(g, par, q, slot):
                link = chain(p, ph + "tree", SETS * g + q, 1)
                p.wait_ge(S(ph + "y_used"), GT * g + 4 * q + 4)
                if late(g, 1) or q:
                    p.wait_ge(S(ph + "sum_done"), SETS * g + q)
                p.tensor_tensor(tree[:, :, :], prod[:, slot, :, 0:256], prod[:, slot, :, 256:512], ALU.add).then_inc(S(ph + "prod_used"), 1)
                p.wait_ge(S(ph + "prod_used"), SETS * g + q + 1)
                link(p.tensor_tensor(tree2[:, :, :], tree[:, :, 0:128], tree[:, :, 128:256], ALU.add))
                p.tensor_tensor(ysum[:, par].rearrange("p (j d) -> p j d", d=D)[:, 4 * q:4 * q + 4, :], tree2[:, :, 0:64], tree2[:, :, 64:128],
                                ALU.add).then_inc(S(ph + "sum_done"), 1)
                if q == SETS - 1:
                    p.wait_ge(S(ph + "sum_done"), SETS * g + SETS)
                    p.tensor_tensor(grp(g), grp(g), four(ysum[:, par]), ALU.add).then_inc(S(ph + "h_added"), 1)

            def step(g, par, ahead):
                if late(g, 1):
                    sums(g - 1, 1 - par, SETS - 1, (par + 1) % 2)
                if ahead is not None:
                    split_p(p, ph, ahead, 1 - par, ph == "m")
                sums(g, par, 0, par)
                sums(g, par, 1, 1 - par)

            split_p(p, ph, 0, 0, ph == "m")
            step(0, 0, 1)
            with p.Fori(0, (NG - 3) // 2) as i:
                for u in (0, 1):
                    step(2 * i + 1 + u, 1 - u, 2 * i + 2 + u)
            step(NG - 2, 1, NG - 1)
            step(NG - 1, 0, None)
            sums(NG - 1, 0, SETS - 1, 0)

        def ret_p(p):
            def rope(g, t, sl):
                k = TG * g + t
                p.wait_ge(S("rope_read"), k + 1)
                if late(g, 1) or t >= 2:
                    p.wait_ge(S("ret_mm"), k - 1)
                p.tensor_tensor(rot[:, sl, :, :, :], rA[:, :, :, :], rB[:, :, :, :], ALU.add).then_inc(S("rot_ready"), 1)
                if t == TG - 1:
                    p.wait_ge(S("rot_ready"), k + 1)
                    p.sem_inc(S("tab_used"), 1)

            def step(g, par, ahead):
                for t in range(TG):
                    sl = (par + t) % 2
                    if ahead is not None and t == 0:
                        split_p(p, "r", ahead, 1 - par, False)
                    if t < TG - 1:
                        rope(g, t + 1, 1 - sl)
                    elif ahead is not None:
                        rope(ahead, 0, 1 - sl)

            split_p(p, "r", 0, 0, False)
            rope(0, 0, 0)
            step(0, 0, 1)
            with p.Fori(0, (NG - 3) // 2) as i:
                for u in (0, 1):
                    step(2 * i + 1 + u, 1 - u, 2 * i + 2 + u)
            step(NG - 2, 1, NG - 1)
            step(NG - 1, 0, None)


        @block.sync
        def _(sp):
            def rows_load(b):
                for i in range(3):
                    for c2 in range(2):
                        sp.dma_start(rows[64 * c2:64 * c2 + 64, b % 2, i], A["x_rows"][b, c2, i:i + HH]).then_inc(S("rows_in%d" % (b % 2)), 16)

            sp.dma_start(xch[0:64, :], A["x"][0].rearrange("c h w -> c (h w)")).then_inc(S("xch_in0"), 16)
            for h in range(2):
                sp.dma_start(w1c[64 * h:64 * h + 64, :], A["conv1_wT"]).then_inc(S("embw_in"), 16)
            sp.dma_start(w2c[0:16, :], A["conv2_wT"]).then_inc(S("embw_in"), 16)
            sp.dma_start(w2c[16:17, :], A["L0_tok_conv2_b"].unsqueeze(0)).then_inc(S("embw_in"), 16)
            for n, k in enumerate(("conv1_b", "bn_gamma", "bn_beta", "bn_mean", "bn_var")):
                sp.dma_start(bnv[:, n:n + 1], A["L0_tok_" + k].unsqueeze(1)).then_inc(S("embw_in"), 16)
            sp.dma_start(xch[64:128, :], A["x"][1].rearrange("c h w -> c (h w)")).then_inc(S("xch_in1"), 16)
            rows_load(0)
            rows_load(1)
            for dst, src in ((gam, "L0_attn_gamma"), (bet, "L0_attn_beta"), (bo_row, "L0_attn_bo"), (lgb, "L1_ffn_bg"), (lgb2, "L1_ffn_bias")):
                sp.dma_start(dst[:, :], A[src].partition_broadcast(P)).then_inc(S("row_in"), 16)
            sp.dma_start(ids[:, :], A["x_txt"].rearrange("b (s o) -> (b s) o", o=1)).then_inc(S("ids_in"), 16)
            for b in range(B):
                sp.dma_start(tx["u"][TXT * b:TXT * b + TXT, :], A["L0_txt_U_w"][0:TXT, :]).then_inc(S("txt_in"), 16)
            for dst, src in (("g", "L0_txt_ln_g"), ("b", "L0_txt_ln_b"), ("ob", "L0_txt_b")):
                sp.dma_start(tx[dst][:, :], A[src].partition_broadcast(P)).then_inc(S("txt_in"), 16)
            sp.dma_start(tx["wT"][:, :], A["txt_WT"]).then_inc(S("txt_in"), 16)
            for b in (2, 3):
                sp.wait_ge(S("conv_ready"), 8 * (b - 1))
                sp.dma_start(xch[64 * (b % 2):64 * (b % 2) + 64, :], A["x"][b].rearrange("c h w -> c (h w)")).then_inc(S("xch_in%d" % (b % 2)), 16)
                sp.wait_ge(S("rows_used_v"), b - 1)
                sp.wait_ge(S("rows_used_p"), b - 1)
                rows_load(b)
            sp.wait_ge(S("txt_done"), 1)
            for b in range(B):
                sp.dma_start(hid[0:TXT, b, NT - 1, :], tx["o"][TXT * b:TXT * b + TXT, :]).then_inc(S("txt_put"), 16)
            sp.wait_ge(S("txt_put"), 16 * B)
            sp.wait_ge(S("embed_done"), 1)
            for h in range(2):
                for dst, src in ((wk2, "Wk"), (wq2, "Wq"), (wv2, "Wv")):
                    sp.dma_start(dst[64 * h:64 * h + 64, :], A["L0_attn_" + src]).then_inc(S("attw_in"), 16)
            sp.wait_ge(S("wgp_zero"), 1)
            for h in range(2):
                sp.dma_start(wgp[64 * h:64 * h + 64, h, :], A["L0_attn_Wg"]).then_inc(S("attw_in"), 16)
            sp.dma_start(wo[:, :, :], A["L0_attn_Wo"].rearrange("(m k) d -> k m d", m=2)).then_inc(S("attw_in"), 16)
            sp.dma_start(bgc[:, :], A["bgT"]).then_inc(S("attw_in"), 16)
            sp.wait_ge(S("attn_free"), 1)
            n = S("deepw_in")
            for h in range(2):
                r = slice(64 * h, 64 * h + 64)
                sp.dma_start(wr[r, 0, :], A["router_wT"]).then_inc(n, 16)
                sp.dma_start(wr[r, 1, :], A["L1_ffn_Wg"]).then_inc(n, 16)
                sp.dma_start(fw1[r, :].rearrange("p (e f) -> p e f", e=E), A["L0_ffn_w1"].rearrange("e d f -> d e f")).then_inc(n, 16)
                sp.dma_start(gw1[r, :].rearrange("p (e f) -> p e f", e=E), A["L1_ffn_W1"].rearrange("e d f -> d e f")).then_inc(n, 16)
                sp.dma_start(wqk[r, :], A["w_qk"]).then_inc(n, 16)
                sp.dma_start(bias2[32 * h:32 * h + 1, 0, :], A["L0_ffn_b2"].rearrange("(o e) d -> o (e d)", o=1)).then_inc(n, 16)
                sp.dma_start(bias2[32 * h:32 * h + 1, 1, :], A["L1_ffn_b2"].rearrange("(o e) d -> o (e d)", o=1)).then_inc(n, 16)
            sp.dma_start(fb1[:, :], A["ffn0_b1T"]).then_inc(n, 16)
            sp.dma_start(gb1[:, :], A["ffn1_b1T"]).then_inc(n, 16)
            sp.dma_start(gw2[:, :, :], A["L1_ffn_W2"].rearrange("e f d -> f e d")).then_inc(n, 16)
            sp.wait_ge(S("fw2_zero"), 1)
            for e in range(E):
                h = e % 2
                sp.dma_start(fw2[64 * h:64 * h + 64, e // 2, 64 * h:64 * h + 64], A["L0_ffn_w2"][e]).then_inc(n, 16)
            def tab_load(g, par):
                if late(g, 2):
                    sp.wait_ge(S("tab_used"), g - 1)
                sp.dma_start(tabc[:, par], A["tables"][g if isinstance(g, int) else bass.ds(g, 1)] if isinstance(g, int)
                             else A["tables"][bass.ds(g, 1)].rearrange("o p t c -> (o p) t c")).then_inc(S("tab_in%d" % par), 16)
            tab_load(0, 0)
            tab_load(1, 1)
            with sp.Fori(0, (NG - 3) // 2) as i:
                for u in (0, 1):
                    tab_load(2 * i + 2 + u, u)
            tab_load(NG - 1, 0)
            sp.wait_ge(S("stage_done"), 1)
            for b in range(B):
                sp.dma_start(out[b, 0:(NT - 1) * P, :].rearrange("(t p) d -> p t d", p=P), hid[:, b, 0:NT - 1, :]).then_inc(S("out_done"), 16)
                sp.dma_start(out[b, (NT - 1) * P:L, :], hid[0:TXT, b, NT - 1, :]).then_inc(S("out_done"), 16)
            sp.wait_ge(S("out_done"), 16 * 2 * B)

        @block.tensor
        def _(pe):
            ACC, CONV, WD, TXB = 0, 4, 6, 7
            pe.wait_ge(S("embw_in"), 16 * 9)
            pe.wait_ge(const_ready, 1)

            def conv(b, u):
                pe.wait_ge(S("xch_in%d" % u), 16 * (b // 2 + 1))
                for n in range(8):
                    k = 8 * b + n
                    if k >= 2:
                        pe.wait_ge(S("y_ready"), k - 1)
                    mm = pe.matmul(ps[0:16, CONV + n % 2, :], w1c[64 * u:64 * u + 64, :], xch[64 * u:64 * u + 64, 512 * n:512 * n + 512],
                                   start=True, stop=True).then_inc(S("conv_ready"), 1)
                pe.wait_ge(S("y_ready"), 8 * b + 8)
                yv = yact[0:17, :].rearrange("k (h w) -> k w h", w=WW)
                for half in range(2):
                    if 2 * b + half >= 1:
                        pe.wait_ge(S("wd_ready"), 2 * b + half)
                    for w in range(32):
                        for c2 in range(2):
                            mm = pe.matmul(ps[64 * c2:64 * c2 + 64, WD, 9 * w:9 * w + 9], yv[:, 32 * half + w, :], w2c[0:17, :],
                                           start=True, stop=True, skip_group_check=True)
                    mm.then_inc(S("wd_mm"), 1)

            def add_terms(b):
                if b >= 1:
                    pe.wait_ge(S("embed_out"), b)
                for n, (buf, s) in enumerate(((dA, "termA"), (pD, "termD"), (dB, "termB"), (pE, "termE"), (dC, "termC"))):
                    pe.wait_ge(S(s), b + 1)
                    for q in range(4):
                        mm = pe.matmul(ps[:, ACC + q, :], ident[:, :], buf[:, 8 * q:8 * q + 8, :], start=(n == 0), stop=(n == 4))
                    mm.then_inc(S("term_used"), 1)

            conv(0, 0)
            for b in range(B):
                if b + 1 < B:
                    conv(b + 1, (b + 1) % 2)
                add_terms(b)

            t = ps[:, TXB, :]
            pe.wait_ge(S("tx_v"), 1)
            pe.transpose(t[0:D, 0:P], tx["a"][:, :], ident[:, :]).then_inc(S("tx_pe"), 1)
            for r in range(3):
                pe.wait_ge(S("tx_v"), 2 + 4 * r)
                pe.transpose(t[0:D, 128:256], tx["u"][:, :], ident[:, :]).then_inc(S("tx_pe"), 1)
                pe.wait_ge(S("tx_v"), 3 + 4 * r)
                for b in range(B):
                    mm = pe.matmul(t[TXT * b:TXT * b + TXT, 256:256 + TXT], tx["aT"][:, TXT * b:TXT * b + TXT], tx["uT"][:, TXT * b:TXT * b + TXT],
                                   start=True, stop=True, skip_group_check=True)
                mm.then_inc(S("tx_pe"), 1)
                pe.wait_ge(S("tx_v"), 5 + 4 * r)
                for b in range(B):
                    s = slice(TXT * b, TXT * b + TXT)
                    mm = pe.matmul(t[s, 320:384], tx["p"][s, :], tx["c"][s, :], start=True, stop=True, skip_group_check=True)
                mm.then_inc(S("tx_pe"), 1)
            pe.wait_ge(S("tx_v"), 15)
            pe.transpose(t[0:D, 0:P], tx["z"][:, :], ident[:, :]).then_inc(S("tx_pe"), 1)
            pe.wait_ge(S("tx_v"), 16)
            pe.matmul(t[:, 128:192], tx["zT"][:, :], tx["wT"][:, :], start=True, stop=True).then_inc(S("tx_pe"), 1)

            gram_pe(pe)
            moe_pe(pe, "m", 4)
            ret_pe(pe)
            moe_pe(pe, "x", 8)

        @block.vector
        def _(v):
            def once(name):
                return chain(v, name, 0, 0)

            link = once("v_pre")
            v.memset(ones[:, :], 1.0).then_inc(S("v_set"), 1)
            v.memset(nhalf[:, :], -0.5).then_inc(S("v_set"), 1)
            v.memset(yact[:, :], 1.0).then_inc(S("v_set"), 1)
            link(v.memset(hid[:, :, NT - 1, :], 0.0))
            v.wait_ge(S("embw_in"), 16 * 9)
            link(v.tensor_scalar(bnv[:, 5:6], bnv[:, 4:5], EPS, None, ALU.add))
            v.wait_ge(S("v_set"), 3)
            v.tensor_copy(bnv[:, 9:10], nhalf[0:16, 0:1]).then_inc(S("bn_var"), 1)
            v.wait_ge(S("bn_rs"), 1)
            link(v.tensor_tensor(bnv[:, 7:8], bnv[:, 6:7], bnv[:, 1:2], ALU.mult))
            link(v.tensor_tensor(bnv[:, 8:9], bnv[:, 0:1], bnv[:, 3:4], ALU.subtract))
            link(v.tensor_tensor(bnv[:, 8:9], bnv[:, 8:9], bnv[:, 7:8], ALU.mult))
            v.tensor_tensor(bnv[:, 8:9], bnv[:, 8:9], bnv[:, 2:3], ALU.add).then_inc(S("bn_ready"), 1)
            v.wait_ge(S("ids_in"), 16)
            v.tensor_scalar(idc[:, 0:1], ids[:, :], 0, A["L0_txt_A_w"].shape[0] - 1, ALU.max, ALU.min).then_inc(S("idc_ready"), 1)

            link = once("v_emb")

            def tap(buf, u, i, j):
                return v.tensor_tensor(buf[:, :, :], rows[:, u, i, :, j:j + WW], wdyn[:, u, 3 * i + j, :].unsqueeze(1).to_broadcast([P, CP, WW]), ALU.mult)

            for b in range(B):
                u = b % 2
                v.wait_ge(S("rows_in%d" % u), 16 * 6 * (b // 2 + 1))
                v.wait_ge(S("wd_ready"), 2 * b + 2)
                if b:
                    v.wait_ge(S("term_used"), 5 * b)
                link(tap(dA, u, 1, 0))
                link(tap(dT, u, 1, 1))
                v.tensor_tensor(dA[:, :, :], dA[:, :, :], dT[:, :, :], ALU.add).then_inc(S("termA"), 1)
                tap(dB, u, 1, 2).then_inc(S("termB"), 1)
                link(tap(dC, u, 2, 0))
                v.wait_ge(S("termA"), b + 1)
                link(tap(dT, u, 2, 1))
                link(v.tensor_tensor(dC[:, :, :], dC[:, :, :], dT[:, :, :], ALU.add))
                link(tap(dT, u, 2, 2))
                v.tensor_tensor(dC[:, :, :], dC[:, :, :], dT[:, :, :], ALU.add).then_inc(S("termC"), 1)
                v.wait_ge(S("termC"), b + 1)
                v.wait_ge(S("termB"), b + 1)
                v.sem_inc(S("rows_used_v"), 1)

            link = once("v_txt")
            T = ps[:, 7, :]
            v.wait_ge(S("txt_in"), 16 * 8)
            v.wait_ge(S("gath_in"), 32)
            link(v.tensor_copy(tx["o"][:, :], tx["u"][:, :]))
            v.tensor_copy(tx["q"][:, :], tx["o"][:, :]).then_inc(S("tx_v"), 1)
            v.wait_ge(S("tx_pe"), 1)
            v.tensor_copy(tx["aT"][:, :], T[0:D, 0:P]).then_inc(S("tx_v"), 1)
            for r in range(3):
                v.wait_ge(S("tx_pe"), 2 + 3 * r)
                v.tensor_copy(tx["uT"][:, :], T[0:D, 128:256]).then_inc(S("tx_v"), 1)
                v.wait_ge(S("tx_pe"), 3 + 3 * r)
                sc = T[:, 256:256 + TXT]
                link(v.tensor_reduce(tx["m"][:, 0:1], sc, X, ALU.max))
                v.tensor_scalar(tx["s"][:, :], sc, tx["m"][:, 0:1], None, ALU.subtract).then_inc(S("tx_v"), 1)
                v.wait_ge(S("tx_e"), r + 1)
                link(v.reciprocal(tx["m"][:, 2:3], tx["m"][:, 1:2]))
                v.tensor_scalar(tx["p"][:, :], tx["s"][:, :], tx["m"][:, 2:3], None, ALU.mult).then_inc(S("tx_v"), 1)
                v.wait_ge(S("tx_pe"), 4 + 3 * r)
                if r < 2:
                    v.tensor_tensor(tx["u"][:, :], tx["u"][:, :], T[:, 320:384], ALU.add).then_inc(S("tx_v"), 1)
                else:
                    link(v.tensor_tensor(tx["u"][:, :], tx["u"][:, :], T[:, 320:384], ALU.add))
            link(v.tensor_reduce(tx["m"][:, 3:4], tx["u"][:, :], X, ALU.add))
            link(v.tensor_scalar(tx["m"][:, 3:4], tx["m"][:, 3:4], 1.0 / D, None, ALU.mult))
            link(v.tensor_scalar(tx["u"][:, :], tx["u"][:, :], tx["m"][:, 3:4], None, ALU.subtract))
            link(v.tensor_tensor(tx["q"][:, :], tx["u"][:, :], tx["u"][:, :], ALU.mult))
            link(v.tensor_reduce(tx["m"][:, 4:5], tx["q"][:, :], X, ALU.add))
            v.tensor_scalar(tx["m"][:, 4:5], tx["m"][:, 4:5], 1.0 / D, EPS, ALU.mult, ALU.add).then_inc(S("tx_v"), 1)
            v.wait_ge(S("tx_rs"), 1)
            link(v.tensor_scalar(tx["z"][:, :], tx["u"][:, :], tx["m"][:, 5:6], None, ALU.mult))
            link(v.tensor_tensor(tx["z"][:, :], tx["z"][:, :], tx["g"][:, :], ALU.mult))
            v.tensor_tensor(tx["z"][:, :], tx["z"][:, :], tx["b"][:, :], ALU.add).then_inc(S("tx_v"), 1)
            v.wait_ge(S("tx_pe"), 11)
            v.tensor_copy(tx["zT"][:, :], T[0:D, 0:P]).then_inc(S("tx_v"), 1)
            v.wait_ge(S("tx_pe"), 12)
            v.tensor_tensor(tx["o"][:, :], T[:, 128:192], tx["ob"][:, :], ALU.add).then_inc(S("txt_done"), 1)
            v.wait_ge(S("embed_out"), B)
            v.wait_ge(S("txt_put"), 16 * B)
            v.sem_inc(S("embed_done"), 1)
            attn_v(v)
            deep_prep_v(v)
            moe_v(v, "m", 4)
            ret_v(v)
            moe_v(v, "x", 8)

        @block.scalar
        def _(s):
            s.wait_ge(S("v_set"), 3)
            s.wait_ge(S("bn_ready"), 1)

            def conv(b):
                for n in range(8):
                    s.wait_ge(S("conv_ready"), 8 * b + n + 1)
                    if b and n == 0:
                        s.wait_ge(S("wd_mm"), 2 * b)
                    s.activation(yact[0:16, 512 * n:512 * n + 512], ps[0:16, 4 + n % 2, :], ACT.Relu, bias=bnv[:, 8:9], scale=bnv[:, 7:8]).then_inc(S("y_ready"), 1)
                if b >= 2:
                    s.wait_ge(S("rows_used_v"), b - 1)
                    s.wait_ge(S("rows_used_p"), b - 1)
                for half in range(2):
                    s.wait_ge(S("wd_mm"), 2 * b + half + 1)
                    s.activation(wdyn[:, b % 2, :, 32 * half:32 * half + 32], ps[:, 6, 0:288].rearrange("p (w k) -> p k w", k=9), ACT.Copy).then_inc(S("wd_ready"), 1)

            def store(b):
                s.wait_ge(S("term_used"), 5 * b + 5)
                s.activation(hid[:, b, 0:NT - 1, :], ps[:, 0:4, :].rearrange("p a (c w) -> p (a c) w", w=WW), ACT.Copy).then_inc(S("embed_out"), 1)

            conv(0)
            for b in range(B):
                if b + 1 < B:
                    conv(b + 1)
                store(b)
            for r in range(3):
                s.wait_ge(S("tx_v"), 4 + 4 * r)
                s.activation(tx["s"][:, :], tx["s"][:, :], ACT.Exp, accum_out=tx["m"][:, 1:2]).then_inc(S("tx_e"), 1)
            attn_s(s)
            moe_s(s, "m", 4)
            ret_s(s)
            moe_s(s, "x", 8)

        @block.gpsimd
        def _(p):
            p.memset(ident[:, :], 0.0).then_inc(S("p_set"), 1)
            p.memset(causal[:, :], 1.0).then_inc(S("p_set"), 1)
            p.wait_ge(S("p_set"), 2)
            p.affine_select(out=ident[:, :], in_=ident[:, :], compare_op=ALU.not_equal, fill=1.0, base=0, pattern=[[-1, P]],
                            channel_multiplier=1).then_inc(S("p_set"), 1)
            p.affine_select(out=causal[:, :], in_=causal[:, :], compare_op=ALU.is_ge, fill=0.0, base=0, pattern=[[1, P]],
                            channel_multiplier=-1).then_inc(S("p_set"), 1)
            p.wait_ge(S("p_set"), 4)
            p.sem_inc(const_ready, 1)
            p.wait_ge(S("bn_var"), 1)
            p.tensor_tensor(bnv[:, 6:7], bnv[:, 5:6], bnv[:, 9:10], ALU.pow).then_inc(S("bn_rs"), 1)
            p.wait_ge(S("idc_ready"), 1)
            for n, k in (("a", "A"), ("c", "C")):
                p.indirect_dma_start(out=tx[n][:, :], out_offset=None, in_=A["L0_txt_%s_w" % k],
                                     in_offset=bass.IndirectOffsetOnAxis(ap=idc[:, 0:1], axis=0)).then_inc(S("gath_in"), 16)
            link = chain(p, "p_emb", 0, 0)

            def tap(buf, u, i, j):
                return p.tensor_tensor(buf[:, :, :], rows[:, u, i, :, j:j + WW], wdyn[:, u, 3 * i + j, :].unsqueeze(1).to_broadcast([P, CP, WW]), ALU.mult)

            for b in range(B):
                u = b % 2
                p.wait_ge(S("rows_in%d" % u), 16 * 6 * (b // 2 + 1))
                p.wait_ge(S("wd_ready"), 2 * b + 2)
                if b:
                    p.wait_ge(S("term_used"), 5 * b)
                link(tap(pD, u, 0, 0))
                link(tap(pT, u, 0, 1))
                p.tensor_tensor(pD[:, :, :], pD[:, :, :], pT[:, :, :], ALU.add).then_inc(S("termD"), 1)
                tap(pE, u, 0, 2).then_inc(S("termE"), 1)
                p.wait_ge(S("termD"), b + 1)
                p.wait_ge(S("termE"), b + 1)
                p.sem_inc(S("rows_used_p"), 1)
            p.wait_ge(S("tx_v"), 14)
            p.tensor_tensor(tx["m"][:, 5:6], tx["m"][:, 4:5], nhalf[:, 0:1], ALU.pow).then_inc(S("tx_rs"), 1)
            attn_p(p)
            moe_p(p, "m", 4)
            ret_p(p)
            moe_p(p, "x", 8)
            p.wait_ge(S("xh_added"), NG)
            p.sem_inc(S("stage_done"), 1)

def rotary_tables():
    f = np.float32
    j = np.arange(0, D, 2, dtype=f)
    inv = (f(1.0) / f(10000.0) ** (j / f(D))).astype(f)
    pos = np.arange(NT * P, dtype=f)
    ang = (pos[:, None] * inv[None, :]).astype(f)
    s, c = np.sin(ang), np.cos(ang)
    base = ((j + f(0.4 * D)) / f(1.4 * D)).astype(f)
    scale = (base[None, :] ** (pos[:, None] / f(512.0))).astype(f)
    local = (np.arange(NT * P) % P)[:, None]
    dq, dk = GAMMA ** local, GAMMA ** (-local.astype(np.float64))
    out = np.zeros((NT * P, 2, 2 * D), f)
    for n, (w, m) in enumerate(((scale, dq), (1.0 / scale, dk))):
        cw, sw = (c * w * m).astype(f), (s * w * m).astype(f)
        out[:, 0, D * n:D * n + D] = np.concatenate([cw, cw], 1)
        out[:, 1, D * n:D * n + D] = np.concatenate([-sw, sw], 1)
    t = out.reshape(NG, TG, P, 2, 2 * D).transpose(0, 2, 1, 3, 4)
    return np.ascontiguousarray(t.reshape(NG, P, 2 * TG, 2 * D))


_INS = ['x', 'x_txt', 'L0_tok_conv1_w', 'L0_tok_conv1_b', 'L0_tok_bn_gamma', 'L0_tok_bn_beta', 'L0_tok_bn_mean', 'L0_tok_bn_var',
        'L0_tok_conv2_w', 'L0_tok_conv2_b', 'L0_txt_A_w', 'L0_txt_C_w', 'L0_txt_U_w', 'L0_txt_ln_g', 'L0_txt_ln_b', 'L0_txt_W', 'L0_txt_b',
        'L0_attn_gamma', 'L0_attn_beta', 'L0_attn_Wq', 'L0_attn_Wk', 'L0_attn_Wv', 'L0_attn_Wg', 'L0_attn_bg', 'L0_attn_Wo', 'L0_attn_bo',
        'L0_ffn_router_w', 'L0_ffn_w1', 'L0_ffn_b1', 'L0_ffn_w2', 'L0_ffn_b2', 'L1_ffn_Wg', 'L1_ffn_bg', 'L1_ffn_bias', 'L1_ffn_W1',
        'L1_ffn_b1', 'L1_ffn_W2', 'L1_ffn_b2']


def kernel(**inputs):
    import numpy as _np
    import concourse.bacc as _bacc
    from concourse import mybir as _mybir
    from concourse.bass_utils import run_bass_kernel_spmd as _run

    nc = _bacc.Bacc("TRN2", target_bir_lowering=False, num_devices=1)
    data = {k: _np.ascontiguousarray(inputs[k]) for k in _INS}
    x = data["x"].reshape(B, CP, 2, HH, WW)
    xr = _np.zeros((B, 2, HH + 2, CP, WW + 2), x.dtype)
    xr[:, :, 1:-1, :, 1:-1] = x.transpose(0, 2, 3, 1, 4)
    data["x_rows"] = xr
    wq, wk, wv = (_np.asarray(inputs["L1_attn_W_" + n]) for n in "QKV")
    ev, od = _np.arange(0, D, 2), _np.arange(1, D, 2)
    eo, oe = _np.concatenate([ev, od]), _np.concatenate([od, ev])
    data["w_qk"] = _np.ascontiguousarray(_np.concatenate([wq[:, eo], wk[:, eo], wq[:, oe], wk[:, oe], wv], 1))
    data["tables"] = rotary_tables()
    for name, v in (("conv1_wT", data["L0_tok_conv1_w"].T), ("conv2_wT", data["L0_tok_conv2_w"].T), ("txt_WT", data["L0_txt_W"].T),
                    ("router_wT", data["L0_ffn_router_w"].T), ("ffn0_b1T", data["L0_ffn_b1"].reshape(E // 2, P).T),
                    ("ffn1_b1T", data["L1_ffn_b1"].T), ("bgT", data["L0_attn_bg"].reshape(2, P).T)):
        data[name] = _np.ascontiguousarray(v)
    arrays, args = {}, {}
    for name, v in data.items():
        arrays[f"in_{name}_dram"] = v
        args[name] = nc.dram_tensor(f"in_{name}_dram", v.shape, _mybir.dt.from_np(v.dtype), kind="ExternalInput").ap()
    res = nc.dram_tensor("out_0_dram", (B, L, D), F32, kind="ExternalOutput").ap()
    build(nc, args, res)
    r = _run(nc, [arrays], core_ids=[0])
    return r.results[0]["out_0_dram"]
```

```python
from contextlib import ExitStack
import numpy as np
import concourse.bass as bass
from concourse import mybir

F32 = mybir.dt.float32
F32R = mybir.dt.float32r
I32 = mybir.dt.int32
U32 = mybir.dt.uint32
ALU = mybir.AluOpType
ACT = mybir.ActivationFunctionType
X = mybir.AxisListType.X

P = 128
B, C, HH, WW = 4, 64, 64, 64
D = 64
TXT = 32
L = C * HH + TXT
NT = (L + P - 1) // P
TG = 3
NG = NT // TG
GT = TG * B
GW = GT * D
SETS = 3
EPS = 1e-5
HEADS, HC = 8, 32
E = 8
GAMMA = 0.96875
CP = C // 2


def steps(eng, step):
    step(0, 0, 1, 2)
    with eng.Fori(0, (NG - 3) // 2) as i:
        for u in (0, 1):
            step(2 * i + 1 + u, 1 - u, 2 * i + 2 + u, 2 * i + 3 + u)
    step(NG - 2, 1, NG - 1, None)
    step(NG - 1, 0, None, None)


def late(g, n):
    return not isinstance(g, int) or g >= n


def build(nc, a, out):
    with ExitStack() as ctx:
        top = ctx

        def sb(name, shape, dt=F32, where=None):
            return (where or ctx).enter_context(nc.sbuf_tensor(name, shape, dt))

        def sem(name):
            return ctx.enter_context(nc.semaphore(name))

        hid = sb("hid", [P, B, NT, D])
        ident = sb("ident", [P, P])
        ones = sb("ones", [P, P])
        causal = sb("causal", [P, P])
        desc = sb("desc", [P, E])
        nhalf = sb("nhalf", [P, GT])
        gam = sb("gam", [P, D])
        bet = sb("bet", [P, D])
        bo_row = sb("bo_row", [P, D])
        lgb = sb("lgb", [P, E])
        lgb2 = sb("lgb2", [P, E])
        ln_sum = sb("ln_sum", [P, 2, GT])
        ln_mean = sb("ln_mean", [P, 2, GT])
        ln_var = sb("ln_var", [P, 2, GT])
        ln_ve = sb("ln_ve", [P, 2, GT])
        ln_rs = sb("ln_rs", [P, 2, GT])
        cen = sb("cen", [P, 2, GW])
        sq = sb("sq", [P, 2, GW])
        zz = sb("zz", [P, 2, GW])

        sems = {}

        def S(name):
            if name not in sems:
                sems[name] = sem(name)
            return sems[name]

        const_ready = S("const_ready")

        def grp(g):
            return hid[:, :, bass.ds(g * TG, TG) if not isinstance(g, int) else slice(g * TG, g * TG + TG), :]

        def four(x):
            return x.rearrange("p (b t d) -> p b t d", b=B, t=TG)

        def three(x):
            return x.rearrange("p (b t) -> p b t", b=B)

        def bc(x, n):
            return x.unsqueeze(3).to_broadcast([P, B, TG, n])

        embed = ExitStack()
        XW = WW + 2
        with embed:
            rows = sb("rows", [P, 2, 3, CP, XW], F32, embed)
            xch = sb("xch", [P, HH * WW], F32, embed)
            yact = sb("yact", [32, HH * WW], F32, embed)
            wdyn = sb("wdyn", [P, 2, 9, WW], F32, embed)
            dA, dB, dC, dT, pD, pE, pT = [sb(n, [P, CP, WW], F32, embed) for n in ("dA", "dB", "dC", "dT", "pD", "pE", "pT")]
            w1c = sb("w1c", [P, 16], F32, embed)
            w2c = sb("w2c", [17, 9], F32, embed)
            bnv = sb("bnv", [16, 10], F32, embed)
            tx = {n: sb("tx_" + n, s, F32, embed) for n, s in dict(
                a=[P, D], c=[P, D], u=[P, D], uT=[D, P], aT=[D, P], s=[P, TXT], p=[P, TXT], m=[P, 8],
                g=[P, D], b=[P, D], wT=[D, D], ob=[P, D], z=[P, D], zT=[D, P], o=[P, D], q=[P, D]).items()}
            ids = sb("tx_ids", [P, 1], I32, embed)
            idc = sb("tx_idc", [P, 2], U32, embed)
        attn = ExitStack()
        with attn:
            zs1 = sb("zs1", [P, 2, GW], F32, attn)
            ztH = sb("ztH", [P, 2, NT * P], F32R, attn)
            ztL = sb("ztL", [P, 2, NT * P], F32R, attn)
            wk2 = sb("wk2", [P, 256], F32, attn)
            wq2 = sb("wq2", [P, 256], F32, attn)
            wv2 = sb("wv2", [P, 256], F32, attn)
            wgp = sb("wgp", [P, 2, 256], F32, attn)
            wgH = sb("wgH", [P, 2, 256], F32R, attn)
            wgL = sb("wgL", [P, 2, 256], F32R, attn)
            wo = sb("wo", [P, 2, D], F32, attn)
            bgc = sb("bgc", [P, 2], F32, attn)
            gramS = sb("gramS", [P, 2, 256], F32, attn)
            prodX = sb("prodX", [P, 8, 256], F32, attn)
            part = sb("part", [P, 64], F32, attn)
            at = sb("at", [P, P], F32, attn)
            at2 = sb("at2", [P, P], F32, attn)
            atm = sb("atm", [P, 4 * HEADS], F32, attn)
            wmix = sb("wmix", [P, B, 2, 256], F32, attn)
            wmH = sb("wmH", [P, B, 2, 256], F32R, attn)
            wmL = sb("wmL", [P, B, 2, 256], F32R, attn)
            sig = sb("sig", [P, 2, TG * P], F32, attn)
            og = sb("og", [P, 2, 2, TG * P], F32, attn)
        deep = ExitStack()
        with deep:
            zst = sb("zst", [P, 2, GT, 2, D], F32R, deep)
            zt = sb("zt", [P, 2, GT * P], F32R, deep)
            lg = sb("lg", [P, 12, GT * E], F32, deep)
            rt = sb("rt", [P, 8, GT], F32, deep)
            comb = sb("comb", [P, 2, GT * E], F32, deep)
            wr = sb("wr", [P, 2, E], F32, deep)
            wrH = sb("wrH", [P, 2, E], F32R, deep)
            wrL = sb("wrL", [P, 2, E], F32R, deep)
            fw1 = sb("fw1", [P, E * D], F32, deep)
            fw1H = sb("fw1H", [P, E * D], F32R, deep)
            fw1L = sb("fw1L", [P, E * D], F32R, deep)
            fb1 = sb("fb1", [P, 4], F32, deep)
            fw2 = sb("fw2", [P, 4, P], F32, deep)
            gw1 = sb("gw1", [P, E * P], F32, deep)
            gw1H = sb("gw1H", [P, E * P], F32R, deep)
            gw1L = sb("gw1L", [P, E * P], F32R, deep)
            gb1 = sb("gb1", [P, E], F32, deep)
            gw2 = sb("gw2", [P, E, D], F32, deep)
            bias2 = sb("bias2", [D, 2, E * D], F32, deep)
            b2sp = sb("b2sp", [D, 2, E * D], F32R, deep)
            onesR = sb("onesR", [D, P], F32R, deep)
            NQ = 5 * D
            wqk = sb("wqk", [P, NQ], F32, deep)
            wqkH = sb("wqkH", [P, NQ], F32R, deep)
            wqkL = sb("wqkL", [P, NQ], F32R, deep)
            tabc = sb("tabc", [P, 2, 2 * TG, 2 * D], F32, deep)
            experts = ExitStack()
            with experts:
                hact = sb("hact", [P, 2, E, 512], F32, experts)
                prod = sb("prod", [P, 2, 4, E * D], F32, experts)
                tree = sb("tree", [P, 4, 4 * D], F32, experts)
                tree2 = sb("tree2", [P, 4, 2 * D], F32, experts)
                ysum = sb("ysum", [P, 2, GW], F32, experts)
            retain = ExitStack()
            with retain:
                rA = sb("rA", [P, 2, B, D], F32, retain)
                rB = sb("rB", [P, 2, B, D], F32, retain)
                rot = sb("rot", [P, TG, 2, B, D], F32, retain)
                val = sb("val", [P, TG, B, D], F32, retain)
                qkT = sb("qkT", [P, TG, 4, P], F32, retain)
                pmat = sb("pmat", [P, TG, B, P], F32, retain)
                state = sb("state", [P, TG, B, D], F32, retain)
                stt = sb("stt", [P, 2, D], F32, retain)

        ps = ctx.enter_context(nc.psum_tensor("ps", [P, 8, 512], F32))

        block = ctx.enter_context(nc.Block())
        A = a

        def gram_pe(pe):
            pe.wait_ge(S("txt_put"), 16 * B)

            def back(g, par):
                z = zs1[:, par].rearrange("p (t b d) -> p t b d", b=B, t=TG)
                pe.wait_ge(S("z1_ready"), g + 1)
                if late(g, 1):
                    pe.wait_ge(S("zt_split"), g)
                for pair in range(2):
                    for t in range(TG):
                        mm = pe.transpose(ps[:, 2 + pair, P * t:P * t + P], z[:, t, 2 * pair:2 * pair + 2, :].rearrange("p b d -> p (b d)"), ident[:, :])
                mm.then_inc(S("z1_turned"), 1)
                for t in range(TG):
                    rows_ = TXT if isinstance(g, int) and g == NG - 1 and t == TG - 1 else P
                    for m in range(2):
                        first = isinstance(g, int) and g == 0 and t == 0
                        last = isinstance(g, int) and g == NG - 1 and t == TG - 1
                        mm = pe.matmul(ps[:, m, 0:256], z[0:rows_, t, 2 * m:2 * m + 2, :].rearrange("p b d -> p (b d)"), z[0:rows_, t, :, :],
                                       start=first, stop=last, skip_group_check=True)
                mm.then_inc(S("gram_mm"), 1)

            steps(pe, lambda g, par, ahead, far: back(g, par))
            pe.wait_ge(S("gram_out"), 1)
            pe.wait_ge(S("attw_in"), 16 * 10)
            for m in range(2):
                for t in range(B):
                    h = 64 * (t % 2)
                    mm = pe.matmul(ps[:, 4 + 2 * m + t % 2, 256 * (t // 2):256 * (t // 2) + 256], gramS[h:h + 64, t // 2, P * m:P * m + P],
                                   wk2[h:h + 64, :], start=True, stop=True, skip_group_check=True)
            mm.then_inc(S("x_ready"), 1)
            pe.wait_ge(S("part_ready"), 1)
            for s in range(B):
                h = 64 * (s % 2)
                mm = pe.matmul(ps[:, 2 + s % 2, 32 * (s // 2):32 * (s // 2) + 32], ones[h:h + 64, :], part[h:h + 64, 32 * (s // 2):32 * (s // 2) + 32],
                               start=True, stop=True, skip_group_check=True)
            mm.then_inc(S("att_ready"), 1)
            pe.wait_ge(S("wmix_ready"), 1)

            def mix(g, par):
                for s in range(B):
                    for mc in range(2):
                        k = 2 * s + mc
                        if late(g, 1) or k >= 2:
                            pe.wait_ge(S("og_ready"), 8 * g + k - 1)
                        cs = slice(P * mc, P * mc + P)
                        tok = bass.ds(g * TG * P, TG * P) if not isinstance(g, int) else slice(g * TG * P, (g + 1) * TG * P)
                        n = 0
                        for pair in range(2):
                            for w, z in ((wmH, ztH), (wmH, ztL), (wmL, ztH)):
                                pe.matmul(ps[:, mc, 0:TG * P], w[:, s, pair, cs], z[:, pair, tok], start=(n == 0), stop=(n == 5))
                                n += 1
                        for n, (w, z) in enumerate(((wgH, ztH), (wgH, ztL), (wgL, ztH))):
                            mm = pe.matmul(ps[:, 2 + mc, 0:TG * P], w[:, s % 2, cs], z[:, s // 2, tok], start=(n == 0), stop=(n == 2))
                        mm.then_inc(S("mix_ready"), 1)
                    if late(g, 1) or s >= 1:
                        project(4 * g + s - 1, (s - 1) % 2, (s - 1) % 2)

            def project(k, slot, bank):
                pe.wait_ge(S("og_ready"), 2 * k + 2)
                if not isinstance(k, int) or k >= 2:
                    pe.wait_ge(S("att_added"), k - 1)
                for t in range(TG):
                    for mc in range(2):
                        mm = pe.matmul(ps[:, 4 + bank, D * t:D * t + D], og[:, slot, mc, P * t:P * t + P], wo[:, mc, :],
                                       start=(mc == 0), stop=(mc == 1), skip_group_check=True)
                mm.then_inc(S("proj_ready"), 1)

            mix(0, 0)
            with pe.Fori(1, NG) as g:
                mix(g, 0)
            project(4 * NG - 1, 1, 1)

        def ln_stats(v, ph, g, par):
            link = chain(v, ph + "mean_v", g, 2)
            link(v.tensor_reduce(three(ln_sum[:, par]), grp(g), X, ALU.add))
            link(v.tensor_scalar(ln_mean[:, par], ln_sum[:, par], 1.0 / D, None, ALU.mult))
            v.tensor_tensor(four(cen[:, par]), grp(g), bc(three(ln_mean[:, par]), D), ALU.subtract).then_inc(S(ph + "cen_ready"), 1)

        def ln_var_v(v, ph, g, par, k1, k0):
            v.wait_ge(S(ph + "sq_ready"), g + 1)
            link = chain(v, ph + "var_v", g, 1)
            link(v.tensor_reduce(three(ln_var[:, par]), four(sq[:, par]), X, ALU.add))
            v.tensor_scalar(ln_ve[:, par], ln_var[:, par], k1, k0, ALU.mult, ALU.add).then_inc(S(ph + "ve_ready"), 1)

        def ln_norm(v, ph, g, par):
            v.wait_ge(S(ph + "rs_ready"), g + 1)
            v.tensor_tensor(four(zz[:, par]), four(cen[:, par]), bc(three(ln_rs[:, par]), D), ALU.mult).then_inc(S(ph + "z_ready"), 1)

        def split_low(v, ph, g, par):
            v.wait_ge(S(ph + "zh_ready"), g + 1)
            v.tensor_tensor(zst[:, par, :, 1, :], zz[:, par].rearrange("p (j d) -> p j d", d=D), zst[:, par, :, 0, :].bitcast(F32),
                            ALU.subtract).then_inc(S(ph + "zl_ready"), 1)

        def chain(eng, name, g, per, start=0):
            k = [start]

            def link(ins):
                k[0] += 1
                ins.then_inc(S(name), 1)
                eng.wait_ge(S(name), g * per + k[0])
            return link

        def ln_scalar(s, ph, g, par):
            s.wait_ge(S(ph + "cen_ready"), g + 1)
            s.activation(sq[:, par], cen[:, par], ACT.Square).then_inc(S(ph + "sq_ready"), 1)

        def ln_pool(p, ph, g, par):
            p.wait_ge(S(ph + "ve_ready"), g + 1)
            p.tensor_tensor(ln_rs[:, par], ln_ve[:, par], nhalf[:, :], ALU.pow).then_inc(S(ph + "rs_ready"), 1)

        def turn_pe(pe, ph, g, par):
            pe.wait_ge(S(ph + "zl_ready"), g + 1)
            for q in range(SETS):
                if late(g, 1) or q >= 2:
                    pe.wait_ge(S(ph + "zt_ready"), SETS * g + q - 1)
                for j in range(4):
                    mm = pe.transpose(ps[:, 5 + q % 2, P * j:P * j + P] if (q % 2 == 0) else ps[:, 6, P * j:P * j + P],
                                      zst[:, par, 4 * q + j].rearrange("p s d -> p (s d)").bitcast(F32), ident[:, :])
                mm.then_inc(S(ph + "tp_ready"), 1)

        def moe_pe(pe, ph, CH):
            lay = 0 if ph == "m" else 1
            w1H, w1L = (fw1H, fw1L) if lay == 0 else (gw1H, gw1L)
            pe.wait_ge(S("deep_ready"), 1)

            def logits(g, par):
                pe.wait_ge(S(ph + "zt_ready"), SETS * g + SETS)
                if late(g, 1):
                    pe.wait_ge(S(ph + "lg_read"), g)
                for j in range(GT):
                    for n, w in enumerate((wrH, wrL)):
                        mm = pe.matmul(ps[:, 7, E * j:E * j + E], zt[:, par, P * j:P * j + P], w[:, lay, :], start=(n == 0), stop=(n == 1),
                                       skip_group_check=True)
                mm.then_inc(S(ph + "lg_ready"), 1)

            def hidden(g, par, q):
                for c in range(CH):
                    k = CH * q + c
                    if late(g, 1) or k >= 3:
                        pe.wait_ge(S(ph + "h_ready"), SETS * CH * g + k - 2)
                    for n, w in enumerate((w1H, w1L)):
                        mm = pe.matmul(ps[:, k % 3, :], w[:, P * c:P * c + P], zt[:, par, 512 * q:512 * q + 512], start=(n == 0), stop=(n == 1))
                    mm.then_inc(S(ph + "h_mm"), 1)

            def outputs(g, q, slot):
                pe.wait_ge(S(ph + "h_ready"), SETS * CH * g + CH * q + CH)
                for j in range(4):
                    k = 4 * q + j
                    if late(g, 1) or k >= 2:
                        pe.wait_ge(S(ph + "y_used"), GT * g + k - 1)
                    y = ps[:, 3 + k % 2, :]
                    pe.matmul(y, onesR[:, :], b2sp[:, lay, :], start=True, stop=False, skip_group_check=True)
                    for c in range(CH):
                        if CH == 4:
                            mm = pe.matmul(y[:, P * c:P * c + P], hact[:, slot, c, P * j:P * j + P], fw2[:, c, :], start=False, stop=(c == CH - 1),
                                           skip_group_check=True)
                        else:
                            mm = pe.matmul(y[:, D * c:D * c + D], hact[:, slot, c, P * j:P * j + P], gw2[:, c, :], start=False, stop=(c == CH - 1),
                                           skip_group_check=True)
                    mm.then_inc(S(ph + "y_ready"), 1)

            def step(g, par, ahead, far):
                hidden(g, par, 0)
                if late(g, 1):
                    outputs(g - 1, 2, 1 - par)
                hidden(g, par, 1)
                outputs(g, 0, par)
                if ahead is not None:
                    turn_pe(pe, ph, ahead, 1 - par)
                hidden(g, par, 2)
                if ahead is not None:
                    logits(ahead, 1 - par)
                outputs(g, 1, 1 - par)

            turn_pe(pe, ph, 0, 0)
            logits(0, 0)
            steps(pe, step)
            outputs(NG - 1, 2, 0)

        def ret_pe(pe):
            def turn(g, par, q):
                if q == 0:
                    pe.wait_ge(S("rzl_ready"), g + 1)
                if late(g, 1) or q >= 1:
                    pe.wait_ge(S("rzt_ready"), SETS * g + q)
                for j in range(4):
                    mm = pe.transpose(ps[:, 7, P * j:P * j + P], zst[:, par, 4 * q + j].rearrange("p s d -> p (s d)").bitcast(F32), ident[:, :])
                mm.then_inc(S("rtp_ready"), 1)

            def project(g, par, t):
                k = TG * g + t
                pe.wait_ge(S("rzt_ready"), SETS * g + SETS)
                if late(g, 1) or t >= 1:
                    pe.wait_ge(S("rope_read"), k)
                    pe.wait_ge(S("val_ready"), k)
                for b in range(B):
                    zb = zt[:, par, P * (TG * b + t):P * (TG * b + t) + P]
                    for dst, c in ((ps[:, b // 2, 256 * (b % 2):256 * (b % 2) + 256], slice(0, 4 * D)), (ps[:, 2, D * b:D * b + D], slice(4 * D, NQ))):
                        for n, w in enumerate((wqkH, wqkL)):
                            mm = pe.matmul(dst, zb, w[:, c], start=(n == 0), stop=(n == 1), skip_group_check=True)
                mm.then_inc(S("qkv_mm"), 1)

            def turn_qk(g, t):
                k = TG * g + t
                pe.wait_ge(S("rot_ready"), k + 1)
                if late(g, 1) or t >= 1:
                    pe.wait_ge(S("qkT_ready"), k)
                for pair in range(2):
                    for n in range(2):
                        mm = pe.transpose(ps[:, 4, P * (2 * pair + n):P * (2 * pair + n) + P], rot[:, t, n, 2 * pair:2 * pair + 2, :].rearrange("p b d -> p (b d)"), ident[:, :])
                mm.then_inc(S("qkT_mm"), 1)

            def scores(g, t):
                k = TG * g + t
                pe.wait_ge(S("qkT_ready"), k + 1)
                if late(g, 1) or t >= 1:
                    pe.wait_ge(S("pmat_ready"), k)
                for b in (0, 2, 1, 3):
                    h = slice(64 * (b % 2), 64 * (b % 2) + 64)
                    mm = pe.matmul(ps[:, 5 + b % 2, P * (b // 2):P * (b // 2) + P], qkT[h, t, 2 * (b // 2) + 1, :], qkT[h, t, 2 * (b // 2), :], start=True, stop=True,
                                   skip_group_check=True)
                mm.then_inc(S("score_mm"), 1)

            def outputs(k, t):
                pe.wait_ge(S("state_ready"), k + 1)
                pe.wait_ge(S("pmat_ready"), k + 1)
                for b in range(B):
                    pe.matmul(ps[:, 3, D * b:D * b + D], qkT[:, t, 2 * (b // 2), :], state[:, t, b, :], start=True, stop=False,
                              skip_group_check=True)
                    mm = pe.matmul(ps[:, 3, D * b:D * b + D], pmat[:, t, b, :], val[:, t, b, :], start=False, stop=True,
                                   skip_group_check=True)
                mm.then_inc(S("ret_mm"), 1)

            def key_values(g, t):
                k = TG * g + t
                pe.wait_ge(S("val_ready"), k + 1)
                for pair in range(2):
                    mm = pe.matmul(ps[:, 3, 256 + P * pair:256 + P * pair + P], rot[:, t, 1, 2 * pair:2 * pair + 2, :].rearrange("p b d -> p (b d)"), val[:, t, 2 * pair:2 * pair + 2, :],
                                   start=True, stop=True, skip_group_check=True)
                mm.then_inc(S("kv_mm"), 1)

            def step(g, par, ahead, far):
                for t in range(TG):
                    up = t == 1 and ahead is not None
                    if up:
                        turn(ahead, 1 - par, 0)
                    scores(g, t)
                    if up:
                        turn(ahead, 1 - par, 1)
                    if late(g, 1) or t >= 1:
                        outputs(TG * g + t - 1, (t - 1) % TG)
                    if up:
                        turn(ahead, 1 - par, 2)
                    key_values(g, t)
                    if t < TG - 1 or ahead is not None:
                        turn_qk(g if t < TG - 1 else ahead, (t + 1) % TG)
                    if t == 0:
                        project(g, par, 2)
                    elif ahead is not None:
                        project(ahead, 1 - par, t - 1)

            pe.wait_ge(S("state_zero"), 1)
            for q in range(SETS):
                turn(0, 0, q)
            project(0, 0, 0)
            turn_qk(0, 0)
            project(0, 0, 1)
            steps(pe, step)
            outputs(TG * NG - 1, TG - 1)

        def attn_v(v):
            def low(g):
                v.wait_ge(S("z1h_ready"), g + 1)
                tok = bass.ds(g * TG * P, TG * P) if not isinstance(g, int) else slice(g * TG * P, (g + 1) * TG * P)
                for pair in range(2):
                    ins = v.tensor_tensor(ztL[:, pair, tok], ps[:, 2 + pair, 0:TG * P], ztH[:, pair, tok].bitcast(F32), ALU.subtract)
                ins.then_inc(S("zt_split"), 1)

            def var(g, par):
                ln_var_v(v, "a", g, par, (1.0 + EPS) / D, EPS * EPS)

            def step(g, par, ahead, far):
                if ahead is not None:
                    if late(g, 1):
                        v.wait_ge(S("z1_ready"), g)
                    ln_norm(v, "a", ahead, 1 - par)
                if far is not None:
                    ln_stats(v, "a", far, par)
                low(g)
                if far is not None:
                    var(far, par)

            ln_stats(v, "a", 0, 0)
            var(0, 0)
            ln_stats(v, "a", 1, 1)
            ln_norm(v, "a", 0, 0)
            var(1, 1)
            steps(v, step)
            v.wait_ge(S("gram_mm"), NG)
            v.tensor_copy(gramS[:, :, :], ps[:, 0:2, 0:256]).then_inc(S("gram_out"), 1)
            v.wait_ge(S("attw_in"), 16 * 10)
            link = chain(v, "v_mid", 0, 0)
            link(v.tensor_scalar(wgH[:, :, :], wgp[:, :, :], 1.0, None, ALU.mult))
            link(v.tensor_tensor(wgL[:, :, :], wgp[:, :, :], wgH[:, :, :].bitcast(F32), ALU.subtract))
            v.wait_ge(S("x_ready"), 1)
            for h in range(2):
                link(v.tensor_tensor(prodX[:, 4 * h:4 * h + 4, :].rearrange("p (s r) c -> p r s c", r=2), ps[:, 4 + 2 * h:6 + 2 * h, :].rearrange("p r (s c) -> p r s c", s=2),
                                     wq2[:, :].unsqueeze(1).unsqueeze(1).to_broadcast([P, 2, 2, 256]), ALU.mult))
            v.tensor_reduce(part[:, :], prodX[:, :, :].rearrange("p m (h c) -> p (m h) c", c=HC), X, ALU.add).then_inc(S("part_ready"), 1)
            v.wait_ge(S("att_ready"), 1)
            SC = 1.0 / np.sqrt(HC) / np.sqrt(L)
            a4 = at[:, :].rearrange("p (s t h) -> p s t h", s=B, t=B)
            b4 = at2[:, :].rearrange("p (s t h) -> p s t h", s=B, t=B)
            m3 = atm[:, :].rearrange("p (s h) -> p s h", s=B)
            link(v.tensor_scalar(at[:, :].rearrange("p (q r x) -> p r q x", q=2, r=2), ps[:, 2:4, 0:64].rearrange("p r (q x) -> p r q x", q=2), float(SC), None, ALU.mult))
            link(v.tensor_reduce(m3, a4.rearrange("p s t h -> p s h t"), X, ALU.max))
            v.tensor_tensor(a4, a4, m3.unsqueeze(2).to_broadcast([P, B, B, HEADS]), ALU.subtract).then_inc(S("att_sub"), 1)
            v.wait_ge(S("att_exp"), 1)
            link(v.tensor_reduce(m3, b4.rearrange("p s t h -> p s h t"), X, ALU.add))
            link(v.reciprocal(atm[:, :], atm[:, :]))
            link(v.tensor_tensor(b4, b4, m3.unsqueeze(2).to_broadcast([P, B, B, HEADS]), ALU.mult))
            for s in range(B):
                for pair in range(2):
                    for h in range(2):
                        r = slice(64 * h, 64 * h + 64)
                        ins = v.tensor_tensor(wmix[r, s, pair, :].rearrange("p (h c) -> p h c", c=HC), wv2[r, :].rearrange("p (h c) -> p h c", c=HC),
                                              b4[r, s, 2 * pair + h, :].unsqueeze(2).to_broadcast([64, HEADS, HC]), ALU.mult)
            link(ins)
            link(v.tensor_scalar(wmH[:, :, :, :], wmix[:, :, :, :], 1.0, None, ALU.mult))
            v.tensor_tensor(wmL[:, :, :, :], wmix[:, :, :, :], wmH[:, :, :, :].bitcast(F32), ALU.subtract).then_inc(S("wmix_ready"), 1)
            v.wait_ge(S("bo_added"), 1)

            def gate(g):
                for s in range(B):
                    for mc in range(2):
                        k = 2 * s + mc
                        v.wait_ge(S("sig_ready"), 8 * g + k + 1)
                        if (late(g, 1) or s >= 2) and mc == 0:
                            v.wait_ge(S("proj_ready"), 4 * g + s - 1)
                        v.tensor_tensor(og[:, s % 2, mc, :], sig[:, mc, :], ps[:, mc, 0:TG * P], ALU.mult).then_inc(S("og_ready"), 1)
                    if late(g, 1) or s >= 1:
                        add(g if s else g - 1, (s - 1) % B, 4 * g + s - 1)

            def add(g, s, k):
                v.wait_ge(S("proj_ready"), k + 1)
                dst = hid[:, s, bass.ds(g * TG, TG) if not isinstance(g, int) else slice(g * TG, g * TG + TG), :]
                v.tensor_tensor(dst, dst, ps[:, 4 + s % 2, 0:TG * D].rearrange("p (t d) -> p t d", d=D), ALU.add).then_inc(S("att_added"), 1)

            gate(0)
            with v.Fori(1, NG) as g:
                gate(g)
            add(NG - 1, B - 1, 4 * NG - 1)
            v.wait_ge(S("att_added"), 4 * NG)
            v.sem_inc(S("attn_free"), 1)

        def deep_prep_v(v):
            v.memset(fw2[:, :, :], 0.0).then_inc(S("fw2_zero"), 1)
            link = chain(v, "v_deep", 0, 0)
            link(v.tensor_scalar(onesR[:, :], ones[0:D, :], 1.0, None, ALU.mult))
            v.wait_ge(S("deepw_in"), 16 * (14 + 3 + 8))
            link(v.memset(b2sp[:, :, :].bitcast(F32), 0.0))
            for src, hi, lo in ((wr, wrH, wrL), (fw1, fw1H, fw1L), (gw1, gw1H, gw1L), (wqk, wqkH, wqkL)):
                i = tuple(slice(None) for _ in src.shape)
                link(v.tensor_scalar(hi[i], src[i], 1.0, None, ALU.mult))
                link(v.tensor_tensor(lo[i], src[i], hi[i].bitcast(F32), ALU.subtract))
            link(v.tensor_scalar(b2sp[0:1, :, :], bias2[0:1, :, :], 1.0, None, ALU.mult))
            link(v.tensor_scalar(b2sp[32:33, :, :], bias2[32:33, :, :], 1.0, None, ALU.mult))
            link(v.tensor_tensor(b2sp[32:33, :, :], bias2[32:33, :, :], b2sp[32:33, :, :].bitcast(F32), ALU.subtract))
            link(v.tensor_tensor(lgb[:, :], lgb[:, :], lgb2[:, :], ALU.add))
            for e in range(E):
                ins = v.memset(desc[:, e:e + 1], float(E - e))
            link(ins)
            v.sem_inc(S("deep_ready"), 1)

        def moe_v(v, ph, CH):
            R = lambda n: lg[:, n, :].rearrange("p (j e) -> p j e", e=E)
            bce = lambda x: x.unsqueeze(2).to_broadcast([P, GT, E])
            row = lambda x: x.unsqueeze(1).to_broadcast([P, GT, E])

            def top_two(g):
                link = chain(v, ph + "top_v", g, 11)
                v.wait_ge(S(ph + "lg_ready"), g + 1)
                src = ps[:, 7, 0:GT * E].rearrange("p (j e) -> p j e", e=E)
                if ph == "x":
                    v.tensor_tensor(R(0), src, row(lgb[:, :]), ALU.add).then_inc(S(ph + "lg_read"), 1)
                else:
                    v.tensor_copy(R(0), src).then_inc(S(ph + "lg_read"), 1)
                yield
                v.wait_ge(S(ph + "lg_read"), g + 1)
                cur = 0
                for n in range(2):
                    link(v.tensor_reduce(rt[:, n, :], R(cur), X, ALU.max))
                    yield
                    link(v.tensor_tensor(R(1), R(cur), bce(rt[:, n, :]), ALU.is_equal))
                    link(v.tensor_tensor(R(1), R(1), row(desc[:, :]), ALU.mult))
                    yield
                    link(v.tensor_reduce(rt[:, 2, :], R(1), X, ALU.max))
                    link(v.tensor_tensor(R(2 + n), R(1), bce(rt[:, 2, :]), ALU.is_equal))
                    if n == 0:
                        link(v.scalar_tensor_tensor(lg[:, 4, :], lg[:, 2, :], -1e30, lg[:, 0, :], ALU.mult, ALU.add))
                        cur = 4
                    yield
                v.tensor_tensor(rt[:, 3, :], rt[:, 0, :], rt[:, 1, :], ALU.subtract).then_inc(S(ph + "gap_ready"), 1)

            def weights(g, par):
                link = chain(v, ph + "wgt_v", g, 3)
                v.wait_ge(S(ph + "tanh_ready"), g + 1)
                v.tensor_scalar(rt[:, 6, :], rt[:, 4, :], -0.5, 0.5, ALU.mult, ALU.add)
                link(v.tensor_scalar(rt[:, 5, :], rt[:, 4, :], 0.5, 0.5, ALU.mult, ALU.add))
                link(v.tensor_tensor(R(2), R(2), bce(rt[:, 5, :]), ALU.mult))
                link(v.tensor_tensor(R(3), R(3), bce(rt[:, 6, :]), ALU.mult))
                v.tensor_tensor(comb[:, par], lg[:, 2, :], lg[:, 3, :], ALU.add).then_inc(S(ph + "comb_ready"), 1)
                v.wait_ge(S(ph + "comb_ready"), g + 1)

            def scale(g, par, q, slot, between=()):
                if late(g, 1) or q >= 2:
                    v.wait_ge(S(ph + "prod_used"), SETS * g + q - 1)
                for j in range(4):
                    k = 4 * q + j
                    v.wait_ge(S(ph + "y_ready"), GT * g + k + 1)
                    v.tensor_tensor(prod[:, slot, j, :].rearrange("p (e d) -> p e d", d=D), ps[:, 3 + k % 2, :].rearrange("p (e d) -> p e d", d=D),
                                    comb[:, par, E * k:E * k + E].unsqueeze(2).to_broadcast([P, E, D]), ALU.mult).then_inc(S(ph + "y_used"), 1)
                    for _ in (0, 1):
                        next(between, None) if between else None

            def var(g, par):
                ln_var_v(v, ph, g, par, 1.0 / D, EPS)

            def step(g, par, ahead, far):
                if late(g, 1):
                    scale(g - 1, 1 - par, 2, 1 - par)
                    weights(g, par)
                if ahead is not None:
                    if ph == "m" and late(g, 1):
                        v.wait_ge(S(ph + "hz_added"), g)
                    ln_norm(v, ph, ahead, 1 - par)
                scale(g, par, 0, par, split(ahead, 1 - par) if ahead is not None else ())
                if far is not None:
                    ln_stats(v, ph, far, par)
                if ahead is not None:
                    top = top_two(ahead)
                    scale(g, par, 1, 1 - par, top)
                    for _ in top:
                        pass
                else:
                    scale(g, par, 1, 1 - par)
                if far is not None:
                    var(far, par)

            def split(g, par):
                yield
                yield
                split_low(v, ph, g, par)

            if ph == "x":
                v.wait_ge(S("ret_added"), NT)
            ln_stats(v, ph, 0, 0)
            var(0, 0)
            ln_stats(v, ph, 1, 1)
            ln_norm(v, ph, 0, 0)
            split_low(v, ph, 0, 0)
            var(1, 1)
            for _ in top_two(0):
                pass
            weights(0, 0)
            steps(v, step)
            scale(NG - 1, 0, 2, 0)

        def ret_v(v):
            def rope(g, par, t):
                k = TG * g + t
                if t == 0:
                    v.wait_ge(S("tab_in%d" % par), 8 * (g - par) + 16)
                v.wait_ge(S("qkv_mm"), k + 1)
                if late(g, 1) or t >= 1:
                    v.wait_ge(S("rot_ready"), k)
                tb = lambda n: tabc[:, par, 2 * t + n, :].rearrange("p (n d) -> p n d", n=2).unsqueeze(1).to_broadcast([P, B, 2, D])
                q4 = lambda c: ps[:, 0:2, :].rearrange("p a (c y) -> p (a c) y", c=2)[:, :, c:c + 2 * D].rearrange("p b (n d) -> p b n d", n=2)
                v.tensor_tensor(rA[:, :, :, :].rearrange("p n b d -> p b n d"), q4(0), tb(0), ALU.mult)
                v.tensor_tensor(rB[:, :, :, :].rearrange("p n b d -> p b n d"), q4(2 * D), tb(1), ALU.mult).then_inc(S("rope_read"), 1)

            def mask(g, t):
                k = TG * g + t
                v.wait_ge(S("score_mm"), k + 1)
                v.tensor_tensor(pmat[:, t, :, :].rearrange("p (j r) n -> p r j n", r=2), ps[:, 5:7, 0:256].rearrange("p r (j n) -> p r j n", j=2), causal[:, :].unsqueeze(1).unsqueeze(1).to_broadcast([P, 2, 2, P]),
                                ALU.mult).then_inc(S("pmat_ready"), 1)

            def add(k):
                dst = hid[:, :, bass.ds(k, 1) if not isinstance(k, int) else slice(k, k + 1), :].rearrange("p b t d -> p b (t d)")
                v.tensor_tensor(dst, dst, ps[:, 3, 0:256].rearrange("p (b d) -> p b d", b=B), ALU.add).then_inc(S("ret_added"), 1)

            def update(g, t):
                k = TG * g + t
                v.wait_ge(S("kv_mm"), k + 1)
                if late(g, 1) or t >= 1:
                    add(k - 1)
                for h in range(2):
                    r = slice(64 * h, 64 * h + 64)
                    own = state[r, t, :, :].rearrange("p (j r) d -> p r j d", r=2)[:, h]
                    kv = ps[r, 3, 256:512].rearrange("p (j c) -> p j c", j=2)[:, :, D * h:D * h + D]
                    ins = v.tensor_tensor(stt[r, :, :], own, kv, ALU.add)
                ins.then_inc(S("stt_v"), 1)
                v.wait_ge(S("stt_v"), k + 1)
                for h in range(2):
                    r = slice(64 * h, 64 * h + 64)
                    new = state[r, (t + 1) % TG, :, :].rearrange("p (j r) d -> p r j d", r=2)[:, h]
                    ins = v.tensor_scalar(new, stt[r, :, :], float(GAMMA ** P), None, ALU.mult)
                ins.then_inc(S("state_ready"), 1)

            def var(g, par):
                ln_var_v(v, "r", g, par, 1.0 / D, EPS)

            def step(g, par, ahead, far):
                for t in range(TG):
                    if t < TG - 1 or ahead is not None:
                        rope(g if t < TG - 1 else ahead, par if t < TG - 1 else 1 - par, (t + 1) % TG)
                    if t == 0 and ahead is not None:
                        ln_norm(v, "r", ahead, 1 - par)
                    mask(g, t)
                    if t == 0 and ahead is not None:
                        split_low(v, "r", ahead, 1 - par)
                    if t == 1 and far is not None:
                        ln_stats(v, "r", far, par)
                    if t == 2 and far is not None:
                        var(far, par)
                    update(g, t)

            v.wait_ge(S("mh_added"), NG)
            v.memset(state[:, :, :, :], 0.0).then_inc(S("state_zero"), 1)
            ln_stats(v, "r", 0, 0)
            var(0, 0)
            ln_stats(v, "r", 1, 1)
            ln_norm(v, "r", 0, 0)
            split_low(v, "r", 0, 0)
            var(1, 1)
            rope(0, 0, 0)
            steps(v, step)
            v.wait_ge(S("ret_mm"), NT)
            add(NT - 1)

        def attn_s(s):
            def high(g):
                tok = bass.ds(g * TG * P, TG * P) if not isinstance(g, int) else slice(g * TG * P, (g + 1) * TG * P)
                s.wait_ge(S("z1_turned"), g + 1)
                s.activation(ztH[:, :, tok], ps[:, 2:4, 0:TG * P], ACT.Copy).then_inc(S("z1h_ready"), 1)

            def step(g, par, ahead, far):
                if far is not None:
                    ln_scalar(s, "a", far, par)
                high(g)

            ln_scalar(s, "a", 0, 0)
            ln_scalar(s, "a", 1, 1)
            steps(s, step)
            s.wait_ge(S("att_sub"), 1)
            s.activation(at2[:, :], at[:, :], ACT.Exp).then_inc(S("att_exp"), 1)

            def gate(g):
                for k in range(8):
                    s.wait_ge(S("mix_ready"), 8 * g + k + 1)
                    if late(g, 1) or k >= 2:
                        s.wait_ge(S("og_ready"), 8 * g + k - 1)
                    s.activation(sig[:, k % 2, :], ps[:, 2 + k % 2, 0:TG * P], ACT.Sigmoid, bias=bgc[:, k % 2:k % 2 + 1]).then_inc(S("sig_ready"), 1)

            gate(0)
            with s.Fori(1, NG) as g:
                gate(g)

        def split_s(s, ph, g, par):
            s.wait_ge(S(ph + "z_ready"), g + 1)
            if late(g, 2):
                s.wait_ge(S(ph + "tp_ready"), SETS * (g - 1))
            s.activation(zst[:, par, :, 0, :], zz[:, par].rearrange("p (j d) -> p j d", d=D), ACT.Copy).then_inc(S(ph + "zh_ready"), 1)

        def evac_s(s, ph, g, par, banks):
            for q in range(SETS):
                s.wait_ge(S(ph + "tp_ready"), SETS * g + q + 1)
                s.activation(zt[:, par, 512 * q:512 * q + 512], ps[:, banks[q % len(banks)], :], ACT.Copy).then_inc(S(ph + "zt_ready"), 1)

        def moe_s(s, ph, CH):
            bias = fb1 if ph == "m" else gb1
            fn = ACT.Gelu if ph == "m" else ACT.Relu
            s.wait_ge(S("deep_ready"), 1)

            def act(g, q, slot):
                for c in range(CH):
                    k = CH * q + c
                    s.wait_ge(S(ph + "h_mm"), SETS * CH * g + k + 1)
                    if (late(g, 1) or q >= 2) and c == 0:
                        s.wait_ge(S(ph + "y_ready"), GT * g + 4 * q - 4)
                    s.activation(hact[:, slot, c, :], ps[:, k % 3, :], fn, bias=bias[:, c:c + 1]).then_inc(S(ph + "h_ready"), 1)

            def tanh(g):
                s.wait_ge(S(ph + "gap_ready"), g + 1)
                s.activation(rt[:, 4, :], rt[:, 3, :], ACT.Tanh, scale=0.5).then_inc(S(ph + "tanh_ready"), 1)

            def step(g, par, ahead, far):
                act(g, 0, par)
                if late(g, 1):
                    tanh(g)
                if ahead is not None:
                    split_s(s, ph, ahead, 1 - par)
                act(g, 1, 1 - par)
                if ahead is not None:
                    evac_s(s, ph, ahead, 1 - par, (5, 6))
                if far is not None:
                    ln_scalar(s, ph, far, par)
                act(g, 2, par)

            ln_scalar(s, ph, 0, 0)
            ln_scalar(s, ph, 1, 1)
            split_s(s, ph, 0, 0)
            evac_s(s, ph, 0, 0, (5, 6))
            tanh(0)
            steps(s, step)

        def ret_s(s):
            def values(g, t):
                s.wait_ge(S("qkv_mm"), TG * g + t + 1)
                s.activation(val[:, t, :, :], ps[:, 2, 0:4 * D].rearrange("p (b d) -> p b d", b=B), ACT.Copy).then_inc(S("val_ready"), 1)

            def turned(g, t):
                s.wait_ge(S("qkT_mm"), TG * g + t + 1)
                s.activation(qkT[:, t, :, :], ps[:, 4, :].rearrange("p (n q) -> p n q", n=4), ACT.Copy).then_inc(S("qkT_ready"), 1)

            def step(g, par, ahead, far):
                for t in range(TG):
                    if t == 0 and ahead is not None:
                        split_s(s, "r", ahead, 1 - par)
                    if t == 1 and ahead is not None:
                        evac_s(s, "r", ahead, 1 - par, (7,))
                    if t < TG - 1 or ahead is not None:
                        turned(g if t < TG - 1 else ahead, (t + 1) % TG)
                    if t == 0:
                        values(g, 2)
                    elif ahead is not None:
                        values(ahead, t - 1)
                    if t == 1 and far is not None:
                        ln_scalar(s, "r", far, par)

            ln_scalar(s, "r", 0, 0)
            ln_scalar(s, "r", 1, 1)
            split_s(s, "r", 0, 0)
            evac_s(s, "r", 0, 0, (7,))
            values(0, 0)
            turned(0, 0)
            values(0, 1)
            steps(s, step)

        def attn_p(p):
            p.wait_ge(S("embed_done"), 1)
            p.memset(wgp[:, :, :], 0.0).then_inc(S("wgp_zero"), 1)
            p.wait_ge(S("row_in"), 16 * 5)
            row = lambda x: x[:, :].unsqueeze(1).unsqueeze(1).to_broadcast([P, B, TG, D])

            def affine(g, par):
                link = chain(p, "p_aff", g, 1)
                p.wait_ge(S("az_ready"), g + 1)
                if late(g, 1):
                    p.wait_ge(S("gram_mm"), g)
                z3 = zs1[:, par].rearrange("p (t b d) -> p b t d", b=B, t=TG)
                link(p.tensor_tensor(z3, four(zz[:, par]), row(gam), ALU.mult))
                p.tensor_tensor(z3, z3, row(bet), ALU.add).then_inc(S("z1_ready"), 1)

            def step(g, par, ahead, far):
                if ahead is not None:
                    affine(ahead, 1 - par)
                if far is not None:
                    ln_pool(p, "a", far, par)

            ln_pool(p, "a", 0, 0)
            affine(0, 0)
            ln_pool(p, "a", 1, 1)
            steps(p, step)
            p.wait_ge(S("acen_ready"), NG)
            for b in range(B):
                ins = p.tensor_tensor(hid[:, b], hid[:, b], bo_row[:, :].unsqueeze(1).to_broadcast([P, NT, D]), ALU.add)
            ins.then_inc(S("bo_added"), 1)

        def moe_p(p, ph, CH):
            def sums(g, par, q, slot):
                link = chain(p, ph + "tree", SETS * g + q, 1)
                p.wait_ge(S(ph + "y_used"), GT * g + 4 * q + 4)
                if late(g, 1) or q:
                    p.wait_ge(S(ph + "sum_done"), SETS * g + q)
                p.tensor_tensor(tree[:, :, :], prod[:, slot, :, 0:256], prod[:, slot, :, 256:512], ALU.add).then_inc(S(ph + "prod_used"), 1)
                p.wait_ge(S(ph + "prod_used"), SETS * g + q + 1)
                link(p.tensor_tensor(tree2[:, :, :], tree[:, :, 0:128], tree[:, :, 128:256], ALU.add))
                p.tensor_tensor(ysum[:, par].rearrange("p (j d) -> p j d", d=D)[:, 4 * q:4 * q + 4, :], tree2[:, :, 0:64], tree2[:, :, 64:128],
                                ALU.add).then_inc(S(ph + "sum_done"), 1)
                if q == SETS - 1:
                    p.wait_ge(S(ph + "sum_done"), SETS * g + SETS)
                    p.tensor_tensor(grp(g), grp(g), four(ysum[:, par]), ALU.add).then_inc(S(ph + "h_added"), 1)

            def residual(g, par):
                p.wait_ge(S(ph + "z_ready"), g + 1)
                p.tensor_tensor(grp(g), grp(g), four(zz[:, par]), ALU.add).then_inc(S(ph + "hz_added"), 1)

            def step(g, par, ahead, far):
                if ahead is not None and ph == "m":
                    residual(ahead, 1 - par)
                if late(g, 1):
                    sums(g - 1, 1 - par, 2, 1 - par)
                sums(g, par, 0, par)
                sums(g, par, 1, 1 - par)
                if far is not None:
                    ln_pool(p, ph, far, par)

            ln_pool(p, ph, 0, 0)
            ln_pool(p, ph, 1, 1)
            if ph == "m":
                residual(0, 0)
            steps(p, step)
            sums(NG - 1, 0, 2, 0)

        def ret_p(p):
            def rope(g, t):
                p.wait_ge(S("rope_read"), TG * g + t + 1)
                p.tensor_tensor(rot[:, t, :, :, :], rA[:, :, :, :], rB[:, :, :, :], ALU.add).then_inc(S("rot_ready"), 1)

            def step(g, par, ahead, far):
                for t in range(TG):
                    if t < TG - 1 or ahead is not None:
                        rope(g if t < TG - 1 else ahead, (t + 1) % TG)
                    if t == 2 and far is not None:
                        ln_pool(p, "r", far, par)

            ln_pool(p, "r", 0, 0)
            ln_pool(p, "r", 1, 1)
            rope(0, 0)
            steps(p, step)

        @block.sync
        def _(sp):
            def rows_load(b):
                for i in range(3):
                    for c2 in range(2):
                        sp.dma_start(rows[64 * c2:64 * c2 + 64, b % 2, i], A["x_rows"][b, c2, i:i + HH]).then_inc(S("rows_in%d" % (b % 2)), 16)

            sp.dma_start(xch[0:64, :], A["x"][0].rearrange("c h w -> c (h w)")).then_inc(S("xch_in0"), 16)
            for h in range(2):
                sp.dma_start(w1c[64 * h:64 * h + 64, :], A["conv1_wT"]).then_inc(S("embw_in"), 16)
            sp.dma_start(w2c[0:16, :], A["conv2_wT"]).then_inc(S("embw_in"), 16)
            sp.dma_start(w2c[16:17, :], A["L0_tok_conv2_b"].unsqueeze(0)).then_inc(S("embw_in"), 16)
            for n, k in enumerate(("conv1_b", "bn_gamma", "bn_beta", "bn_mean", "bn_var")):
                sp.dma_start(bnv[:, n:n + 1], A["L0_tok_" + k].unsqueeze(1)).then_inc(S("embw_in"), 16)
            sp.dma_start(xch[64:128, :], A["x"][1].rearrange("c h w -> c (h w)")).then_inc(S("xch_in1"), 16)
            rows_load(0)
            rows_load(1)
            for dst, src in ((gam, "L0_attn_gamma"), (bet, "L0_attn_beta"), (bo_row, "L0_attn_bo"), (lgb, "L1_ffn_bg"), (lgb2, "L1_ffn_bias")):
                sp.dma_start(dst[:, :], A[src].partition_broadcast(P)).then_inc(S("row_in"), 16)
            sp.dma_start(ids[:, :], A["x_txt"].rearrange("b (s o) -> (b s) o", o=1)).then_inc(S("ids_in"), 16)
            for b in range(B):
                sp.dma_start(tx["u"][TXT * b:TXT * b + TXT, :], A["L0_txt_U_w"][0:TXT, :]).then_inc(S("txt_in"), 16)
            for dst, src in (("g", "L0_txt_ln_g"), ("b", "L0_txt_ln_b"), ("ob", "L0_txt_b")):
                sp.dma_start(tx[dst][:, :], A[src].partition_broadcast(P)).then_inc(S("txt_in"), 16)
            sp.dma_start(tx["wT"][:, :], A["txt_WT"]).then_inc(S("txt_in"), 16)
            for b in (2, 3):
                sp.wait_ge(S("conv_ready"), 8 * (b - 1))
                sp.dma_start(xch[64 * (b % 2):64 * (b % 2) + 64, :], A["x"][b].rearrange("c h w -> c (h w)")).then_inc(S("xch_in%d" % (b % 2)), 16)
                sp.wait_ge(S("rows_used_v"), b - 1)
                sp.wait_ge(S("rows_used_p"), b - 1)
                rows_load(b)
            sp.wait_ge(S("txt_done"), 1)
            for b in range(B):
                sp.dma_start(hid[0:TXT, b, NT - 1, :], tx["o"][TXT * b:TXT * b + TXT, :]).then_inc(S("txt_put"), 16)
            sp.wait_ge(S("txt_put"), 16 * B)
            sp.wait_ge(S("embed_done"), 1)
            for h in range(2):
                for dst, src in ((wk2, "Wk"), (wq2, "Wq"), (wv2, "Wv")):
                    sp.dma_start(dst[64 * h:64 * h + 64, :], A["L0_attn_" + src]).then_inc(S("attw_in"), 16)
            sp.wait_ge(S("wgp_zero"), 1)
            for h in range(2):
                sp.dma_start(wgp[64 * h:64 * h + 64, h, :], A["L0_attn_Wg"]).then_inc(S("attw_in"), 16)
            sp.dma_start(wo[:, :, :], A["L0_attn_Wo"].rearrange("(m k) d -> k m d", m=2)).then_inc(S("attw_in"), 16)
            sp.dma_start(bgc[:, :], A["bgT"]).then_inc(S("attw_in"), 16)
            sp.wait_ge(S("attn_free"), 1)
            n = S("deepw_in")
            for h in range(2):
                r = slice(64 * h, 64 * h + 64)
                sp.dma_start(wr[r, 0, :], A["router_wT"]).then_inc(n, 16)
                sp.dma_start(wr[r, 1, :], A["L1_ffn_Wg"]).then_inc(n, 16)
                sp.dma_start(fw1[r, :].rearrange("p (e f) -> p e f", e=E), A["L0_ffn_w1"].rearrange("e d f -> d e f")).then_inc(n, 16)
                sp.dma_start(gw1[r, :].rearrange("p (e f) -> p e f", e=E), A["L1_ffn_W1"].rearrange("e d f -> d e f")).then_inc(n, 16)
                sp.dma_start(wqk[r, :], A["w_qk"]).then_inc(n, 16)
                sp.dma_start(bias2[32 * h:32 * h + 1, 0, :], A["L0_ffn_b2"].rearrange("(o e) d -> o (e d)", o=1)).then_inc(n, 16)
                sp.dma_start(bias2[32 * h:32 * h + 1, 1, :], A["L1_ffn_b2"].rearrange("(o e) d -> o (e d)", o=1)).then_inc(n, 16)
            sp.dma_start(fb1[:, :], A["ffn0_b1T"]).then_inc(n, 16)
            sp.dma_start(gb1[:, :], A["ffn1_b1T"]).then_inc(n, 16)
            sp.dma_start(gw2[:, :, :], A["L1_ffn_W2"].rearrange("e f d -> f e d")).then_inc(n, 16)
            sp.wait_ge(S("fw2_zero"), 1)
            for e in range(E):
                h = e % 2
                sp.dma_start(fw2[64 * h:64 * h + 64, e // 2, 64 * h:64 * h + 64], A["L0_ffn_w2"][e]).then_inc(n, 16)
            def tab_load(g, par):
                if late(g, 2):
                    sp.wait_ge(S("rope_read"), TG * (g - 1))
                sp.dma_start(tabc[:, par], A["tables"][g if isinstance(g, int) else bass.ds(g, 1)] if isinstance(g, int)
                             else A["tables"][bass.ds(g, 1)].rearrange("o p t c -> (o p) t c")).then_inc(S("tab_in%d" % par), 16)
            tab_load(0, 0)
            tab_load(1, 1)
            with sp.Fori(0, (NG - 3) // 2) as i:
                for u in (0, 1):
                    tab_load(2 * i + 2 + u, u)
            tab_load(NG - 1, 0)
            sp.wait_ge(S("stage_done"), 1)
            for b in range(B):
                sp.dma_start(out[b, 0:(NT - 1) * P, :].rearrange("(t p) d -> p t d", p=P), hid[:, b, 0:NT - 1, :]).then_inc(S("out_done"), 16)
                sp.dma_start(out[b, (NT - 1) * P:L, :], hid[0:TXT, b, NT - 1, :]).then_inc(S("out_done"), 16)
            sp.wait_ge(S("out_done"), 16 * 2 * B)

        @block.tensor
        def _(pe):
            ACC, CONV, WD, TXB = 0, 4, 6, 7
            pe.wait_ge(S("embw_in"), 16 * 9)
            pe.wait_ge(const_ready, 1)

            def conv(b, u):
                pe.wait_ge(S("xch_in%d" % u), 16 * (b // 2 + 1))
                for n in range(8):
                    k = 8 * b + n
                    if k >= 2:
                        pe.wait_ge(S("y_ready"), k - 1)
                    mm = pe.matmul(ps[0:16, CONV + n % 2, :], w1c[64 * u:64 * u + 64, :], xch[64 * u:64 * u + 64, 512 * n:512 * n + 512],
                                   start=True, stop=True).then_inc(S("conv_ready"), 1)
                pe.wait_ge(S("y_ready"), 8 * b + 8)
                yv = yact[0:17, :].rearrange("k (h w) -> k w h", w=WW)
                for half in range(2):
                    if 2 * b + half >= 1:
                        pe.wait_ge(S("wd_ready"), 2 * b + half)
                    for w in range(32):
                        for c2 in range(2):
                            mm = pe.matmul(ps[64 * c2:64 * c2 + 64, WD, 9 * w:9 * w + 9], yv[:, 32 * half + w, :], w2c[0:17, :],
                                           start=True, stop=True, skip_group_check=True)
                    mm.then_inc(S("wd_mm"), 1)

            def add_terms(b):
                if b >= 1:
                    pe.wait_ge(S("embed_out"), b)
                for n, (buf, s) in enumerate(((dA, "termA"), (pD, "termD"), (dB, "termB"), (pE, "termE"), (dC, "termC"))):
                    pe.wait_ge(S(s), b + 1)
                    for q in range(4):
                        mm = pe.matmul(ps[:, ACC + q, :], ident[:, :], buf[:, 8 * q:8 * q + 8, :], start=(n == 0), stop=(n == 4))
                    mm.then_inc(S("term_used"), 1)

            conv(0, 0)
            for b in range(B):
                if b + 1 < B:
                    conv(b + 1, (b + 1) % 2)
                add_terms(b)

            t = ps[:, TXB, :]
            pe.wait_ge(S("tx_v"), 1)
            pe.transpose(t[0:D, 0:P], tx["a"][:, :], ident[:, :]).then_inc(S("tx_pe"), 1)
            for r in range(3):
                pe.wait_ge(S("tx_v"), 2 + 4 * r)
                pe.transpose(t[0:D, 128:256], tx["u"][:, :], ident[:, :]).then_inc(S("tx_pe"), 1)
                pe.wait_ge(S("tx_v"), 3 + 4 * r)
                for b in range(B):
                    mm = pe.matmul(t[TXT * b:TXT * b + TXT, 256:256 + TXT], tx["aT"][:, TXT * b:TXT * b + TXT], tx["uT"][:, TXT * b:TXT * b + TXT],
                                   start=True, stop=True, skip_group_check=True)
                mm.then_inc(S("tx_pe"), 1)
                pe.wait_ge(S("tx_v"), 5 + 4 * r)
                for b in range(B):
                    s = slice(TXT * b, TXT * b + TXT)
                    mm = pe.matmul(t[s, 320:384], tx["p"][s, :], tx["c"][s, :], start=True, stop=True, skip_group_check=True)
                mm.then_inc(S("tx_pe"), 1)
            pe.wait_ge(S("tx_v"), 15)
            pe.transpose(t[0:D, 0:P], tx["z"][:, :], ident[:, :]).then_inc(S("tx_pe"), 1)
            pe.wait_ge(S("tx_v"), 16)
            pe.matmul(t[:, 128:192], tx["zT"][:, :], tx["wT"][:, :], start=True, stop=True).then_inc(S("tx_pe"), 1)

            gram_pe(pe)
            moe_pe(pe, "m", 4)
            ret_pe(pe)
            moe_pe(pe, "x", 8)

        @block.vector
        def _(v):
            def once(name):
                return chain(v, name, 0, 0)

            link = once("v_pre")
            v.memset(ones[:, :], 1.0).then_inc(S("v_set"), 1)
            v.memset(nhalf[:, :], -0.5).then_inc(S("v_set"), 1)
            v.memset(yact[:, :], 1.0).then_inc(S("v_set"), 1)
            link(v.memset(hid[:, :, NT - 1, :], 0.0))
            v.wait_ge(S("embw_in"), 16 * 9)
            link(v.tensor_scalar(bnv[:, 5:6], bnv[:, 4:5], EPS, None, ALU.add))
            v.wait_ge(S("v_set"), 3)
            v.tensor_copy(bnv[:, 9:10], nhalf[0:16, 0:1]).then_inc(S("bn_var"), 1)
            v.wait_ge(S("bn_rs"), 1)
            link(v.tensor_tensor(bnv[:, 7:8], bnv[:, 6:7], bnv[:, 1:2], ALU.mult))
            link(v.tensor_tensor(bnv[:, 8:9], bnv[:, 0:1], bnv[:, 3:4], ALU.subtract))
            link(v.tensor_tensor(bnv[:, 8:9], bnv[:, 8:9], bnv[:, 7:8], ALU.mult))
            v.tensor_tensor(bnv[:, 8:9], bnv[:, 8:9], bnv[:, 2:3], ALU.add).then_inc(S("bn_ready"), 1)
            v.wait_ge(S("ids_in"), 16)
            v.tensor_scalar(idc[:, 0:1], ids[:, :], 0, A["L0_txt_A_w"].shape[0] - 1, ALU.max, ALU.min).then_inc(S("idc_ready"), 1)

            link = once("v_emb")

            def tap(buf, u, i, j):
                return v.tensor_tensor(buf[:, :, :], rows[:, u, i, :, j:j + WW], wdyn[:, u, 3 * i + j, :].unsqueeze(1).to_broadcast([P, CP, WW]), ALU.mult)

            for b in range(B):
                u = b % 2
                v.wait_ge(S("rows_in%d" % u), 16 * 6 * (b // 2 + 1))
                v.wait_ge(S("wd_ready"), 2 * b + 2)
                if b:
                    v.wait_ge(S("term_used"), 5 * b)
                link(tap(dA, u, 1, 0))
                link(tap(dT, u, 1, 1))
                v.tensor_tensor(dA[:, :, :], dA[:, :, :], dT[:, :, :], ALU.add).then_inc(S("termA"), 1)
                tap(dB, u, 1, 2).then_inc(S("termB"), 1)
                link(tap(dC, u, 2, 0))
                v.wait_ge(S("termA"), b + 1)
                link(tap(dT, u, 2, 1))
                link(v.tensor_tensor(dC[:, :, :], dC[:, :, :], dT[:, :, :], ALU.add))
                link(tap(dT, u, 2, 2))
                v.tensor_tensor(dC[:, :, :], dC[:, :, :], dT[:, :, :], ALU.add).then_inc(S("termC"), 1)
                v.wait_ge(S("termC"), b + 1)
                v.wait_ge(S("termB"), b + 1)
                v.sem_inc(S("rows_used_v"), 1)

            link = once("v_txt")
            T = ps[:, 7, :]
            v.wait_ge(S("txt_in"), 16 * 8)
            v.wait_ge(S("gath_in"), 32)
            link(v.tensor_copy(tx["o"][:, :], tx["u"][:, :]))
            v.tensor_copy(tx["q"][:, :], tx["o"][:, :]).then_inc(S("tx_v"), 1)
            v.wait_ge(S("tx_pe"), 1)
            v.tensor_copy(tx["aT"][:, :], T[0:D, 0:P]).then_inc(S("tx_v"), 1)
            for r in range(3):
                v.wait_ge(S("tx_pe"), 2 + 3 * r)
                v.tensor_copy(tx["uT"][:, :], T[0:D, 128:256]).then_inc(S("tx_v"), 1)
                v.wait_ge(S("tx_pe"), 3 + 3 * r)
                sc = T[:, 256:256 + TXT]
                link(v.tensor_reduce(tx["m"][:, 0:1], sc, X, ALU.max))
                v.tensor_scalar(tx["s"][:, :], sc, tx["m"][:, 0:1], None, ALU.subtract).then_inc(S("tx_v"), 1)
                v.wait_ge(S("tx_e"), r + 1)
                link(v.reciprocal(tx["m"][:, 2:3], tx["m"][:, 1:2]))
                v.tensor_scalar(tx["p"][:, :], tx["s"][:, :], tx["m"][:, 2:3], None, ALU.mult).then_inc(S("tx_v"), 1)
                v.wait_ge(S("tx_pe"), 4 + 3 * r)
                if r < 2:
                    v.tensor_tensor(tx["u"][:, :], tx["u"][:, :], T[:, 320:384], ALU.add).then_inc(S("tx_v"), 1)
                else:
                    link(v.tensor_tensor(tx["u"][:, :], tx["u"][:, :], T[:, 320:384], ALU.add))
            link(v.tensor_reduce(tx["m"][:, 3:4], tx["u"][:, :], X, ALU.add))
            link(v.tensor_scalar(tx["m"][:, 3:4], tx["m"][:, 3:4], 1.0 / D, None, ALU.mult))
            link(v.tensor_scalar(tx["u"][:, :], tx["u"][:, :], tx["m"][:, 3:4], None, ALU.subtract))
            link(v.tensor_tensor(tx["q"][:, :], tx["u"][:, :], tx["u"][:, :], ALU.mult))
            link(v.tensor_reduce(tx["m"][:, 4:5], tx["q"][:, :], X, ALU.add))
            v.tensor_scalar(tx["m"][:, 4:5], tx["m"][:, 4:5], 1.0 / D, EPS, ALU.mult, ALU.add).then_inc(S("tx_v"), 1)
            v.wait_ge(S("tx_rs"), 1)
            link(v.tensor_scalar(tx["z"][:, :], tx["u"][:, :], tx["m"][:, 5:6], None, ALU.mult))
            link(v.tensor_tensor(tx["z"][:, :], tx["z"][:, :], tx["g"][:, :], ALU.mult))
            v.tensor_tensor(tx["z"][:, :], tx["z"][:, :], tx["b"][:, :], ALU.add).then_inc(S("tx_v"), 1)
            v.wait_ge(S("tx_pe"), 11)
            v.tensor_copy(tx["zT"][:, :], T[0:D, 0:P]).then_inc(S("tx_v"), 1)
            v.wait_ge(S("tx_pe"), 12)
            v.tensor_tensor(tx["o"][:, :], T[:, 128:192], tx["ob"][:, :], ALU.add).then_inc(S("txt_done"), 1)
            v.wait_ge(S("embed_out"), B)
            v.wait_ge(S("txt_put"), 16 * B)
            v.sem_inc(S("embed_done"), 1)
            attn_v(v)
            deep_prep_v(v)
            moe_v(v, "m", 4)
            ret_v(v)
            moe_v(v, "x", 8)

        @block.scalar
        def _(s):
            s.wait_ge(S("v_set"), 3)
            s.wait_ge(S("bn_ready"), 1)

            def conv(b):
                for n in range(8):
                    s.wait_ge(S("conv_ready"), 8 * b + n + 1)
                    if b and n == 0:
                        s.wait_ge(S("wd_mm"), 2 * b)
                    s.activation(yact[0:16, 512 * n:512 * n + 512], ps[0:16, 4 + n % 2, :], ACT.Relu, bias=bnv[:, 8:9], scale=bnv[:, 7:8]).then_inc(S("y_ready"), 1)
                if b >= 2:
                    s.wait_ge(S("rows_used_v"), b - 1)
                    s.wait_ge(S("rows_used_p"), b - 1)
                for half in range(2):
                    s.wait_ge(S("wd_mm"), 2 * b + half + 1)
                    s.activation(wdyn[:, b % 2, :, 32 * half:32 * half + 32], ps[:, 6, 0:288].rearrange("p (w k) -> p k w", k=9), ACT.Copy).then_inc(S("wd_ready"), 1)

            def store(b):
                s.wait_ge(S("term_used"), 5 * b + 5)
                s.activation(hid[:, b, 0:NT - 1, :], ps[:, 0:4, :].rearrange("p a (c w) -> p (a c) w", w=WW), ACT.Copy).then_inc(S("embed_out"), 1)

            conv(0)
            for b in range(B):
                if b + 1 < B:
                    conv(b + 1)
                store(b)
            for r in range(3):
                s.wait_ge(S("tx_v"), 4 + 4 * r)
                s.activation(tx["s"][:, :], tx["s"][:, :], ACT.Exp, accum_out=tx["m"][:, 1:2]).then_inc(S("tx_e"), 1)
            attn_s(s)
            moe_s(s, "m", 4)
            ret_s(s)
            moe_s(s, "x", 8)

        @block.gpsimd
        def _(p):
            p.memset(ident[:, :], 0.0).then_inc(S("p_set"), 1)
            p.memset(causal[:, :], 1.0).then_inc(S("p_set"), 1)
            p.wait_ge(S("p_set"), 2)
            p.affine_select(out=ident[:, :], in_=ident[:, :], compare_op=ALU.not_equal, fill=1.0, base=0, pattern=[[-1, P]],
                            channel_multiplier=1).then_inc(S("p_set"), 1)
            p.affine_select(out=causal[:, :], in_=causal[:, :], compare_op=ALU.is_ge, fill=0.0, base=0, pattern=[[1, P]],
                            channel_multiplier=-1).then_inc(S("p_set"), 1)
            p.wait_ge(S("p_set"), 4)
            p.sem_inc(const_ready, 1)
            p.wait_ge(S("bn_var"), 1)
            p.tensor_tensor(bnv[:, 6:7], bnv[:, 5:6], bnv[:, 9:10], ALU.pow).then_inc(S("bn_rs"), 1)
            p.wait_ge(S("idc_ready"), 1)
            for n, k in (("a", "A"), ("c", "C")):
                p.indirect_dma_start(out=tx[n][:, :], out_offset=None, in_=A["L0_txt_%s_w" % k],
                                     in_offset=bass.IndirectOffsetOnAxis(ap=idc[:, 0:1], axis=0)).then_inc(S("gath_in"), 16)
            link = chain(p, "p_emb", 0, 0)

            def tap(buf, u, i, j):
                return p.tensor_tensor(buf[:, :, :], rows[:, u, i, :, j:j + WW], wdyn[:, u, 3 * i + j, :].unsqueeze(1).to_broadcast([P, CP, WW]), ALU.mult)

            for b in range(B):
                u = b % 2
                p.wait_ge(S("rows_in%d" % u), 16 * 6 * (b // 2 + 1))
                p.wait_ge(S("wd_ready"), 2 * b + 2)
                if b:
                    p.wait_ge(S("term_used"), 5 * b)
                link(tap(pD, u, 0, 0))
                link(tap(pT, u, 0, 1))
                p.tensor_tensor(pD[:, :, :], pD[:, :, :], pT[:, :, :], ALU.add).then_inc(S("termD"), 1)
                tap(pE, u, 0, 2).then_inc(S("termE"), 1)
                p.wait_ge(S("termD"), b + 1)
                p.wait_ge(S("termE"), b + 1)
                p.sem_inc(S("rows_used_p"), 1)
            p.wait_ge(S("tx_v"), 14)
            p.tensor_tensor(tx["m"][:, 5:6], tx["m"][:, 4:5], nhalf[:, 0:1], ALU.pow).then_inc(S("tx_rs"), 1)
            attn_p(p)
            moe_p(p, "m", 4)
            ret_p(p)
            moe_p(p, "x", 8)
            p.wait_ge(S("xh_added"), NG)
            p.sem_inc(S("stage_done"), 1)

def rotary_tables():
    f = np.float32
    j = np.arange(0, D, 2, dtype=f)
    inv = (f(1.0) / f(10000.0) ** (j / f(D))).astype(f)
    pos = np.arange(NT * P, dtype=f)
    ang = (pos[:, None] * inv[None, :]).astype(f)
    s, c = np.sin(ang), np.cos(ang)
    base = ((j + f(0.4 * D)) / f(1.4 * D)).astype(f)
    scale = (base[None, :] ** (pos[:, None] / f(512.0))).astype(f)
    local = (np.arange(NT * P) % P)[:, None]
    dq, dk = GAMMA ** local, GAMMA ** (-local.astype(np.float64))
    out = np.zeros((NT * P, 2, 2 * D), f)
    for n, (w, m) in enumerate(((scale, dq), (1.0 / scale, dk))):
        cw, sw = (c * w * m).astype(f), (s * w * m).astype(f)
        out[:, 0, D * n:D * n + D] = np.concatenate([cw, cw], 1)
        out[:, 1, D * n:D * n + D] = np.concatenate([-sw, sw], 1)
    t = out.reshape(NG, TG, P, 2, 2 * D).transpose(0, 2, 1, 3, 4)
    return np.ascontiguousarray(t.reshape(NG, P, 2 * TG, 2 * D))


_INS = ['x', 'x_txt', 'L0_tok_conv1_w', 'L0_tok_conv1_b', 'L0_tok_bn_gamma', 'L0_tok_bn_beta', 'L0_tok_bn_mean', 'L0_tok_bn_var',
        'L0_tok_conv2_w', 'L0_tok_conv2_b', 'L0_txt_A_w', 'L0_txt_C_w', 'L0_txt_U_w', 'L0_txt_ln_g', 'L0_txt_ln_b', 'L0_txt_W', 'L0_txt_b',
        'L0_attn_gamma', 'L0_attn_beta', 'L0_attn_Wq', 'L0_attn_Wk', 'L0_attn_Wv', 'L0_attn_Wg', 'L0_attn_bg', 'L0_attn_Wo', 'L0_attn_bo',
        'L0_ffn_router_w', 'L0_ffn_w1', 'L0_ffn_b1', 'L0_ffn_w2', 'L0_ffn_b2', 'L1_ffn_Wg', 'L1_ffn_bg', 'L1_ffn_bias', 'L1_ffn_W1',
        'L1_ffn_b1', 'L1_ffn_W2', 'L1_ffn_b2']


def kernel(**inputs):
    import numpy as _np
    import concourse.bacc as _bacc
    from concourse import mybir as _mybir
    from concourse.bass_utils import run_bass_kernel_spmd as _run

    nc = _bacc.Bacc("TRN2", target_bir_lowering=False, num_devices=1)
    data = {k: _np.ascontiguousarray(inputs[k]) for k in _INS}
    x = data["x"].reshape(B, CP, 2, HH, WW)
    xr = _np.zeros((B, 2, HH + 2, CP, WW + 2), x.dtype)
    xr[:, :, 1:-1, :, 1:-1] = x.transpose(0, 2, 3, 1, 4)
    data["x_rows"] = xr
    wq, wk, wv = (_np.asarray(inputs["L1_attn_W_" + n]) for n in "QKV")
    ev, od = _np.arange(0, D, 2), _np.arange(1, D, 2)
    eo, oe = _np.concatenate([ev, od]), _np.concatenate([od, ev])
    data["w_qk"] = _np.ascontiguousarray(_np.concatenate([wq[:, eo], wk[:, eo], wq[:, oe], wk[:, oe], wv], 1))
    data["tables"] = rotary_tables()
    for name, v in (("conv1_wT", data["L0_tok_conv1_w"].T), ("conv2_wT", data["L0_tok_conv2_w"].T), ("txt_WT", data["L0_txt_W"].T),
                    ("router_wT", data["L0_ffn_router_w"].T), ("ffn0_b1T", data["L0_ffn_b1"].reshape(E // 2, P).T),
                    ("ffn1_b1T", data["L1_ffn_b1"].T), ("bgT", data["L0_attn_bg"].reshape(2, P).T)):
        data[name] = _np.ascontiguousarray(v)
    arrays, args = {}, {}
    for name, v in data.items():
        arrays[f"in_{name}_dram"] = v
        args[name] = nc.dram_tensor(f"in_{name}_dram", v.shape, _mybir.dt.from_np(v.dtype), kind="ExternalInput").ap()
    res = nc.dram_tensor("out_0_dram", (B, L, D), F32, kind="ExternalOutput").ap()
    build(nc, args, res)
    r = _run(nc, [arrays], core_ids=[0])
    return r.results[0]["out_0_dram"]
```

```python
from contextlib import ExitStack
import numpy as np
import concourse.bass as bass
from concourse import mybir

F32 = mybir.dt.float32
F32R = mybir.dt.float32r
I32 = mybir.dt.int32
U32 = mybir.dt.uint32
ALU = mybir.AluOpType
ACT = mybir.ActivationFunctionType
X = mybir.AxisListType.X

P = 128
B, C, HH, WW = 4, 64, 64, 64
D = 64
TXT = 32
L = C * HH + TXT
NT = (L + P - 1) // P
TG = 3
NG = NT // TG
GT = TG * B
GW = GT * D
SETS = 3
EPS = 1e-5
HEADS, HC = 8, 32
E = 8
GAMMA = 0.96875
CT = 32 * SETS
LAG = 5
CK, KK = 16, 9
WQ = 1024
HS = 6
CP = C // 2


def steps(eng, step):
    step(0, 0, 1, 2)
    with eng.Fori(0, (NG - 3) // 2) as i:
        for u in (0, 1):
            step(2 * i + 1 + u, 1 - u, 2 * i + 2 + u, 2 * i + 3 + u)
    step(NG - 2, 1, NG - 1, None)
    step(NG - 1, 0, None, None)


def late(g, n):
    return not isinstance(g, int) or g >= n


def build(nc, a, out, wd_dram):
    with ExitStack() as ctx:
        top = ctx

        def sb(name, shape, dt=F32, where=None):
            return (where or ctx).enter_context(nc.sbuf_tensor(name, shape, dt))

        def sem(name):
            return ctx.enter_context(nc.semaphore(name))

        hid = sb("hid", [P, B, NT, D])
        ident = sb("ident", [P, P])
        ones = sb("ones", [P, P])
        causal = sb("causal", [P, P])
        desc = sb("desc", [P, E])
        nhalf = sb("nhalf", [P, GT])
        gam = sb("gam", [P, D])
        bet = sb("bet", [P, D])
        bo_row = sb("bo_row", [P, D])
        lgb = sb("lgb", [P, 2 * E])
        lgb2 = sb("lgb2", [P, E])
        ln_sum = sb("ln_sum", [P, 2, GT])
        ln_mean = sb("ln_mean", [P, 2, GT])
        ln_var = sb("ln_var", [P, 2, GT])
        ln_ve = sb("ln_ve", [P, 2, GT])
        ln_rs = sb("ln_rs", [P, 2, GT])
        cen = sb("cen", [P, 2, GW])
        sq = sb("sq", [P, 2, GW])
        zz = sb("zz", [P, 2, GW])

        sems = {}

        def S(name):
            if name not in sems:
                sems[name] = sem(name)
            return sems[name]

        const_ready = S("const_ready")

        def grp(g):
            return hid[:, :, bass.ds(g * TG, TG) if not isinstance(g, int) else slice(g * TG, g * TG + TG), :]

        def four(x):
            return x.rearrange("p (b t d) -> p b t d", b=B, t=TG)

        def three(x):
            return x.rearrange("p (b t) -> p b t", b=B)

        def bc(x, n):
            return x.unsqueeze(3).to_broadcast([P, B, TG, n])

        embed = ExitStack()
        XW = WW + 2
        with embed:
            rows = sb("rows", [P, 2, 3, CP, XW], F32, embed)
            xch = sb("xch", [P, HH * WW], F32, embed)
            yact = sb("yact", [2 * CK + 1, HH * WW], F32, embed)
            wdT = sb("wdT", [2 * KK, 2, WQ], F32, embed)
            wdyn = sb("wdyn", [P, 2, KK, WW], F32, embed)
            dA, dC, dT, pD, pE, pT = [sb(n, [P, CP, WW], F32, embed) for n in ("dA", "dC", "dT", "pD", "pE", "pT")]
            w1c = sb("w1c", [P, 2 * CK], F32, embed)
            w2c = sb("w2c", [2 * CK + 1, 2 * KK], F32, embed)
            bnv = sb("bnv", [2 * CK, 10], F32, embed)
            tx = {n: sb("tx_" + n, s, F32, embed) for n, s in dict(
                a=[P, D], c=[P, D], u=[P, D], uT=[D, P], aT=[D, P], s=[P, TXT], p=[P, TXT], m=[P, 8],
                g=[P, D], b=[P, D], wT=[D, D], ob=[P, D], z=[P, D], zT=[D, P], o=[P, D], q=[P, D]).items()}
            ids = sb("tx_ids", [P, 1], I32, embed)
            idc = sb("tx_idc", [P, 2], U32, embed)
        wr = sb("wr", [P, 2, E], F32)
        wrS = sb("wrS", [P, 2, 2 * E], F32R)
        fw1 = sb("fw1", [P, E * D], F32)
        fw1H = sb("fw1H", [P, E * D], F32R)
        fw1L = sb("fw1L", [P, E * D], F32R)
        fb1 = sb("fb1", [P, 4], F32)
        fw2 = sb("fw2", [P, 4, D], F32)
        fw2S = sb("fw2S", [P, 4, 2 * D], F32R)
        gw1 = sb("gw1", [P, E * P], F32)
        gw1H = sb("gw1H", [P, E * P], F32R)
        gw1L = sb("gw1L", [P, E * P], F32R)
        gb1 = sb("gb1", [P, E], F32)
        gw2 = sb("gw2", [P, E, D], F32)
        gw2S = sb("gw2S", [P, E, 2 * D], F32R)
        bias2 = sb("bias2", [CT, 2, SETS, D], F32)
        bias2S = sb("bias2S", [CT, 2, SETS, 2 * D], F32R)
        pick = sb("pick", [CT, SETS, E], F32)
        pickM = sb("pickM", [CT, SETS * E * D], F32R)
        fold = sb("fold", [P, D], F32)
        NQ = 5 * D
        wqk = sb("wqk", [P, NQ], F32)
        wqkH = sb("wqkH", [P, NQ], F32R)
        wqkL = sb("wqkL", [P, NQ], F32R)
        attn = ExitStack()
        with attn:
            zs1 = sb("zs1", [P, 2, GW], F32, attn)
            ztH = sb("ztH", [P, 2, NT * P], F32R, attn)
            ztL = sb("ztL", [P, 2, NT * P], F32R, attn)
            wk2 = sb("wk2", [P, 256], F32, attn)
            wq2 = sb("wq2", [P, 256], F32, attn)
            wv2 = sb("wv2", [P, 256], F32, attn)
            wgp = sb("wgp", [P, 2, 256], F32, attn)
            wgH = sb("wgH", [P, 2, 256], F32R, attn)
            wgL = sb("wgL", [P, 2, 256], F32R, attn)
            wo = sb("wo", [P, 2, D], F32, attn)
            bgc = sb("bgc", [P, 2], F32, attn)
            gramS = sb("gramS", [P, 2, 256], F32, attn)
            prodX = sb("prodX", [P, 8, 256], F32, attn)
            part = sb("part", [P, 64], F32, attn)
            at = sb("at", [P, P], F32, attn)
            at2 = sb("at2", [P, P], F32, attn)
            atm = sb("atm", [P, 4 * HEADS], F32, attn)
            wmH = sb("wmH", [P, B, 2, 256], F32R, attn)
            wmL = sb("wmL", [P, B, 2, 256], F32R, attn)
            sig = sb("sig", [P, 2, TG * P], F32, attn)
        wmix = prodX[:, :, :].rearrange("p (s r) c -> p s r c", s=B)

        def gated(slot, mc, t0, n):
            return zs1[:, slot, TG * P * mc + t0:TG * P * mc + t0 + n]

        deep = ExitStack()
        with deep:
            zst = sb("zst", [P, 2, GT, 2, D], F32R, deep)
            zt = sb("zt", [P, 2, GT * P], F32R, deep)
            lg = sb("lg", [P, 12, GT * E], F32, deep)
            rt = sb("rt", [P, 8, GT], F32, deep)
            comb = sb("comb", [P, GT * E], F32, deep)
            pickX = sb("pickX", [CT, SETS * E * P], F32R, deep)
            tabc = sb("tabc", [P, 2, 2 * TG, 2 * D], F32, deep)
            combS = sb("combS", [P, 4, SETS, 32], F32R, deep)
            combT = sb("combT", [CT, 2, 512], F32R, deep)
            experts = ExitStack()
            with experts:
                hact = sb("hact", [P, 4, 512], F32, experts)
                hc = sb("hc", [P, HS, 512], F32, experts)
                hcH = sb("hcH", [P, HS, 512], F32R, experts)
                hcL = sb("hcL", [P, HS, 512], F32R, experts)
                obuf = sb("obuf", [P, 2, 512], F32, experts)
            retain = ExitStack()
            with retain:
                rA = sb("rA", [P, 2, B, D], F32, retain)
                rB = sb("rB", [P, 2, B, D], F32, retain)
                rot = sb("rot", [P, TG, 2, B, D], F32, retain)
                val = sb("val", [P, TG, B, D], F32, retain)
                qkT = sb("qkT", [P, TG, 4, P], F32, retain)
                pmat = sb("pmat", [P, TG, B, P], F32, retain)
                state = sb("state", [P, TG, B, D], F32, retain)
                stt = sb("stt", [P, 2, D], F32, retain)

        ps = ctx.enter_context(nc.psum_tensor("ps", [P, 8, 512], F32))

        block = ctx.enter_context(nc.Block())
        A = a

        def gram_pe(pe):
            pe.wait_ge(S("txt_put"), 16 * B)

            def back(g, par):
                z = zs1[:, par].rearrange("p (t b d) -> p t b d", b=B, t=TG)
                pe.wait_ge(S("z1_ready"), g + 1)
                if late(g, 2):
                    pe.wait_ge(S("zt_split"), g - 1)
                for pair in range(2):
                    for t in range(TG):
                        mm = pe.transpose(ps[:, 2 + 2 * par + pair, P * t:P * t + P], z[:, t, 2 * pair:2 * pair + 2, :].rearrange("p b d -> p (b d)"), ident[:, :])
                mm.then_inc(S("z1_turned"), 1)
                for t in range(TG):
                    rows_ = TXT if isinstance(g, int) and g == NG - 1 and t == TG - 1 else P
                    for m in range(2):
                        first = isinstance(g, int) and g == 0 and t == 0
                        last = isinstance(g, int) and g == NG - 1 and t == TG - 1
                        mm = pe.matmul(ps[:, m, 0:256], z[0:rows_, t, 2 * m:2 * m + 2, :].rearrange("p b d -> p (b d)"), z[0:rows_, t, :, :],
                                       start=first, stop=last, skip_group_check=True)
                mm.then_inc(S("gram_mm"), 1)

            steps(pe, lambda g, par, ahead, far: back(g, par))
            pe.wait_ge(S("gram_out"), 1)
            pe.wait_ge(S("attw_in"), 16 * 10)
            for m in range(2):
                for t in range(B):
                    h = 64 * (t % 2)
                    mm = pe.matmul(ps[:, 4 + 2 * m + t % 2, 256 * (t // 2):256 * (t // 2) + 256], gramS[h:h + 64, t // 2, P * m:P * m + P],
                                   wk2[h:h + 64, :], start=True, stop=True, skip_group_check=True)
            mm.then_inc(S("x_ready"), 1)
            pe.wait_ge(S("part_ready"), 1)
            for s in range(B):
                h = 64 * (s % 2)
                mm = pe.matmul(ps[:, 2 + s % 2, 32 * (s // 2):32 * (s // 2) + 32], ones[h:h + 64, :], part[h:h + 64, 32 * (s // 2):32 * (s // 2) + 32],
                               start=True, stop=True, skip_group_check=True)
            mm.then_inc(S("att_ready"), 1)
            pe.wait_ge(S("wmix_ready"), 1)

            def mix(g, par):
                for s in range(B):
                    for mc in range(2):
                        k = 2 * s + mc
                        if late(g, 1) or k >= 2:
                            pe.wait_ge(S("og_ready"), 8 * g + k - 1)
                        cs = slice(P * mc, P * mc + P)
                        tok = bass.ds(g * TG * P, TG * P) if not isinstance(g, int) else slice(g * TG * P, (g + 1) * TG * P)
                        n = 0
                        for pair in range(2):
                            for w, z in ((wmH, ztH), (wmH, ztL), (wmL, ztH)):
                                pe.matmul(ps[:, mc, 0:TG * P], w[:, s, pair, cs], z[:, pair, tok], start=(n == 0), stop=(n == 5))
                                n += 1
                        for n, (w, z) in enumerate(((wgH, ztH), (wgH, ztL), (wgL, ztH))):
                            mm = pe.matmul(ps[:, 2 + mc, 0:TG * P], w[:, s % 2, cs], z[:, s // 2, tok], start=(n == 0), stop=(n == 2))
                        mm.then_inc(S("mix_ready"), 1)
                    if late(g, 1) or s >= 1:
                        project(4 * g + s - 1, (s - 1) % 2, (s - 1) % 2)

            def project(k, slot, bank):
                pe.wait_ge(S("og_ready"), 2 * k + 2)
                if not isinstance(k, int) or k >= 2:
                    pe.wait_ge(S("att_added"), k - 1)
                for t in range(TG):
                    for mc in range(2):
                        mm = pe.matmul(ps[:, 4 + bank, D * t:D * t + D], gated(slot, mc, P * t, P), wo[:, mc, :],
                                       start=(mc == 0), stop=(mc == 1), skip_group_check=True)
                mm.then_inc(S("proj_ready"), 1)

            mix(0, 0)
            with pe.Fori(1, NG) as g:
                mix(g, 0)
            project(4 * NG - 1, 1, 1)

        def ln_stats(v, ph, g, par):
            for _ in ln_stats_parts(v, ph, g, par):
                pass

        def ln_stats_parts(v, ph, g, par):
            link = chain(v, ph + "ln_v", g, 3)
            link(v.tensor_reduce(three(ln_sum[:, par]), grp(g), X, ALU.add))
            yield
            link(v.tensor_scalar(ln_mean[:, par], ln_sum[:, par], 1.0 / D, None, ALU.mult))
            v.tensor_tensor(four(cen[:, par]), grp(g), bc(three(ln_mean[:, par]), D), ALU.subtract).then_inc(S(ph + "cen_ready"), 1)

        def ln_var_v(v, ph, g, par, k1, k0):
            v.wait_ge(S(ph + "sq_ready"), g + 1)
            link = chain(v, ph + "ln_v", g, 3, start=2)
            link(v.tensor_reduce(three(ln_var[:, par]), four(sq[:, par]), X, ALU.add))
            v.tensor_scalar(ln_ve[:, par], ln_var[:, par], k1, k0, ALU.mult, ALU.add).then_inc(S(ph + "ve_ready"), 1)

        def ln_norm(v, ph, g, par):
            v.wait_ge(S(ph + "rs_ready"), g + 1)
            v.tensor_tensor(four(zz[:, par]), four(cen[:, par]), bc(three(ln_rs[:, par]), D), ALU.mult).then_inc(S(ph + "z_ready"), 1)

        def next_norms_v(v, ph):
            for g in (0, 1):
                ln_stats(v, ph, g, g)
                yield
                ln_var_v(v, ph, g, g, 1.0 / D, EPS)
                yield
            ln_norm(v, ph, 0, 0)
            yield
            ln_norm(v, ph, 1, 1)
            yield

        def split_low(v, ph, g, par):
            v.wait_ge(S(ph + "zh_ready"), g + 1)
            v.tensor_tensor(zst[:, par, :, 1, :], zz[:, par].rearrange("p (j d) -> p j d", d=D), zst[:, par, :, 0, :].bitcast(F32),
                            ALU.subtract).then_inc(S(ph + "zl_ready"), 1)

        def chain(eng, name, g, per, start=0):
            k = [start]

            def link(ins):
                k[0] += 1
                ins.then_inc(S(name), 1)
                eng.wait_ge(S(name), g * per + k[0])
            return link

        def ln_scalar(s, ph, g, par):
            s.wait_ge(S(ph + "cen_ready"), g + 1)
            s.activation(sq[:, par], cen[:, par], ACT.Square).then_inc(S(ph + "sq_ready"), 1)

        def ln_pool(p, ph, g, par):
            p.wait_ge(S(ph + "ve_ready"), g + 1)
            p.tensor_tensor(ln_rs[:, par], ln_ve[:, par], nhalf[:, :], ALU.pow).then_inc(S(ph + "rs_ready"), 1)

        def own(ph, k):
            return ph == "x" and k % 4 == 3

        def others(ph, g, k):
            return g * 18 + k - k // 4 if ph == "x" else g * 12 + k

        def set_at(CH, k, after):
            q, r = divmod(k - after - LAG + 1, CH)
            if r:
                return None
            return (0, q - 1) if q >= 1 else (1, q - 1 + SETS)

        def moe_pe(pe, ph, CH):
            lay = 0 if ph == "m" else 1
            K, U = SETS * CH, CH // 4
            w1H, w1L, w2 = (fw1H, fw1L, fw2S) if lay == 0 else (gw1H, gw1L, gw2S)
            pick_ = pickM if lay == 0 else pickX
            pe.wait_ge(S("deep_ready"), 1)

            def turn(g, par, q):
                if q == 0:
                    pe.wait_ge(S(ph + "zl_ready"), g + 1)
                if late(g, 1) or q >= 1:
                    pe.wait_ge(S(ph + "zt_ready"), SETS * g + q)
                for j in range(4):
                    mm = pe.transpose(ps[:, 6, P * j:P * j + P], zst[:, par, 4 * q + j].rearrange("p s d -> p (s d)").bitcast(F32), ident[:, :])
                mm.then_inc(S(ph + "tp_ready"), 1)

            def logits(g, par):
                pe.wait_ge(S(ph + "zt_ready"), SETS * g + SETS)
                if late(g, 1):
                    pe.wait_ge(S(ph + "ct_ready"), g)
                for j in range(GT):
                    mm = pe.matmul(ps[:, 7, 2 * E * j:2 * E * j + 2 * E], zt[:, par, P * j:P * j + P], wrS[:, lay, :], start=True, stop=True,
                                   skip_group_check=True)
                mm.then_inc(S(ph + "lg_ready"), 1)

            def turn_comb(g):
                pe.wait_ge(S(ph + "comb_ready"), g + 1)
                for j in range(4):
                    mm = pe.transpose(ps[0:CT, 7, P * j:P * j + P], combS[:, j].rearrange("p q c -> p (q c)").bitcast(F32), ident[:, :])
                mm.then_inc(S(ph + "ct_mm"), 1)

            def hidden(g, par, k):
                q, c = divmod(k, CH)
                if late(g, 1) or k >= 2:
                    pe.wait_ge(S(ph + "h_act"), K * g + k - 1)
                for n, w in enumerate((w1H, w1L)):
                    mm = pe.matmul(ps[:, k % 2, :], w[:, P * c:P * c + P], zt[:, par, 512 * q:512 * q + 512], start=(n == 0), stop=(n == 1))
                mm.then_inc(S(ph + "h_mm"), 1)

            def spread(g, par, k):
                if k == 0:
                    pe.wait_ge(S(ph + "ct_ready"), g + 1)
                if late(g, 1) or k >= 2:
                    pe.wait_ge(S(ph + "hc_ready"), K * g + k - 1)
                pe.matmul(ps[:, 2 + k % 2, :], pick_[:, P * k:P * k + P], combT[:, par, :], start=True, stop=True).then_inc(S(ph + "c_mm"), 1)

            def outputs(g, par, k):
                q, c = divmod(k, CH)
                y = ps[:, 4 + (par + q) % 2, :]
                if own(ph, k):
                    pe.wait_ge(S(ph + "low_v"), 6 * g + k // 4 + 1)
                else:
                    pe.wait_ge(S(ph + "low_p"), others(ph, g, k + 1))
                if c == 0:
                    if late(g, 1) or q >= 2:
                        pe.wait_ge(S(ph + "h_added"), SETS * g + q - 1)
                    pe.matmul(y, bias2S[:, lay, q, :], combT[:, par, :], start=True, stop=False)
                for h in (hcH, hcL):
                    mm = pe.matmul(y, w2[:, c, :], h[:, k % HS, :], start=False, stop=(c == CH - 1 and h is hcL))
                mm.then_inc(S(ph + "y_mm"), 1)

            def back(g, par, q):
                pe.wait_ge(S(ph + "ob_ready"), SETS * g + q + 1)
                for j in range(4):
                    mm = pe.matmul(ps[:, 4 + (par + q) % 2, D * j:D * j + D], obuf[:, (par + q) % 2, P * j:P * j + P], fold[:, :], start=True, stop=True,
                                   skip_group_check=True)
                mm.then_inc(S(ph + "y_back"), 1)

            def step(g, par, ahead, far):
                for k in range(K):
                    hidden(g, par, k)
                    if k >= LAG:
                        outputs(g, par, k - LAG)
                    elif late(g, 1):
                        outputs(g - 1, 1 - par, K + k - LAG)
                    spread(g, par, k)
                    done = set_at(CH, k, 2)
                    if done and (done[0] == 0 or late(g, 1)):
                        back(g - done[0], par if done[0] == 0 else 1 - par, done[1])
                    if ahead is not None:
                        if k in (0, U, 2 * U):
                            turn(ahead, 1 - par, k // U)
                        if k == 3 * U:
                            logits(ahead, 1 - par)
                        if k == 10 * U:
                            turn_comb(ahead)

            if ph == "x":
                pe.wait_ge(S("pickx_ready"), 1)
            for q in range(SETS):
                turn(0, 0, q)
            logits(0, 0)
            turn_comb(0)
            steps(pe, step)
            for k in range(K - LAG, K):
                outputs(NG - 1, 0, k)
                if set_at(CH, k + LAG, 2) == (0, 1):
                    back(NG - 1, 0, 1)
            back(NG - 1, 0, 2)

        def ret_pe(pe):
            def turn(g, par, q):
                if q == 0:
                    pe.wait_ge(S("rzl_ready"), g + 1)
                if late(g, 1) or q >= 1:
                    pe.wait_ge(S("rzt_ready"), SETS * g + q)
                for j in range(4):
                    mm = pe.transpose(ps[:, 7, P * j:P * j + P], zst[:, par, 4 * q + j].rearrange("p s d -> p (s d)").bitcast(F32), ident[:, :])
                mm.then_inc(S("rtp_ready"), 1)

            def project(g, par, t):
                k = TG * g + t
                pe.wait_ge(S("rzt_ready"), SETS * g + SETS)
                if late(g, 1) or t >= 1:
                    pe.wait_ge(S("rope_read"), k)
                    pe.wait_ge(S("val_ready"), k)
                for b in range(B):
                    zb = zt[:, par, P * (TG * b + t):P * (TG * b + t) + P]
                    for dst, c in ((ps[:, b // 2, 256 * (b % 2):256 * (b % 2) + 256], slice(0, 4 * D)), (ps[:, 2, D * b:D * b + D], slice(4 * D, NQ))):
                        for n, w in enumerate((wqkH, wqkL)):
                            mm = pe.matmul(dst, zb, w[:, c], start=(n == 0), stop=(n == 1), skip_group_check=True)
                mm.then_inc(S("qkv_mm"), 1)

            def turn_qk(g, t):
                k = TG * g + t
                pe.wait_ge(S("rot_ready"), k + 1)
                if late(g, 1) or t >= 1:
                    pe.wait_ge(S("qkT_ready"), k)
                for pair in range(2):
                    for n in range(2):
                        mm = pe.transpose(ps[:, 4, P * (2 * pair + n):P * (2 * pair + n) + P], rot[:, t, n, 2 * pair:2 * pair + 2, :].rearrange("p b d -> p (b d)"), ident[:, :])
                mm.then_inc(S("qkT_mm"), 1)

            def scores(g, t):
                k = TG * g + t
                pe.wait_ge(S("qkT_ready"), k + 1)
                if late(g, 1) or t >= 1:
                    pe.wait_ge(S("pmat_ready"), k)
                for b in (0, 2, 1, 3):
                    h = slice(64 * (b % 2), 64 * (b % 2) + 64)
                    mm = pe.matmul(ps[:, 5 + b % 2, P * (b // 2):P * (b // 2) + P], qkT[h, t, 2 * (b // 2) + 1, :], qkT[h, t, 2 * (b // 2), :], start=True, stop=True,
                                   skip_group_check=True)
                mm.then_inc(S("score_mm"), 1)

            def outputs(k, t):
                pe.wait_ge(S("state_ready"), k + 1)
                pe.wait_ge(S("pmat_ready"), k + 1)
                for b in range(B):
                    pe.matmul(ps[:, 3, D * b:D * b + D], qkT[:, t, 2 * (b // 2), :], state[:, t, b, :], start=True, stop=False,
                              skip_group_check=True)
                    mm = pe.matmul(ps[:, 3, D * b:D * b + D], pmat[:, t, b, :], val[:, t, b, :], start=False, stop=True,
                                   skip_group_check=True)
                mm.then_inc(S("ret_mm"), 1)

            def key_values(g, t):
                k = TG * g + t
                pe.wait_ge(S("val_ready"), k + 1)
                for pair in range(2):
                    mm = pe.matmul(ps[:, 3, 256 + P * pair:256 + P * pair + P], rot[:, t, 1, 2 * pair:2 * pair + 2, :].rearrange("p b d -> p (b d)"), val[:, t, 2 * pair:2 * pair + 2, :],
                                   start=True, stop=True, skip_group_check=True)
                mm.then_inc(S("kv_mm"), 1)

            def step(g, par, ahead, far):
                for t in range(TG):
                    up = t == 1 and ahead is not None
                    if up:
                        turn(ahead, 1 - par, 0)
                    scores(g, t)
                    if up:
                        turn(ahead, 1 - par, 1)
                    if late(g, 1) or t >= 1:
                        outputs(TG * g + t - 1, (t - 1) % TG)
                    if up:
                        turn(ahead, 1 - par, 2)
                    key_values(g, t)
                    if t < TG - 1 or ahead is not None:
                        turn_qk(g if t < TG - 1 else ahead, (t + 1) % TG)
                    if t == 0:
                        project(g, par, 2)
                    elif ahead is not None:
                        project(ahead, 1 - par, t - 1)

            pe.wait_ge(S("state_zero"), 1)
            for q in range(SETS):
                turn(0, 0, q)
            project(0, 0, 0)
            turn_qk(0, 0)
            project(0, 0, 1)
            steps(pe, step)
            outputs(TG * NG - 1, TG - 1)

        def attn_v(v, once):
            def low(g, par):
                v.wait_ge(S("z1h_ready"), g + 1)
                tok = bass.ds(g * TG * P, TG * P) if not isinstance(g, int) else slice(g * TG * P, (g + 1) * TG * P)
                for pair in range(2):
                    ins = v.tensor_tensor(ztL[:, pair, tok], ps[:, 2 + 2 * par + pair, 0:TG * P], ztH[:, pair, tok].bitcast(F32), ALU.subtract)
                ins.then_inc(S("zt_split"), 1)

            def var(g, par):
                ln_var_v(v, "a", g, par, (1.0 + EPS) / D, EPS * EPS)

            def step(g, par, ahead, far):
                if ahead is not None:
                    if late(g, 1):
                        v.wait_ge(S("z1_ready"), g)
                    ln_norm(v, "a", ahead, 1 - par)
                if far is not None:
                    ln_stats(v, "a", far, par)
                if far is not None:
                    var(far, par)
                low(g, par)

            ln_stats(v, "a", 0, 0)
            var(0, 0)
            ln_stats(v, "a", 1, 1)
            ln_norm(v, "a", 0, 0)
            var(1, 1)
            steps(v, step)
            v.wait_ge(S("gram_mm"), NG)
            v.tensor_copy(gramS[:, :, :], ps[:, 0:2, 0:256]).then_inc(S("gram_out"), 1)
            v.wait_ge(S("attw_in"), 16 * 10)
            link = once
            link(v.tensor_scalar(wgH[:, :, :], wgp[:, :, :], 1.0, None, ALU.mult))
            link(v.tensor_tensor(wgL[:, :, :], wgp[:, :, :], wgH[:, :, :].bitcast(F32), ALU.subtract))
            v.wait_ge(S("x_ready"), 1)
            for h in range(2):
                link(v.tensor_tensor(prodX[:, 4 * h:4 * h + 4, :].rearrange("p (s r) c -> p r s c", r=2), ps[:, 4 + 2 * h:6 + 2 * h, :].rearrange("p r (s c) -> p r s c", s=2),
                                     wq2[:, :].unsqueeze(1).unsqueeze(1).to_broadcast([P, 2, 2, 256]), ALU.mult))
            v.tensor_reduce(part[:, :], prodX[:, :, :].rearrange("p m (h c) -> p (m h) c", c=HC), X, ALU.add).then_inc(S("part_ready"), 1)
            v.wait_ge(S("att_ready"), 1)
            SC = 1.0 / np.sqrt(HC) / np.sqrt(L)
            a4 = at[:, :].rearrange("p (s t h) -> p s t h", s=B, t=B)
            b4 = at2[:, :].rearrange("p (s t h) -> p s t h", s=B, t=B)
            m3 = atm[:, :].rearrange("p (s h) -> p s h", s=B)
            link(v.tensor_scalar(at[:, :].rearrange("p (q r x) -> p r q x", q=2, r=2), ps[:, 2:4, 0:64].rearrange("p r (q x) -> p r q x", q=2), float(SC), None, ALU.mult))
            link(v.tensor_reduce(m3, a4.rearrange("p s t h -> p s h t"), X, ALU.max))
            v.tensor_tensor(a4, a4, m3.unsqueeze(2).to_broadcast([P, B, B, HEADS]), ALU.subtract).then_inc(S("att_sub"), 1)
            v.wait_ge(S("att_exp"), 1)
            link(v.tensor_reduce(m3, b4.rearrange("p s t h -> p s h t"), X, ALU.add))
            link(v.reciprocal(atm[:, :], atm[:, :]))
            link(v.tensor_tensor(b4, b4, m3.unsqueeze(2).to_broadcast([P, B, B, HEADS]), ALU.mult))
            for s in range(B):
                for pair in range(2):
                    for h in range(2):
                        r = slice(64 * h, 64 * h + 64)
                        ins = v.tensor_tensor(wmix[r, s, pair, :].rearrange("p (h c) -> p h c", c=HC), wv2[r, :].rearrange("p (h c) -> p h c", c=HC),
                                              b4[r, s, 2 * pair + h, :].unsqueeze(2).to_broadcast([64, HEADS, HC]), ALU.mult)
            link(ins)
            link(v.tensor_scalar(wmH[:, :, :, :], wmix[:, :, :, :], 1.0, None, ALU.mult))
            v.tensor_tensor(wmL[:, :, :, :], wmix[:, :, :, :], wmH[:, :, :, :].bitcast(F32), ALU.subtract).then_inc(S("wmix_ready"), 1)
            v.wait_ge(S("bo_added"), 1)

            def gate(g, between=()):
                for s in range(B):
                    for mc in range(2):
                        k = 2 * s + mc
                        v.wait_ge(S("sig_ready"), 8 * g + k + 1)
                        if (late(g, 1) or s >= 2) and mc == 0:
                            v.wait_ge(S("proj_ready"), 4 * g + s - 1)
                        v.tensor_tensor(gated(s % 2, mc, 0, TG * P), sig[:, mc, :], ps[:, mc, 0:TG * P], ALU.mult).then_inc(S("og_ready"), 1)
                        if between:
                            next(between, None)
                    if late(g, 1) or s >= 1:
                        add(g if s else g - 1, (s - 1) % B, 4 * g + s - 1)

            def add(g, s, k):
                v.wait_ge(S("proj_ready"), k + 1)
                dst = hid[:, s, bass.ds(g * TG, TG) if not isinstance(g, int) else slice(g * TG, g * TG + TG), :]
                v.tensor_tensor(dst, dst, ps[:, 4 + s % 2, 0:TG * D].rearrange("p (t d) -> p t d", d=D), ALU.add).then_inc(S("att_added"), 1)

            gate(0)
            with v.Fori(1, NG - 1) as g:
                gate(g)
            v.wait_ge(S("att_added"), 4 * 2)
            gate(NG - 1, next_norms_v(v, "m"))
            add(NG - 1, B - 1, 4 * NG - 1)
            v.wait_ge(S("att_added"), 4 * NG)
            v.sem_inc(S("attn_free"), 1)

        def deep_prep_p(p, link):
            p.memset(bias2[:, :, :, :], 0.0).then_inc(S("zeroed"), 1)
            p.memset(lgb[:, E:2 * E], 0.0)
            for e in range(E):
                p.memset(desc[:, e:e + 1], float(E - e))
            p.tensor_tensor(fold[:, :], ident[:, 0:D], ident[:, D:P], ALU.add)
            rows3 = ident[0:CT, 0:CT].rearrange("p (q r) -> p q r", q=SETS)
            link(p.tensor_tensor(pick[:, :, :], rows3[:, :, 0:E], rows3[:, :, E:2 * E], ALU.add))
            p.tensor_copy(pickM[:, :].rearrange("p (x n) -> p x n", n=D), pick[:, :, :].rearrange("p q e -> p (q e)").unsqueeze(2).to_broadcast([CT, SETS * E, D]))
            p.tensor_tensor(lgb[:, 0:E], lgb[:, 0:E], lgb2[:, :], ALU.add)
            p.wait_ge(S("deepw_in"), 16 * (10 + 12 + 3 + 2))
            for src, hi, lo in ((fw1, fw1H, fw1L), (gw1, gw1H, gw1L), (wqk, wqkH, wqkL), (wr, wrS[:, :, 0:E], wrS[:, :, E:2 * E]),
                                (fw2, fw2S[:, :, 0:D], fw2S[:, :, D:2 * D]), (gw2, gw2S[:, :, 0:D], gw2S[:, :, D:2 * D]),
                                (bias2, bias2S[:, :, :, 0:D], bias2S[:, :, :, D:2 * D])):
                i = tuple(slice(None) for _ in src.shape)
                link(p.tensor_copy(hi[i], src[i]))
                ins = p.tensor_tensor(lo[i], src[i], hi[i].bitcast(F32), ALU.subtract)
            link(ins)
            p.sem_inc(S("deep_ready"), 1)

        def moe_v(v, ph, CH):
            R = lambda n: lg[:, n, :].rearrange("p (j e) -> p j e", e=E)
            bce = lambda x: x.unsqueeze(2).to_broadcast([P, GT, E])
            row = lambda x: x.unsqueeze(1).to_broadcast([P, GT, E])

            def top_two(g):
                link = chain(v, ph + "top_v", g, 13)
                v.wait_ge(S(ph + "lg_ready"), g + 1)
                src = ps[:, 7, 0:GT * 2 * E].rearrange("p (j e) -> p j e", e=2 * E)
                both = lg[:, 5:7, :].rearrange("p a x -> p (a x)").rearrange("p (j e) -> p j e", e=2 * E)
                if ph == "x":
                    link(v.tensor_tensor(both, src, lgb[:, :].unsqueeze(1).to_broadcast([P, GT, 2 * E]), ALU.add))
                else:
                    link(v.tensor_copy(both, src))
                link(v.tensor_tensor(R(0), both[:, :, 0:E], both[:, :, E:2 * E], ALU.add))
                yield
                cur = 0
                for n in range(2):
                    link(v.tensor_reduce(rt[:, n, :], R(cur), X, ALU.max))
                    yield
                    link(v.tensor_tensor(R(1), R(cur), bce(rt[:, n, :]), ALU.is_equal))
                    link(v.tensor_tensor(R(1), R(1), row(desc[:, :]), ALU.mult))
                    yield
                    link(v.tensor_reduce(rt[:, 2, :], R(1), X, ALU.max))
                    link(v.tensor_tensor(R(2 + n), R(1), bce(rt[:, 2, :]), ALU.is_equal))
                    if n == 0:
                        link(v.scalar_tensor_tensor(lg[:, 4, :], lg[:, 2, :], -1e30, lg[:, 0, :], ALU.mult, ALU.add))
                        cur = 4
                    yield
                v.tensor_tensor(rt[:, 3, :], rt[:, 0, :], rt[:, 1, :], ALU.subtract).then_inc(S(ph + "gap_ready"), 1)

            def weights(g):
                link = chain(v, ph + "wgt_v", g, 4)
                v.wait_ge(S(ph + "tanh_ready"), g + 1)
                v.tensor_scalar(rt[:, 6, :], rt[:, 4, :], -0.5, 0.5, ALU.mult, ALU.add)
                link(v.tensor_scalar(rt[:, 5, :], rt[:, 4, :], 0.5, 0.5, ALU.mult, ALU.add))
                v.tensor_tensor(R(2), R(2), bce(rt[:, 5, :]), ALU.mult)
                link(v.tensor_tensor(R(3), R(3), bce(rt[:, 6, :]), ALU.mult))
                link(v.tensor_tensor(comb[:, :], lg[:, 2, :], lg[:, 3, :], ALU.add))
                cj = comb[:, :].rearrange("p (q j e) -> p q j e", q=SETS, e=E)
                cs = combS[:, :, :, :].rearrange("p j q c -> p q j c")
                if late(g, 1):
                    v.wait_ge(S(ph + "ct_mm"), g)
                link(v.tensor_scalar(cs[:, :, :, 0:E], cj, 1.0, None, ALU.mult))
                v.tensor_tensor(cs[:, :, :, E:2 * E], cj, cs[:, :, :, 0:E].bitcast(F32), ALU.subtract).then_inc(S(ph + "comb_ready"), 1)

            K, U = SETS * CH, CH // 4

            def weigh(g, k):
                v.wait_ge(S(ph + "h_act"), K * g + k + 1)
                v.wait_ge(S(ph + "c_mm"), K * g + k + 1)
                if late(g, 1) or k >= HS:
                    v.wait_ge(S(ph + "low_p"), others(ph, g, k - HS + 1))
                ins = v.tensor_tensor(hc[:, k % HS, :], hact[:, k % 4, :], ps[:, 2 + k % 2, :], ALU.mult)
                ins.then_inc(S(ph + "hc_ready"), 1)

            def own_high(g, k):
                v.wait_ge(S(ph + "hc_ready"), K * g + k + 1)
                if late(g, 1) or k >= HS:
                    v.wait_ge(S(ph + "y_mm"), K * g + k - HS + 1)
                v.tensor_scalar(hcH[:, k % HS, :], hc[:, k % HS, :], 1.0, None, ALU.mult).then_inc(S(ph + "high_v"), 1)

            def own_low(g, k):
                v.wait_ge(S(ph + "high_v"), 6 * g + k // 4 + 1)
                v.tensor_tensor(hcL[:, k % HS, :], hc[:, k % HS, :], hcH[:, k % HS, :].bitcast(F32), ALU.subtract).then_inc(S(ph + "low_v"), 1)

            def add_set(g, par, q):
                v.wait_ge(S(ph + "y_back"), SETS * g + q + 1)
                if ph == "m":
                    v.wait_ge(S("mhz_added"), g + 1)
                j = 4 * q
                while j < 4 * q + 4:
                    b, t = divmod(j, TG)
                    n = min(TG - t, 4 * q + 4 - j)
                    dst = hid[:, b, bass.ds(g * TG + t, n) if not isinstance(g, int) else slice(g * TG + t, g * TG + t + n), :]
                    ins = v.tensor_tensor(dst, dst, ps[:, 4 + (par + q) % 2, D * (j - 4 * q):D * (j - 4 * q + n)].rearrange("p (t d) -> p t d", d=D), ALU.add)
                    j += n
                ins.then_inc(S(ph + "h_added"), 1)

            def var(g, par):
                ln_var_v(v, ph, g, par, 1.0 / D, EPS)

            def norm(g, par):
                if ph == "m" and late(g, 2):
                    v.wait_ge(S("mhz_added"), g - 1)
                ln_norm(v, ph, g, par)

            def step(g, par, ahead, far):
                top = top_two(ahead) if ahead is not None else None
                for k in range(K):
                    weigh(g, k)
                    if k == 0 and far is not None:
                        stats = ln_stats_parts(v, ph, far, par)
                        next(stats)
                        if ph == "m":
                            next(stats, None)
                    if k == 1 and far is not None:
                        next(stats, None)
                    if k == (2 if ph == "m" else 6) and far is not None:
                        var(far, par)
                    if 3 * U < k < 3 * U + 1 + 4 * U and top is not None:
                        for _ in range(2 // U):
                            next(top, None)
                    if k and own(ph, k - 1):
                        own_low(g, k - 1)
                    if not k and late(g, 1) and own(ph, K - 1):
                        own_low(g - 1, K - 1)
                    if k == 7 * U and far is not None:
                        norm(far, par)
                    if k == 9 * U and ahead is not None:
                        weights(ahead)
                    if k == 10 * U and far is not None:
                        split_low(v, ph, far, par)
                    if k == 0 and ahead is None and ph == "m":
                        v.wait_ge(S("mh_added"), SETS * 2)
                        norms = next_norms_v(v, "r")
                    if ahead is None and ph == "m" and k in (0, 1, 3, 4, 6, 7):
                        next(norms)
                    if ahead is None and ph == "m" and k in (9, 10):
                        split_low(v, "r", k - 9, k - 9)
                    done = set_at(CH, k, 3)
                    if done and (done[0] == 0 or late(g, 1)):
                        add_set(g - done[0], par if done[0] == 0 else 1 - par, done[1])
                    if own(ph, k):
                        own_high(g, k)

            if ph == "x":
                v.wait_ge(S("ret_added"), NT)
            else:
                split_low(v, ph, 0, 0)
                split_low(v, ph, 1, 1)
            for _ in top_two(0):
                pass
            weights(0)
            steps(v, step)
            if own(ph, K - 1):
                own_low(NG - 1, K - 1)
            if 2 * CH - 1 + LAG + 3 >= K:
                add_set(NG - 1, 0, 1)
            add_set(NG - 1, 0, 2)

        def ret_v(v):
            def rope(g, par, t):
                k = TG * g + t
                if t == 0:
                    v.wait_ge(S("tab_in%d" % par), 8 * (g - par) + 16)
                v.wait_ge(S("qkv_mm"), k + 1)
                if late(g, 1) or t >= 1:
                    v.wait_ge(S("rot_ready"), k)
                tb = lambda n: tabc[:, par, 2 * t + n, :].rearrange("p (n d) -> p n d", n=2).unsqueeze(1).to_broadcast([P, B, 2, D])
                q4 = lambda c: ps[:, 0:2, :].rearrange("p a (c y) -> p (a c) y", c=2)[:, :, c:c + 2 * D].rearrange("p b (n d) -> p b n d", n=2)
                v.tensor_tensor(rA[:, :, :, :].rearrange("p n b d -> p b n d"), q4(0), tb(0), ALU.mult)
                v.tensor_tensor(rB[:, :, :, :].rearrange("p n b d -> p b n d"), q4(2 * D), tb(1), ALU.mult).then_inc(S("rope_read"), 1)

            def mask(g, t):
                k = TG * g + t
                v.wait_ge(S("score_mm"), k + 1)
                v.tensor_tensor(pmat[:, t, :, :].rearrange("p (j r) n -> p r j n", r=2), ps[:, 5:7, 0:256].rearrange("p r (j n) -> p r j n", j=2), causal[:, :].unsqueeze(1).unsqueeze(1).to_broadcast([P, 2, 2, P]),
                                ALU.mult).then_inc(S("pmat_ready"), 1)

            def add(k):
                dst = hid[:, :, bass.ds(k, 1) if not isinstance(k, int) else slice(k, k + 1), :].rearrange("p b t d -> p b (t d)")
                v.tensor_tensor(dst, dst, ps[:, 3, 0:256].rearrange("p (b d) -> p b d", b=B), ALU.add).then_inc(S("ret_added"), 1)

            def update(g, t):
                k = TG * g + t
                v.wait_ge(S("kv_mm"), k + 1)
                if late(g, 1) or t >= 1:
                    add(k - 1)
                for h in range(2):
                    r = slice(64 * h, 64 * h + 64)
                    own = state[r, t, :, :].rearrange("p (j r) d -> p r j d", r=2)[:, h]
                    kv = ps[r, 3, 256:512].rearrange("p (j c) -> p j c", j=2)[:, :, D * h:D * h + D]
                    ins = v.tensor_tensor(stt[r, :, :], own, kv, ALU.add)
                ins.then_inc(S("stt_v"), 1)
                v.wait_ge(S("stt_v"), k + 1)
                for h in range(2):
                    r = slice(64 * h, 64 * h + 64)
                    new = state[r, (t + 1) % TG, :, :].rearrange("p (j r) d -> p r j d", r=2)[:, h]
                    ins = v.tensor_scalar(new, stt[r, :, :], float(GAMMA ** P), None, ALU.mult)
                ins.then_inc(S("state_ready"), 1)

            def var(g, par):
                ln_var_v(v, "r", g, par, 1.0 / D, EPS)

            def step(g, par, ahead, far):
                for t in range(TG):
                    if t < TG - 1 or ahead is not None:
                        rope(g if t < TG - 1 else ahead, par if t < TG - 1 else 1 - par, (t + 1) % TG)
                    if t == 0 and late(g, 1) and ahead is not None:
                        ln_norm(v, "r", ahead, 1 - par)
                    mask(g, t)
                    if t == 0 and late(g, 1) and ahead is not None:
                        split_low(v, "r", ahead, 1 - par)
                    if ahead is None:
                        if t == 0:
                            v.wait_ge(S("ret_added"), 2 * TG)
                            norms = next_norms_v(v, "x")
                        next(norms)
                        next(norms)
                    if t == 1 and far is not None:
                        ln_stats(v, "r", far, par)
                    if t == 2 and far is not None:
                        var(far, par)
                    update(g, t)

            v.wait_ge(S("mh_added"), SETS * NG)
            v.memset(state[:, :, :, :], 0.0).then_inc(S("state_zero"), 1)
            rope(0, 0, 0)
            steps(v, step)
            split_low(v, "x", 0, 0)
            split_low(v, "x", 1, 1)
            v.wait_ge(S("ret_mm"), NT)
            add(NT - 1)

        def attn_s(s):
            def high(g, par):
                tok = bass.ds(g * TG * P, TG * P) if not isinstance(g, int) else slice(g * TG * P, (g + 1) * TG * P)
                s.wait_ge(S("z1_turned"), g + 1)
                s.activation(ztH[:, :, tok], ps[:, 2 + 2 * par:4 + 2 * par, 0:TG * P], ACT.Copy).then_inc(S("z1h_ready"), 1)

            def step(g, par, ahead, far):
                if far is not None:
                    ln_scalar(s, "a", far, par)
                high(g, par)

            ln_scalar(s, "a", 0, 0)
            ln_scalar(s, "a", 1, 1)
            steps(s, step)
            s.wait_ge(S("att_sub"), 1)
            s.activation(at2[:, :], at[:, :], ACT.Exp).then_inc(S("att_exp"), 1)

            def gate(g, last=False):
                for k in range(8):
                    s.wait_ge(S("mix_ready"), 8 * g + k + 1)
                    if late(g, 1) or k >= 2:
                        s.wait_ge(S("og_ready"), 8 * g + k - 1)
                    s.activation(sig[:, k % 2, :], ps[:, 2 + k % 2, 0:TG * P], ACT.Sigmoid, bias=bgc[:, k % 2:k % 2 + 1]).then_inc(S("sig_ready"), 1)
                    if last and k in (1, 3):
                        ln_scalar(s, "m", k // 2, k // 2)

            gate(0)
            with s.Fori(1, NG - 1) as g:
                gate(g)
            gate(NG - 1, last=True)

        def split_s(s, ph, g, par):
            s.wait_ge(S(ph + "z_ready"), g + 1)
            if late(g, 2):
                s.wait_ge(S(ph + "tp_ready"), SETS * (g - 1))
            s.activation(zst[:, par, :, 0, :], zz[:, par].rearrange("p (j d) -> p j d", d=D), ACT.Copy).then_inc(S(ph + "zh_ready"), 1)

        def evac_s(s, ph, g, par, banks):
            for q in range(SETS):
                s.wait_ge(S(ph + "tp_ready"), SETS * g + q + 1)
                s.activation(zt[:, par, 512 * q:512 * q + 512], ps[:, banks[q % len(banks)], :], ACT.Copy).then_inc(S(ph + "zt_ready"), 1)

        def moe_s(s, ph, CH):
            K, U = SETS * CH, CH // 4
            bias = fb1 if ph == "m" else gb1
            fn = ACT.Gelu if ph == "m" else ACT.Relu
            HL = 1 if ph == "m" else 2
            s.wait_ge(S("deep_ready"), 1)
            s.wait_ge(S("attn_free"), 1)

            def act(g, k):
                s.wait_ge(S(ph + "h_mm"), K * g + k + 1)
                if late(g, 1) or k >= 4:
                    s.wait_ge(S(ph + "hc_ready"), K * g + k - 3)
                c = k % CH
                s.activation(hact[:, k % 4, :], ps[:, k % 2, :], fn, bias=bias[:, c:c + 1]).then_inc(S(ph + "h_act"), 1)

            def high(g, k):
                s.wait_ge(S(ph + "hc_ready"), K * g + k + 1)
                if late(g, 1) or k >= HS:
                    s.wait_ge(S(ph + "y_mm"), K * g + k - HS + 1)
                s.activation(hcH[:, k % HS, :], hc[:, k % HS, :], ACT.Copy).then_inc(S(ph + "high_s"), 1)

            def tanh(g):
                s.wait_ge(S(ph + "gap_ready"), g + 1)
                s.activation(rt[:, 4, :], rt[:, 3, :], ACT.Tanh, scale=0.5).then_inc(S(ph + "tanh_ready"), 1)

            def evac_z(g, par, q):
                s.wait_ge(S(ph + "tp_ready"), SETS * g + q + 1)
                s.activation(zt[:, par, 512 * q:512 * q + 512], ps[:, 6, :], ACT.Copy).then_inc(S(ph + "zt_ready"), 1)

            def evac_comb(g, par):
                s.wait_ge(S(ph + "ct_mm"), g + 1)
                s.activation(combT[:, par, :], ps[0:CT, 7, :], ACT.Copy).then_inc(S(ph + "ct_ready"), 1)

            def evac_out(g, par, q):
                s.wait_ge(S(ph + "y_mm"), K * g + CH * q + CH)
                s.activation(obuf[:, (par + q) % 2, :], ps[:, 4 + (par + q) % 2, :], ACT.Copy).then_inc(S(ph + "ob_ready"), 1)

            def step(g, par, ahead, far):
                for k in range(K):
                    act(g, k)
                    if k >= HL and not own(ph, k - HL):
                        high(g, k - HL)
                    if k < HL and late(g, 1) and not own(ph, K + k - HL):
                        high(g - 1, K + k - HL)
                    done = set_at(CH, k, 1)
                    if done and (done[0] == 0 or late(g, 1)):
                        evac_out(g - done[0], par if done[0] == 0 else 1 - par, done[1])
                    if ahead is not None:
                        if k in (0, U, 2 * U):
                            evac_z(ahead, 1 - par, k // U)
                        if k == 8 * U:
                            tanh(ahead)
                        if k == 10 * U:
                            evac_comb(ahead, 1 - par)
                    if ahead is None and ph == "m":
                        if k in (1, 4):
                            ln_scalar(s, "r", k // 4, k // 4)
                        if k == 8:
                            s.wait_ge(S("mtp_ready"), SETS * NG)
                            split_s(s, "r", 0, 0)
                            split_s(s, "r", 1, 1)
                    if k == (1 if ph == "m" else 4) and far is not None:
                        ln_scalar(s, ph, far, par)
                    if k == 9 * U and far is not None:
                        split_s(s, ph, far, par)

            if ph == "m":
                split_s(s, ph, 0, 0)
                split_s(s, ph, 1, 1)
            for q in range(SETS):
                evac_z(0, 0, q)
            tanh(0)
            evac_comb(0, 0)
            steps(s, step)
            for k in range(K - HL, K):
                if not own(ph, k):
                    high(NG - 1, k)
            if 2 * CH - 1 + LAG + 1 >= K:
                evac_out(NG - 1, 0, 1)
            evac_out(NG - 1, 0, 2)

        def ret_s(s):
            def values(g, t):
                s.wait_ge(S("qkv_mm"), TG * g + t + 1)
                s.activation(val[:, t, :, :], ps[:, 2, 0:4 * D].rearrange("p (b d) -> p b d", b=B), ACT.Copy).then_inc(S("val_ready"), 1)

            def turned(g, t):
                s.wait_ge(S("qkT_mm"), TG * g + t + 1)
                s.activation(qkT[:, t, :, :], ps[:, 4, :].rearrange("p (n q) -> p n q", n=4), ACT.Copy).then_inc(S("qkT_ready"), 1)

            def step(g, par, ahead, far):
                for t in range(TG):
                    if t == 0 and late(g, 1) and ahead is not None:
                        split_s(s, "r", ahead, 1 - par)
                    if ahead is None and t < 2:
                        ln_scalar(s, "x", t, t)
                    if t == 1 and ahead is not None:
                        evac_s(s, "r", ahead, 1 - par, (7,))
                    if t < TG - 1 or ahead is not None:
                        turned(g if t < TG - 1 else ahead, (t + 1) % TG)
                    if t == 0:
                        values(g, 2)
                    elif ahead is not None:
                        values(ahead, t - 1)
                    if t == 1 and far is not None:
                        ln_scalar(s, "r", far, par)

            evac_s(s, "r", 0, 0, (7,))
            values(0, 0)
            turned(0, 0)
            values(0, 1)
            steps(s, step)
            s.wait_ge(S("rtp_ready"), SETS * NG)
            split_s(s, "x", 0, 0)
            split_s(s, "x", 1, 1)

        def attn_p(p):
            p.wait_ge(S("embed_done"), 1)
            p.memset(wgp[:, :, :], 0.0).then_inc(S("zeroed"), 1)
            p.wait_ge(S("row_in"), 16 * 5)
            row = lambda x: x[:, :].unsqueeze(1).unsqueeze(1).to_broadcast([P, B, TG, D])

            def affine(g, par):
                link = chain(p, "p_aff", g, 1)
                p.wait_ge(S("az_ready"), g + 1)
                if late(g, 2):
                    p.wait_ge(S("gram_mm"), g - 1)
                z3 = zs1[:, par].rearrange("p (t b d) -> p b t d", b=B, t=TG)
                link(p.tensor_tensor(z3, four(zz[:, par]), row(gam), ALU.mult))
                p.tensor_tensor(z3, z3, row(bet), ALU.add).then_inc(S("z1_ready"), 1)

            def step(g, par, ahead, far):
                if ahead is not None:
                    affine(ahead, 1 - par)
                if far is not None:
                    ln_pool(p, "a", far, par)

            ln_pool(p, "a", 0, 0)
            affine(0, 0)
            ln_pool(p, "a", 1, 1)
            steps(p, step)
            p.wait_ge(S("acen_ready"), NG)
            for b in range(B):
                ins = p.tensor_tensor(hid[:, b], hid[:, b], bo_row[:, :].unsqueeze(1).to_broadcast([P, NT, D]), ALU.add)
            ins.then_inc(S("bo_added"), 1)

        def moe_p(p, ph, CH):
            K, U = SETS * CH, CH // 4

            def low(g, k):
                p.wait_ge(S(ph + "high_s"), others(ph, g, k + 1))
                p.tensor_tensor(hcL[:, k % HS, :], hc[:, k % HS, :], hcH[:, k % HS, :].bitcast(F32), ALU.subtract).then_inc(S(ph + "low_p"), 1)

            def residual(g, par):
                p.wait_ge(S(ph + "z_ready"), g + 1)
                p.tensor_tensor(grp(g), grp(g), four(zz[:, par]), ALU.add).then_inc(S(ph + "hz_added"), 1)

            def step(g, par, ahead, far):
                for k in range(K):
                    if k and not own(ph, k - 1):
                        low(g, k - 1)
                    if not k and late(g, 1) and not own(ph, K - 1):
                        low(g - 1, K - 1)
                    if k == 4 * U and far is not None:
                        ln_pool(p, ph, far, par)
                    if k == 8 * U and far is not None and ph == "m":
                        residual(far, par)
                    if ahead is None and ph == "m" and k in (4, 5):
                        ln_pool(p, "r", k - 4, k - 4)

            if ph == "m":
                ln_pool(p, ph, 0, 0)
                ln_pool(p, ph, 1, 1)
                residual(0, 0)
                residual(1, 1)
            steps(p, step)
            if not own(ph, K - 1):
                low(NG - 1, K - 1)

        def ret_p(p):
            def rope(g, t):
                p.wait_ge(S("rope_read"), TG * g + t + 1)
                p.tensor_tensor(rot[:, t, :, :, :], rA[:, :, :, :], rB[:, :, :, :], ALU.add).then_inc(S("rot_ready"), 1)

            def step(g, par, ahead, far):
                for t in range(TG):
                    if t < TG - 1 or ahead is not None:
                        rope(g if t < TG - 1 else ahead, (t + 1) % TG)
                    if t == 2 and far is not None:
                        ln_pool(p, "r", far, par)
                    if ahead is None and t:
                        ln_pool(p, "x", t - 1, t - 1)

            p.tensor_copy(pickX[:, :].rearrange("p (x n) -> p x n", n=P), pick[:, :, :].rearrange("p q e -> p (q e)").unsqueeze(2).to_broadcast([CT, SETS * E, P])).then_inc(S("pickx_ready"), 1)
            rope(0, 0)
            steps(p, step)

        @block.sync
        def _(sp):
            def rows_load(b):
                for i in range(3):
                    for c2 in range(2):
                        sp.dma_start(rows[64 * c2:64 * c2 + 64, b % 2, i], A["x_rows"][b, c2, i:i + HH]).then_inc(S("rows_in%d" % (b % 2)), 16)

            def xch_load(pair):
                for u in range(2):
                    sp.dma_start(xch[64 * u:64 * u + 64, :], A["x"][2 * pair + u].rearrange("c h w -> c (h w)")).then_inc(S("xch_in"), 16)

            def wdyn_load(b):
                for slot in (0, 1):
                    sp.wait_ge(S("wd_stored%d" % slot), 32 * (b // 2 + 1))
                for c2 in range(2):
                    sp.dma_start(wdyn[64 * c2:64 * c2 + 64, b % 2], wd_dram[b // 2, KK * (b % 2):KK * (b % 2) + KK].rearrange("k h w -> h k w")).then_inc(S("wd_in%d" % (b % 2)), 16)

            for dst, src in ((w1c, "conv1_blocks"), (w2c, "conv2_blocks"), (bnv[:, 0:5], "bn_columns")):
                sp.dma_start(dst[:, :], A[src]).then_inc(S("embw_in"), 16)
            sp.dma_start(ids[:, :], A["x_txt"].rearrange("b (s o) -> (b s) o", o=1)).then_inc(S("ids_in"), 16)
            xch_load(0)
            for b in range(B):
                sp.dma_start(tx["u"][TXT * b:TXT * b + TXT, :], A["L0_txt_U_w"][0:TXT, :]).then_inc(S("txt_in"), 16)
            for dst, src in (("g", "L0_txt_ln_g"), ("b", "L0_txt_ln_b"), ("ob", "L0_txt_b")):
                sp.dma_start(tx[dst][:, :], A[src].partition_broadcast(P)).then_inc(S("txt_in"), 16)
            sp.dma_start(tx["wT"][:, :], A["txt_WT"]).then_inc(S("txt_in"), 16)
            rows_load(0)
            wdyn_load(0)
            wdyn_load(1)
            rows_load(1)
            sp.wait_ge(S("conv_ready"), 8)
            xch_load(1)
            for dst, src in ((gam, "L0_attn_gamma"), (bet, "L0_attn_beta"), (bo_row, "L0_attn_bo"), (lgb[:, 0:E], "L1_ffn_bg"), (lgb2, "L1_ffn_bias")):
                sp.dma_start(dst[:, :], A[src].partition_broadcast(P)).then_inc(S("row_in"), 16)
            for b in (2, 3):
                sp.wait_ge(S("rows_used_v"), b - 1)
                sp.wait_ge(S("rows_used_p"), b - 1)
                rows_load(b)
                wdyn_load(b)
            sp.wait_ge(S("txt_done"), 1)
            for b in range(B):
                sp.dma_start(hid[0:TXT, b, NT - 1, :], tx["o"][TXT * b:TXT * b + TXT, :]).then_inc(S("txt_put"), 16)
            sp.wait_ge(S("txt_put"), 16 * B)
            sp.wait_ge(S("embed_done"), 1)
            for h in range(2):
                for dst, src in ((wk2, "Wk"), (wq2, "Wq"), (wv2, "Wv")):
                    sp.dma_start(dst[64 * h:64 * h + 64, :], A["L0_attn_" + src]).then_inc(S("attw_in"), 16)
            sp.wait_ge(S("zeroed"), 1)
            for h in range(2):
                sp.dma_start(wgp[64 * h:64 * h + 64, h, :], A["L0_attn_Wg"]).then_inc(S("attw_in"), 16)
            sp.dma_start(wo[:, :, :], A["L0_attn_Wo"].rearrange("(m k) d -> k m d", m=2)).then_inc(S("attw_in"), 16)
            sp.dma_start(bgc[:, :], A["bgT"]).then_inc(S("attw_in"), 16)
            n = S("deepw_in")
            for h in range(2):
                r = slice(64 * h, 64 * h + 64)
                sp.dma_start(wr[r, 0, :], A["router_wT"]).then_inc(n, 16)
                sp.dma_start(wr[r, 1, :], A["L1_ffn_Wg"]).then_inc(n, 16)
                sp.dma_start(fw1[r, :].rearrange("p (e f) -> p e f", e=E), A["L0_ffn_w1"].rearrange("e d f -> d e f")).then_inc(n, 16)
                sp.dma_start(gw1[r, :].rearrange("p (e f) -> p e f", e=E), A["L1_ffn_W1"].rearrange("e d f -> d e f")).then_inc(n, 16)
                sp.dma_start(wqk[r, :], A["w_qk"]).then_inc(n, 16)
            sp.dma_start(fb1[:, :], A["ffn0_b1T"]).then_inc(n, 16)
            sp.dma_start(gb1[:, :], A["ffn1_b1T"]).then_inc(n, 16)
            sp.dma_start(gw2[:, :, :], A["L1_ffn_W2"].rearrange("e f d -> f e d")).then_inc(n, 16)
            for h in range(2):
                sp.dma_start(fw2[64 * h:64 * h + 64, :, :], A["L0_ffn_w2"][bass.ds(h, E // 2, step=2)].rearrange("e f d -> f e d")).then_inc(n, 16)
            sp.wait_ge(S("zeroed"), 2)
            for lay, src in enumerate(("L0_ffn_b2", "L1_ffn_b2")):
                for q in range(SETS):
                    for i in range(2):
                        r = 32 * q + E * i
                        sp.dma_start(bias2[r:r + E, lay, q, :], A[src]).then_inc(n, 16)
            def tab_load(g, par):
                if late(g, 2):
                    sp.wait_ge(S("rope_read"), TG * (g - 1))
                sp.dma_start(tabc[:, par], A["tables"][g if isinstance(g, int) else bass.ds(g, 1)] if isinstance(g, int)
                             else A["tables"][bass.ds(g, 1)].rearrange("o p t c -> (o p) t c")).then_inc(S("tab_in%d" % par), 16)
            sp.wait_ge(S("attn_free"), 1)
            tab_load(0, 0)
            tab_load(1, 1)
            with sp.Fori(0, (NG - 3) // 2) as i:
                for u in (0, 1):
                    tab_load(2 * i + 2 + u, u)
            tab_load(NG - 1, 0)
            for g0, g1 in ((0, 4), (4, 8), (8, NG)):
                sp.wait_ge(S("xh_added"), SETS * g1)
                t0, t1 = TG * g0, min(TG * g1, NT - 1)
                for b in range(B):
                    sp.dma_start(out[b, t0 * P:t1 * P, :].rearrange("(t p) d -> p t d", p=P), hid[:, b, t0:t1, :]).then_inc(S("out_done"), 16)
            for b in range(B):
                sp.dma_start(out[b, (NT - 1) * P:L, :], hid[0:TXT, b, NT - 1, :]).then_inc(S("out_done"), 16)
            sp.wait_ge(S("out_done"), 16 * 4 * B)

        @block.tensor
        def _(pe):
            ACC, CONV, WD, TXB = 0, 4, 6, 7
            pe.wait_ge(S("embw_in"), 16 * 3)
            pe.wait_ge(const_ready, 1)

            def conv(pair):
                pe.wait_ge(S("xch_in"), 32 * (pair + 1))
                for n in range(8 + 1):
                    k = 8 * pair + n
                    if n < 8:
                        if k >= 2:
                            pe.wait_ge(S("y_ready"), k - 1)
                        pe.matmul(ps[0:2 * CK, CONV + n % 2, :], w1c[:, :], xch[:, 512 * n:512 * n + 512], start=True, stop=True).then_inc(S("conv_ready"), 1)
                    if n:
                        pe.wait_ge(S("y_ready"), k)
                        if k >= 2:
                            pe.wait_ge(S("wdt_ready"), k - 1)
                        pe.matmul(ps[0:2 * KK, WD, :], w2c[:, :], yact[:, 512 * n - 512:512 * n], start=True, stop=True).then_inc(S("wd_mm"), 1)

            def add_terms(b):
                if b >= 1:
                    pe.wait_ge(S("embed_out"), b)
                for n, (buf, s) in enumerate(((dA, "termA"), (pD, "termD"), (dC, "termC"), (pE, "termE"))):
                    pe.wait_ge(S(s), b + 1)
                    for q in range(4):
                        mm = pe.matmul(ps[:, ACC + q, :], ident[:, :], buf[:, 8 * q:8 * q + 8, :], start=(n == 0), stop=(n == 3))
                    mm.then_inc(S("term_used"), 1)

            conv(0)

            t = ps[:, TXB, :]
            pe.wait_ge(S("tx_v"), 1)
            pe.transpose(t[0:D, 0:P], tx["a"][:, :], ident[:, :]).then_inc(S("tx_pe"), 1)
            for r in range(3):
                pe.wait_ge(S("tx_v"), 2 + 4 * r)
                pe.transpose(t[0:D, 128:256], tx["u"][:, :], ident[:, :]).then_inc(S("tx_pe"), 1)
                pe.wait_ge(S("tx_v"), 3 + 4 * r)
                for b in range(B):
                    mm = pe.matmul(t[TXT * b:TXT * b + TXT, 256:256 + TXT], tx["aT"][:, TXT * b:TXT * b + TXT], tx["uT"][:, TXT * b:TXT * b + TXT],
                                   start=True, stop=True, skip_group_check=True)
                mm.then_inc(S("tx_pe"), 1)
                pe.wait_ge(S("tx_v"), 5 + 4 * r)
                for b in range(B):
                    s = slice(TXT * b, TXT * b + TXT)
                    mm = pe.matmul(t[s, 320:384], tx["p"][s, :], tx["c"][s, :], start=True, stop=True, skip_group_check=True)
                mm.then_inc(S("tx_pe"), 1)
            pe.wait_ge(S("tx_v"), 15)
            pe.transpose(t[0:D, 0:P], tx["z"][:, :], ident[:, :]).then_inc(S("tx_pe"), 1)
            pe.wait_ge(S("tx_v"), 16)
            pe.matmul(t[:, 128:192], tx["zT"][:, :], tx["wT"][:, :], start=True, stop=True).then_inc(S("tx_pe"), 1)

            add_terms(0)
            conv(1)
            for b in range(1, B):
                add_terms(b)
            gram_pe(pe)
            moe_pe(pe, "m", 4)
            ret_pe(pe)
            moe_pe(pe, "x", 8)

        @block.vector
        def _(v):
            once = link = chain(v, "v_once", 0, 0)
            v.memset(ones[:, :], 1.0).then_inc(S("v_set"), 1)
            v.memset(nhalf[:, :], -0.5).then_inc(S("v_set"), 1)
            v.memset(yact[:, :], 1.0).then_inc(S("v_set"), 1)
            link(v.memset(hid[:, :, NT - 1, :], 0.0))
            v.wait_ge(S("embw_in"), 16 * 3)
            link(v.tensor_scalar(bnv[:, 5:6], bnv[:, 4:5], EPS, None, ALU.add))
            v.wait_ge(S("v_set"), 3)
            v.tensor_copy(bnv[:, 9:10], nhalf[0:2 * CK, 0:1]).then_inc(S("small_ready"), 1)
            v.wait_ge(S("root_ready"), 1)
            link(v.tensor_tensor(bnv[:, 7:8], bnv[:, 6:7], bnv[:, 1:2], ALU.mult))
            link(v.tensor_tensor(bnv[:, 8:9], bnv[:, 0:1], bnv[:, 3:4], ALU.subtract))
            link(v.tensor_tensor(bnv[:, 8:9], bnv[:, 8:9], bnv[:, 7:8], ALU.mult))
            v.tensor_tensor(bnv[:, 8:9], bnv[:, 8:9], bnv[:, 2:3], ALU.add).then_inc(S("bn_ready"), 1)
            v.wait_ge(S("ids_in"), 16)
            v.tensor_scalar(idc[:, 0:1], ids[:, :], 0, A["L0_txt_A_w"].shape[0] - 1, ALU.max, ALU.min).then_inc(S("small_ready"), 1)


            T = ps[:, 7, :]
            v.wait_ge(S("txt_in"), 16 * 8)
            v.wait_ge(S("gath_in"), 32)
            link(v.tensor_copy(tx["o"][:, :], tx["u"][:, :]))
            v.tensor_copy(tx["q"][:, :], tx["o"][:, :]).then_inc(S("tx_v"), 1)
            v.wait_ge(S("tx_pe"), 1)
            v.tensor_copy(tx["aT"][:, :], T[0:D, 0:P]).then_inc(S("tx_v"), 1)
            for r in range(3):
                v.wait_ge(S("tx_pe"), 2 + 3 * r)
                v.tensor_copy(tx["uT"][:, :], T[0:D, 128:256]).then_inc(S("tx_v"), 1)
                v.wait_ge(S("tx_pe"), 3 + 3 * r)
                sc = T[:, 256:256 + TXT]
                link(v.tensor_reduce(tx["m"][:, 0:1], sc, X, ALU.max))
                v.tensor_scalar(tx["s"][:, :], sc, tx["m"][:, 0:1], None, ALU.subtract).then_inc(S("tx_v"), 1)
                v.wait_ge(S("tx_e"), r + 1)
                link(v.reciprocal(tx["m"][:, 2:3], tx["m"][:, 1:2]))
                v.tensor_scalar(tx["p"][:, :], tx["s"][:, :], tx["m"][:, 2:3], None, ALU.mult).then_inc(S("tx_v"), 1)
                v.wait_ge(S("tx_pe"), 4 + 3 * r)
                if r < 2:
                    v.tensor_tensor(tx["u"][:, :], tx["u"][:, :], T[:, 320:384], ALU.add).then_inc(S("tx_v"), 1)
                else:
                    link(v.tensor_tensor(tx["u"][:, :], tx["u"][:, :], T[:, 320:384], ALU.add))
            link(v.tensor_reduce(tx["m"][:, 3:4], tx["u"][:, :], X, ALU.add))
            link(v.tensor_scalar(tx["m"][:, 3:4], tx["m"][:, 3:4], 1.0 / D, None, ALU.mult))
            link(v.tensor_scalar(tx["u"][:, :], tx["u"][:, :], tx["m"][:, 3:4], None, ALU.subtract))
            link(v.tensor_tensor(tx["q"][:, :], tx["u"][:, :], tx["u"][:, :], ALU.mult))
            link(v.tensor_reduce(tx["m"][:, 4:5], tx["q"][:, :], X, ALU.add))
            v.tensor_scalar(tx["m"][:, 4:5], tx["m"][:, 4:5], 1.0 / D, EPS, ALU.mult, ALU.add).then_inc(S("tx_v"), 1)
            v.wait_ge(S("root_ready"), 2)
            link(v.tensor_scalar(tx["z"][:, :], tx["u"][:, :], tx["m"][:, 5:6], None, ALU.mult))
            link(v.tensor_tensor(tx["z"][:, :], tx["z"][:, :], tx["g"][:, :], ALU.mult))
            v.tensor_tensor(tx["z"][:, :], tx["z"][:, :], tx["b"][:, :], ALU.add).then_inc(S("tx_v"), 1)
            v.wait_ge(S("tx_pe"), 11)
            v.tensor_copy(tx["zT"][:, :], T[0:D, 0:P]).then_inc(S("tx_v"), 1)
            v.wait_ge(S("tx_pe"), 12)
            v.tensor_tensor(tx["o"][:, :], T[:, 128:192], tx["ob"][:, :], ALU.add).then_inc(S("txt_done"), 1)
            def tap(buf, u, i, j):
                return v.tensor_tensor(buf[:, :, :], rows[:, u, i, :, j:j + WW], wdyn[:, u, 3 * i + j, :].unsqueeze(1).to_broadcast([P, CP, WW]), ALU.mult)

            for b in range(B):
                u = b % 2
                v.wait_ge(S("rows_in%d" % u), 16 * 6 * (b // 2 + 1))
                v.wait_ge(S("wd_in%d" % u), 32 * (b // 2 + 1))
                for i, buf, term, nth in ((1, dA, "termA", 1), (2, dC, "termC", 3)):
                    if b:
                        v.wait_ge(S("term_used"), 4 * (b - 1) + nth)
                    link(tap(buf, u, i, 0))
                    link(tap(dT, u, i, 1))
                    link(v.tensor_tensor(buf[:, :, :], buf[:, :, :], dT[:, :, :], ALU.add))
                    link(tap(dT, u, i, 2))
                    v.tensor_tensor(buf[:, :, :], buf[:, :, :], dT[:, :, :], ALU.add).then_inc(S(term), 1)
                    v.wait_ge(S(term), b + 1)
                v.sem_inc(S("rows_used_v"), 1)
            v.wait_ge(S("embed_out"), B)
            v.wait_ge(S("txt_put"), 16 * B)
            v.sem_inc(S("embed_done"), 1)
            attn_v(v, once)
            once(v.memset(combS[:, :, :, :].bitcast(F32), 0.0))
            v.wait_ge(S("deep_ready"), 1)
            moe_v(v, "m", 4)
            ret_v(v)
            moe_v(v, "x", 8)

        @block.scalar
        def _(s):
            s.wait_ge(S("v_set"), 3)
            s.wait_ge(S("bn_ready"), 1)

            def conv(pair):
                for n in range(8 + 1):
                    k = 8 * pair + n
                    if n < 8:
                        s.wait_ge(S("conv_ready"), k + 1)
                        if pair and n == 0:
                            s.wait_ge(S("wd_mm"), 8)
                        s.activation(yact[0:2 * CK, 512 * n:512 * n + 512], ps[0:2 * CK, 4 + n % 2, :], ACT.Relu, bias=bnv[:, 8:9], scale=bnv[:, 7:8]).then_inc(S("y_ready"), 1)
                    if n:
                        m = n - 1
                        s.wait_ge(S("wd_mm"), k)
                        quarter = 4 * pair + m // 2
                        if quarter >= 2 and m % 2 == 0:
                            s.wait_ge(S("wd_stored%d" % (quarter % 2)), 16 * (quarter // 2))
                        s.activation(wdT[:, (m // 2) % 2, 512 * (m % 2):512 * (m % 2) + 512], ps[0:2 * KK, 6, :], ACT.Copy).then_inc(S("wdt_ready"), 1)
                        if m % 2:
                            s.wait_ge(S("wdt_ready"), k)
                            r = WQ // WW * (m // 2)
                            s.dma_start(wd_dram[pair, :, r:r + WQ // WW, :].rearrange("k h w -> k (h w)"), wdT[:, (m // 2) % 2, :]).then_inc(S("wd_stored%d" % (quarter % 2)), 16)

            def store(b):
                s.wait_ge(S("term_used"), 4 * b + 4)
                s.activation(hid[:, b, 0:NT - 1, :], ps[:, 0:4, :].rearrange("p a (c w) -> p (a c) w", w=WW), ACT.Copy).then_inc(S("embed_out"), 1)

            conv(0)
            for r in range(3):
                s.wait_ge(S("tx_v"), 4 + 4 * r)
                s.activation(tx["s"][:, :], tx["s"][:, :], ACT.Exp, accum_out=tx["m"][:, 1:2]).then_inc(S("tx_e"), 1)
            store(0)
            conv(1)
            for b in range(1, B):
                store(b)
            attn_s(s)
            moe_s(s, "m", 4)
            ret_s(s)
            moe_s(s, "x", 8)

        @block.gpsimd
        def _(p):
            p.memset(ident[:, :], 0.0).then_inc(S("p_set"), 1)
            p.memset(causal[:, :], 1.0).then_inc(S("p_set"), 1)
            p.wait_ge(S("p_set"), 2)
            p.affine_select(out=ident[:, :], in_=ident[:, :], compare_op=ALU.not_equal, fill=1.0, base=0, pattern=[[-1, P]],
                            channel_multiplier=1).then_inc(S("p_set"), 1)
            p.affine_select(out=causal[:, :], in_=causal[:, :], compare_op=ALU.is_ge, fill=0.0, base=0, pattern=[[1, P]],
                            channel_multiplier=-1).then_inc(S("p_set"), 1)
            p.wait_ge(S("p_set"), 4)
            p.sem_inc(const_ready, 1)
            p.wait_ge(S("small_ready"), 1)
            p.tensor_tensor(bnv[:, 6:7], bnv[:, 5:6], bnv[:, 9:10], ALU.pow).then_inc(S("root_ready"), 1)
            p.wait_ge(S("small_ready"), 2)
            for n, k in (("a", "A"), ("c", "C")):
                p.indirect_dma_start(out=tx[n][:, :], out_offset=None, in_=A["L0_txt_%s_w" % k],
                                     in_offset=bass.IndirectOffsetOnAxis(ap=idc[:, 0:1], axis=0)).then_inc(S("gath_in"), 16)
            p.wait_ge(S("tx_v"), 14)
            p.tensor_tensor(tx["m"][:, 5:6], tx["m"][:, 4:5], nhalf[:, 0:1], ALU.pow).then_inc(S("root_ready"), 1)
            once = link = chain(p, "p_once", 0, 0)

            def tap(buf, u, i, j):
                return p.tensor_tensor(buf[:, :, :], rows[:, u, i, :, j:j + WW], wdyn[:, u, 3 * i + j, :].unsqueeze(1).to_broadcast([P, CP, WW]), ALU.mult)

            for b in range(B):
                u = b % 2
                p.wait_ge(S("rows_in%d" % u), 16 * 6 * (b // 2 + 1))
                p.wait_ge(S("wd_in%d" % u), 32 * (b // 2 + 1))
                if b:
                    p.wait_ge(S("term_used"), 4 * b)
                link(tap(pD, u, 0, 0))
                link(tap(pT, u, 0, 1))
                p.tensor_tensor(pD[:, :, :], pD[:, :, :], pT[:, :, :], ALU.add).then_inc(S("termD"), 1)
                tap(pE, u, 0, 2).then_inc(S("termE"), 1)
                p.wait_ge(S("termD"), b + 1)
                p.wait_ge(S("termE"), b + 1)
                p.sem_inc(S("rows_used_p"), 1)
            attn_p(p)
            deep_prep_p(p, once)
            moe_p(p, "m", 4)
            ret_p(p)
            moe_p(p, "x", 8)

def rotary_tables():
    f = np.float32
    j = np.arange(0, D, 2, dtype=f)
    inv = (f(1.0) / f(10000.0) ** (j / f(D))).astype(f)
    pos = np.arange(NT * P, dtype=f)
    ang = (pos[:, None] * inv[None, :]).astype(f)
    s, c = np.sin(ang), np.cos(ang)
    base = ((j + f(0.4 * D)) / f(1.4 * D)).astype(f)
    scale = (base[None, :] ** (pos[:, None] / f(512.0))).astype(f)
    local = (np.arange(NT * P) % P)[:, None]
    dq, dk = GAMMA ** local, GAMMA ** (-local.astype(np.float64))
    out = np.zeros((NT * P, 2, 2 * D), f)
    for n, (w, m) in enumerate(((scale, dq), (1.0 / scale, dk))):
        cw, sw = (c * w * m).astype(f), (s * w * m).astype(f)
        out[:, 0, D * n:D * n + D] = np.concatenate([cw, cw], 1)
        out[:, 1, D * n:D * n + D] = np.concatenate([-sw, sw], 1)
    t = out.reshape(NG, TG, P, 2, 2 * D).transpose(0, 2, 1, 3, 4)
    return np.ascontiguousarray(t.reshape(NG, P, 2 * TG, 2 * D))


_INS = ['x', 'x_txt', 'L0_tok_conv1_w', 'L0_tok_conv1_b', 'L0_tok_bn_gamma', 'L0_tok_bn_beta', 'L0_tok_bn_mean', 'L0_tok_bn_var',
        'L0_tok_conv2_w', 'L0_tok_conv2_b', 'L0_txt_A_w', 'L0_txt_C_w', 'L0_txt_U_w', 'L0_txt_ln_g', 'L0_txt_ln_b', 'L0_txt_W', 'L0_txt_b',
        'L0_attn_gamma', 'L0_attn_beta', 'L0_attn_Wq', 'L0_attn_Wk', 'L0_attn_Wv', 'L0_attn_Wg', 'L0_attn_bg', 'L0_attn_Wo', 'L0_attn_bo',
        'L0_ffn_router_w', 'L0_ffn_w1', 'L0_ffn_b1', 'L0_ffn_w2', 'L0_ffn_b2', 'L1_ffn_Wg', 'L1_ffn_bg', 'L1_ffn_bias', 'L1_ffn_W1',
        'L1_ffn_b1', 'L1_ffn_W2', 'L1_ffn_b2']


def kernel(**inputs):
    import numpy as _np
    import concourse.bacc as _bacc
    from concourse import mybir as _mybir
    from concourse.bass_utils import run_bass_kernel_spmd as _run

    nc = _bacc.Bacc("TRN2", target_bir_lowering=False, num_devices=1)
    data = {k: _np.ascontiguousarray(inputs[k]) for k in _INS}
    x = data["x"].reshape(B, CP, 2, HH, WW)
    xr = _np.zeros((B, 2, HH + 2, CP, WW + 2), x.dtype)
    xr[:, :, 1:-1, :, 1:-1] = x.transpose(0, 2, 3, 1, 4)
    data["x_rows"] = xr
    wq, wk, wv = (_np.asarray(inputs["L1_attn_W_" + n]) for n in "QKV")
    ev, od = _np.arange(0, D, 2), _np.arange(1, D, 2)
    eo, oe = _np.concatenate([ev, od]), _np.concatenate([od, ev])
    data["w_qk"] = _np.ascontiguousarray(_np.concatenate([wq[:, eo], wk[:, eo], wq[:, oe], wk[:, oe], wv], 1))
    data["tables"] = rotary_tables()
    c1, c2 = data["L0_tok_conv1_w"].T, data["L0_tok_conv2_w"].T
    b1, b2 = _np.zeros((P, 2 * CK), c1.dtype), _np.zeros((2 * CK + 1, 2 * KK), c2.dtype)
    for u in range(2):
        b1[C * u:C * u + C, CK * u:CK * u + CK] = c1
        b2[CK * u:CK * u + CK, KK * u:KK * u + KK] = c2
        b2[2 * CK, KK * u:KK * u + KK] = data["L0_tok_conv2_b"]
    data["conv1_blocks"], data["conv2_blocks"] = b1, b2
    cols = _np.stack([data["L0_tok_" + k] for k in ("conv1_b", "bn_gamma", "bn_beta", "bn_mean", "bn_var")], 1)
    data["bn_columns"] = _np.ascontiguousarray(_np.concatenate([cols, cols], 0))
    for name, v in (("txt_WT", data["L0_txt_W"].T),
                    ("router_wT", data["L0_ffn_router_w"].T), ("ffn0_b1T", data["L0_ffn_b1"].reshape(E // 2, P).T),
                    ("ffn1_b1T", data["L1_ffn_b1"].T), ("bgT", data["L0_attn_bg"].reshape(2, P).T)):
        data[name] = _np.ascontiguousarray(v)
    arrays, args = {}, {}
    for name, v in data.items():
        arrays[f"in_{name}_dram"] = v
        args[name] = nc.dram_tensor(f"in_{name}_dram", v.shape, _mybir.dt.from_np(v.dtype), kind="ExternalInput").ap()
    res = nc.dram_tensor("out_0_dram", (B, L, D), F32, kind="ExternalOutput").ap()
    wd_dram = nc.dram_tensor("dynamic_weights", (B // 2, 2 * KK, HH, WW), F32, kind="Internal").ap()
    build(nc, args, res, wd_dram)
    r = _run(nc, [arrays], core_ids=[0])
    return r.results[0]["out_0_dram"]
```
